# Optimizing a Trainium2 kernel written in Bass

```python
import numpy as np
import jax
import jax.numpy as jnp

def _softmax(x, axis=-1):
    return jax.nn.softmax(x, axis=axis)

def _gelu(x):
    return jax.nn.gelu(x, approximate=True)

def _silu(x):
    return jax.nn.silu(x)

def _sigmoid(x):
    return jax.nn.sigmoid(x)

def _layernorm(x, axis=-1, eps=1e-05):
    m = jnp.mean(x, axis=axis, keepdims=True)
    v = jnp.var(x, axis=axis, keepdims=True)
    return (x - m) / jnp.sqrt(v + eps)

def _scatter_add(tgt, idx, src, axis=0):
    return tgt.at[idx].add(src)

def _segment_sum(src, seg, n):
    return jax.ops.segment_sum(src, seg, n)
kernel_name = 'mk_flamingo_gated_d1_seqx_r4_db9ae3'

def setup_inputs(seed: int=0):
    np.random.seed(seed)
    _w = jnp.asarray

    def _rec_inputs():
        import jax
        import jax.numpy as jnp
        _rk = jax.random.key(seed)
        x = -0.0002928 + 1 * jax.random.normal(jax.random.fold_in(_rk, 1), (16, 256, 256), jnp.float32)
        _lenS = 256 - jax.random.randint(jax.random.fold_in(_rk, 7), (16,), 0, max(1, 256 // 4) + 1, jnp.int32)
        _lenS2 = 77 - jax.random.randint(jax.random.fold_in(_rk, 8), (16,), 0, max(1, 77 // 4) + 1, jnp.int32)
        _ctx_1024P = jax.random.normal(jax.random.fold_in(_rk, 11), (16, 16, 256), jnp.float32)
        _ctx_1024c = jax.random.dirichlet(jax.random.fold_in(_rk, 511), 0.3 * jnp.ones((16,), jnp.float32), (16, 77))
        _ctx_1024t = jnp.einsum('bsk,bkd->bsd', _ctx_1024c, _ctx_1024P)
        _ctx_1024t = _ctx_1024t * jax.lax.rsqrt(jnp.mean(jnp.square(_ctx_1024t)) + 1e-12) * 0.953939
        ctx_1024 = -1.39393e-06 + 0.999914 * (_ctx_1024t + 0.3 * jax.random.normal(jax.random.fold_in(_rk, 611), (16, 77, 256), jnp.float32))
        fside_Bx16xSxS2_0 = 9.80324e-06 + 0.100009 * jax.random.normal(jax.random.fold_in(_rk, 12), (16, 16, 256, 77), jnp.float32)
        fside_SxS2_0 = -2.64403e-05 + 0.100002 * jax.random.normal(jax.random.fold_in(_rk, 14), (256, 77), jnp.float32)
        _validS = jnp.arange(256)[None, :] < _lenS[:, None]
        _validS2 = jnp.arange(77)[None, :] < _lenS2[:, None]
        _causal = jnp.tril(jnp.ones((256, 256), dtype=bool))
        mask_BxS2_bf0 = jnp.logical_not(jnp.ones((16, 77), dtype=bool))
        _g = jax.random.normal(jax.random.fold_in(_rk, 9001), (2, 1), jnp.float32)
        _g = jnp.sign(_g) * jnp.maximum(jnp.abs(_g), 1.0) + (_g == 0) * 1.0
        g_xattn = _g[0]
        g_ffn = _g[1]
        return (x, ctx_1024, fside_Bx16xSxS2_0, fside_SxS2_0, mask_BxS2_bf0, g_xattn, g_ffn)
    x, ctx_1024, fside_Bx16xSxS2_0, fside_SxS2_0, mask_BxS2_bf0, g_xattn, g_ffn = _rec_inputs()

    def _L0_xattn_setup():
        import jax, jax.numpy as jnp
        import numpy as np
        E = 256
        H = 16
        D = E // H
        key = jax.random.key(seed)
        ks = jax.random.split(key, 12)
        B, T, S = (2, 512, 512)
        inp = {'query': jax.random.normal(ks[0], (B, T, E), jnp.float32), 'key': jax.random.normal(ks[1], (B, S, E), jnp.float32), 'value': jax.random.normal(ks[2], (B, S, E), jnp.float32), 'spatial_bias': jax.random.normal(ks[3], (B, H, T, S), jnp.float32) * 0.1, 'directional_bias': jax.random.normal(ks[4], (B, H, T, S), jnp.float32) * 0.1, 'key_padding_mask': jnp.zeros((B, S), dtype=bool), 'attn_mask': jax.random.normal(ks[5], (T, S), jnp.float32) * 0.1, 'Wq': jax.random.normal(ks[6], (E, E), jnp.float32) / np.sqrt(E), 'bq': jnp.zeros((E,), jnp.float32), 'Wk': jax.random.normal(ks[7], (E, E), jnp.float32) / np.sqrt(E), 'bk': jnp.zeros((E,), jnp.float32), 'Wv': jax.random.normal(ks[8], (E, E), jnp.float32) / np.sqrt(E), 'bv': jnp.zeros((E,), jnp.float32), 'Wo': jax.random.normal(ks[9], (E, E), jnp.float32) / np.sqrt(E), 'bo': jnp.zeros((E,), jnp.float32)}
        return inp
    _L0_xattn_all = _L0_xattn_setup()
    _L0_xattn_in = {k: v for k, v in _L0_xattn_all.items() if k in ('Wq', 'bq', 'Wk', 'bk', 'Wv', 'bv', 'Wo', 'bo')}
    del _L0_xattn_all

    def _L0_ffn_setup():
        import jax, jax.numpy as jnp
        import numpy as np
        H_DIM, E_DIM = (256, 128)
        N_SHARED, N_ROUTED, TOP_K = (2, 16, 4)
        B, S = (4, 512)
        key = jax.random.key(seed)
        ks = jax.random.split(key, 6)
        sc = 1.0 / np.sqrt(H_DIM)
        ec = 1.0 / np.sqrt(E_DIM)
        return {'x': jax.random.normal(ks[0], (B, S, H_DIM), dtype=jnp.float32), 'shared_up': jax.random.uniform(ks[1], (N_SHARED, E_DIM, H_DIM), jnp.float32, -sc, sc), 'shared_down': jax.random.uniform(ks[2], (N_SHARED, H_DIM, E_DIM), jnp.float32, -ec, ec), 'routed_up': jax.random.uniform(ks[3], (N_ROUTED, E_DIM, H_DIM), jnp.float32, -sc, sc), 'routed_down': jax.random.uniform(ks[4], (N_ROUTED, H_DIM, E_DIM), jnp.float32, -ec, ec), 'router_w': jax.random.uniform(ks[5], (N_ROUTED, H_DIM), jnp.float32, -sc, sc)}
    _L0_ffn_all = _L0_ffn_setup()
    _L0_ffn_in = {k: v for k, v in _L0_ffn_all.items() if k in ('shared_up', 'shared_down', 'routed_up', 'routed_down', 'router_w')}
    del _L0_ffn_all
    return {'x': x, 'ctx_1024': ctx_1024, 'fside_Bx16xSxS2_0': fside_Bx16xSxS2_0, 'fside_SxS2_0': fside_SxS2_0, 'mask_BxS2_bf0': mask_BxS2_bf0, 'g_xattn': g_xattn, 'g_ffn': g_ffn, 'L0_xattn_Wq': _L0_xattn_in['Wq'], 'L0_xattn_bq': _L0_xattn_in['bq'], 'L0_xattn_Wk': _L0_xattn_in['Wk'], 'L0_xattn_bk': _L0_xattn_in['bk'], 'L0_xattn_Wv': _L0_xattn_in['Wv'], 'L0_xattn_bv': _L0_xattn_in['bv'], 'L0_xattn_Wo': _L0_xattn_in['Wo'], 'L0_xattn_bo': _L0_xattn_in['bo'], 'L0_ffn_shared_up': _L0_ffn_in['shared_up'], 'L0_ffn_shared_down': _L0_ffn_in['shared_down'], 'L0_ffn_routed_up': _L0_ffn_in['routed_up'], 'L0_ffn_routed_down': _L0_ffn_in['routed_down'], 'L0_ffn_router_w': _L0_ffn_in['router_w']}

def reference(x, ctx_1024, fside_Bx16xSxS2_0, fside_SxS2_0, mask_BxS2_bf0, g_xattn, g_ffn, L0_xattn_Wq, L0_xattn_bq, L0_xattn_Wk, L0_xattn_bk, L0_xattn_Wv, L0_xattn_bv, L0_xattn_Wo, L0_xattn_bo, L0_ffn_shared_up, L0_ffn_shared_down, L0_ffn_routed_up, L0_ffn_routed_down, L0_ffn_router_w):
    import jax
    import jax.numpy as jnp

    def _L0_xattn_ref(query, key, value, spatial_bias, directional_bias, key_padding_mask, attn_mask, Wq, bq, Wk, bk, Wv, bv, Wo, bo):
        import jax, jax.numpy as jnp
        import numpy as np
        E = 256
        H = 16
        D = E // H
        B, T, _ = query.shape
        S = key.shape[1]
        scale = D ** (-0.5)
        q = (query @ Wq.T + bq).reshape(B, T, H, D).transpose(0, 2, 1, 3)
        k = (key @ Wk.T + bk).reshape(B, S, H, D).transpose(0, 2, 1, 3)
        v = (value @ Wv.T + bv).reshape(B, S, H, D).transpose(0, 2, 1, 3)
        scores = jnp.einsum('bhtd,bhsd->bhts', q, k) * scale
        scores = scores + attn_mask[None, None, :, :]
        pad = key_padding_mask[:, None, None, :]
        scores = jnp.where(pad, -jnp.inf, scores)
        if T == S:
            scores = scores + spatial_bias + directional_bias
        probs = jax.nn.softmax(scores, axis=-1)
        out = jnp.einsum('bhts,bhsd->bhtd', probs, v)
        out = out.transpose(0, 2, 1, 3).reshape(B, T, E)
        return out @ Wo.T + bo

    def _L0_ffn_ref(x, shared_up, shared_down, routed_up, routed_down, router_w):
        import jax, jax.numpy as jnp
        import numpy as np
        H_DIM, E_DIM = (256, 128)
        N_SHARED, N_ROUTED, TOP_K = (2, 16, 4)
        B, S = (4, 512)
        b, s, h = x.shape
        xt = x.reshape(-1, h)
        up_s = jnp.einsum('th,seh->tse', xt, shared_up)
        shared = jnp.einsum('tse,she->th', jax.nn.gelu(up_s, approximate=False), shared_down)
        probs = jax.nn.softmax(xt @ router_w.T, axis=-1)
        topk_p, topk_i = jax.lax.top_k(probs, TOP_K)
        gate = jnp.zeros_like(probs).at[jnp.arange(xt.shape[0])[:, None], topk_i].add(topk_p)
        up_r = jnp.einsum('th,reh->tre', xt, routed_up)
        act = jax.nn.gelu(up_r, approximate=False) * gate[:, :, None]
        routed = jnp.einsum('tre,rhe->th', act, routed_down)
        return (shared + routed).reshape(b, s, h)
    x = x + jnp.tanh(g_xattn[0]) * _L0_xattn_ref(_layernorm(x, axis=-1), ctx_1024, ctx_1024, fside_Bx16xSxS2_0, fside_Bx16xSxS2_0, mask_BxS2_bf0, fside_SxS2_0, L0_xattn_Wq, L0_xattn_bq, L0_xattn_Wk, L0_xattn_bk, L0_xattn_Wv, L0_xattn_bv, L0_xattn_Wo, L0_xattn_bo)
    x = x + jnp.tanh(g_ffn[0]) * _L0_ffn_ref(_layernorm(x, axis=-1), L0_ffn_shared_up, L0_ffn_shared_down, L0_ffn_routed_up, L0_ffn_routed_down, L0_ffn_router_w)
    return x

_drawn_inputs = setup_inputs


def setup_inputs(seed=0):
    import zlib

    import numpy as np

    out = dict(_drawn_inputs(seed))
    spreads = {'L0_xattn_bq': (0.0, 0.461),
     'L0_xattn_bk': (0.0, 0.8),
     'L0_xattn_bv': (0.0, 0.1),
     'L0_xattn_bo': (0.0, 0.1)}
    factors = {'fside_SxS2_0': 5.629}
    for name, (base, spread) in spreads.items():
        noise = np.random.default_rng([zlib.crc32(name.encode()), seed]).standard_normal(out[name].shape)
        drawn = base * np.exp(spread * noise) if base else spread * noise
        out[name] = jnp.asarray(drawn.astype(out[name].dtype))
    for name, factor in factors.items():
        out[name] = (out[name] * factor).astype(out[name].dtype)
    return out
```

```python
from contextlib import ExitStack

import concourse.bass as bass
from concourse import mybir

F32 = mybir.dt.float32
FR = mybir.dt.float32r
U8 = mybir.dt.uint8
U32 = mybir.dt.uint32
ALU = mybir.AluOpType
ACT = mybir.ActivationFunctionType
X = mybir.AxisListType.X

B, T, E = 16, 256, 256
H, D, S = 16, 16, 77
N_SHARED, N_ROUTED, TOP_K, HID = 2, 16, 4, 128
NE = N_SHARED + N_ROUTED
LN_EPS = 1e-5
SCALE = D ** -0.5
P = 128

TOK = 512
G = B * T // TOK
TILES = TOK // P
BPG = TOK // T
C = E // P
HPC = H // C
QH = 4
QN = H // QH
QW = QH * S
HS = H * S
NCH = -(-HS // P)
HSP = NCH * P
SPLIT = -(-HPC * S // P)
FIRST2 = HPC * S // P
NSLOT = SPLIT + NCH - FIRST2
HB = 3
LAG = 2
CTX = B * S

HI, LO = 0, 1
PASSES = ((HI, HI), (HI, LO), (LO, HI))

NBANK = 3


def att_units():
    u = [("XT", 0), ("XT", 1), ("Q", 0), ("Q", 1)]
    for step in ("S0", "S1", "PT0", "S2", "PT1", "PV0", "S3", "PT2", "PT3", "PV1"):
        k = {"S": QN, "P": 3}[step[0]] if step[:2] != "PV" else 1
        u += [(step, i) for i in range(k)]
    return u + [("O", 0), ("O", 1), ("X2", 0), ("X2", 1), ("R", 0), ("RT", 0), ("GT", 0)]


UNITS = att_units()
BANK = {u: i % NBANK for i, u in enumerate(UNITS)}
USE = {u: i // NBANK for i, u in enumerate(UNITS)}
USES = [sum(1 for u in UNITS if BANK[u] == k) for k in range(NBANK)]

KW = [412, 410, 410]
K_UNITS = [(m, sum(KW[:i]), KW[i]) for m in range(C) for i in range(len(KW))]
V_UNITS = B // 2
CTX_UNITS = len(K_UNITS) + V_UNITS
CTX_USES = [len(range(k, CTX_UNITS, NBANK)) for k in range(NBANK)]


def full_count(u, n):
    return n * USES[BANK[u]] + (CTX_USES[BANK[u]] + USE[u] + 1)


V_PIECES = []
for _h in range(H):
    _r = _h * S
    while _r < (_h + 1) * S:
        _k = _r // P
        _n = min((_h + 1) * S, (_k + 1) * P) - _r
        _slot = _k if _h < HPC else SPLIT + _k - FIRST2
        V_PIECES.append((_h, _r - _h * S, _n, _slot, _r % P))
        _r += _n

SLOT = {"LN1": 0, "XT": 1, "Q": 2, "S0": 3, "S1": 4, "N0": 4, "N1": 5, "PT0": 6, "S2": 6, "PT1": 7, "N2": 7,
        "PV0": 8, "S3": 8, "PT2": 9, "N3": 9, "PT3": 11, "PV1": 12, "O": 13, "LN2": 13, "X2": 15, "R": 15,
        "RT": 16, "GATE": 16, "GT": 17}

WP = NE // 2
ROUTER_STEPS = 18


def block_program(nc, x, ctxT, mask, attn_mask, g_x, g_f, wkvT, wqoT, bqk, bo, bv, wffn, wr, ident_c, pick_c, iota_c,
                  out):
    with ExitStack() as es:
        def sb(name, shape, dt=F32):
            return es.enter_context(nc.sbuf_tensor(name, shape, dt))

        def sem(name):
            return es.enter_context(nc.semaphore(name))

        k_scr = nc.dram_tensor("k_scr", [2, C, P, CTX], F32, kind="Internal").ap()
        v_scr = nc.dram_tensor("v_scr", [B, S, 2, E], F32, kind="Internal").ap()
        x1_scr = nc.dram_tensor("x1_scr", [G, P, TILES * E], F32, kind="Internal").ap()

        w_ffn = sb("w_ffn", [P, 2, NE, 4 * P], FR)
        w_qo = sb("w_qo", [P, 2, 2, C * E], FR)
        w_rt = sb("w_rt", [P, 2, C * N_ROUTED], FR)
        pick = sb("pick", [P, N_ROUTED, P], FR)
        k_blk = sb("k_blk", [P, 2, C, HPC * S], FR)
        v_blk = sb("v_blk", [P, 2, NSLOT, P], FR)
        p_t = sb("p_t", [P, 2, NCH, 2 * P], FR)
        scr = sb("scr", [P, 2, HSP])
        xo_t = sb("xo_t", [P, 2, C, TOK], FR)
        q_t = sb("q_t", [P, 2, C, TOK], FR)
        x2_t = sb("x2_t", [P, 2, C, TOK], FR)
        gel = sb("gel", [P, 2, TOK])
        hid = sb("hid", [P, HB, 2, TOK], FR)
        gate_t = sb("gate_t", [P, TOK], FR)
        xn = sb("xn", [P, TILES, E])
        x_in = sb("x_in", [P, TILES, E])
        x_res = sb("x_res", [P, TILES, E])
        x_out = sb("x_out", [P, TILES, E])
        ident = sb("ident", [P, P])
        pick_f = sb("pick_f", [P, N_ROUTED])
        iota = sb("iota", [P, N_ROUTED])
        am = sb("am", [P, 2, S])
        mask_u = sb("mask_u", [P, BPG * S], U8)
        mask_f = sb("mask_f", [P, BPG, S])
        am_b = sb("am_b", [P, BPG, 2, S])
        b_qk = sb("b_qk", [P, 2 * C])
        bo_b = sb("bo_b", [P, E])
        bv_b = sb("bv_b", [P, E])
        wr_f = sb("wr_f", [P, C * N_ROUTED])
        g_raw = sb("g_raw", [P, 2])
        g_tan = sb("g_tan", [P, 2])
        neg_half = sb("neg_half", [P, TILES])
        unused = sb("unused", [P, 1])
        st = sb("st", [P, TILES, 6])
        mv = sb("mv", [P, TILES, 2])
        ve = sb("ve", [P, TILES])
        rstd = sb("rstd", [P, TILES])
        mx = sb("mx", [P, 2, H])
        den = sb("den", [P, 2, H])
        rden = sb("rden", [P, 2, H])
        r_max = sb("r_max", [P, TILES])
        r_sum = sb("r_sum", [P, TILES])
        r_rcp = sb("r_rcp", [P, TILES])
        r_exp = sb("r_exp", [P, TILES, N_ROUTED])
        r_prob = sb("r_prob", [P, TILES, N_ROUTED])
        r_top = sb("r_top", [P, TILES, 8])
        r_idx = sb("r_idx", [P, TILES, 8], U32)
        r_idf = sb("r_idf", [P, TILES, 8])
        r_eq = sb("r_eq", [P, TILES, N_ROUTED, TOP_K])
        r_sel = sb("r_sel", [P, TILES, N_ROUTED])
        gate2 = sb("gate2", [P, TILES, 2 * N_ROUTED])

        ctx_raw = scr[:, :, 0:CTX]
        ctx_t = [p_t[:, l, :, :].rearrange("p k n -> p (k n)")[:, 0:C * CTX].rearrange("p (c n) -> p c n", c=C)
                 for l in (HI, LO)]
        w_kv = q_t
        k_st = xo_t
        v_st = x2_t
        v_f = xn
        kv_raw = x_res
        qo_raw = x_out
        lg_t = scr[0:N_ROUTED, 1, 0:TOK]
        ffn_t = scr[:, 0, 0:C * TOK].rearrange("p (c n) -> p c n", c=C)
        w_stage = [gel[:, :, :].rearrange("p a n -> p (a n)"), x_out[:, :, :].rearrange("p a n -> p (a n)")]

        banks = [es.enter_context(nc.psum_tensor(f"bank{k}", [P, 512], F32)) for k in range(NBANK)]
        up_ps = [es.enter_context(nc.psum_tensor(f"up_ps{k}", [P, 512], F32)) for k in range(2)]
        dn_ps = [es.enter_context(nc.psum_tensor(f"dn_ps{k}", [P, 512], F32)) for k in range(C)]
        gt_ps = es.enter_context(nc.psum_tensor("gt_ps", [P, 512], F32))

        bank_full = [sem(f"bank_full{k}") for k in range(NBANK)]
        bank_free = [sem(f"bank_free{k}") for k in range(NBANK)]
        consts_in, ctx_in, kv_in, qo_in, small_in = (sem(s) for s in (
            "consts_in", "ctx_in", "kv_in", "qo_in", "small_in"))
        ctx_hi, ctx_lo, kv_hi, kv_lo, qo_hi, qo_lo = (sem(s) for s in (
            "ctx_hi", "ctx_lo", "kv_hi", "kv_lo", "qo_hi", "qo_lo"))
        k_hi, v_hi, v_lo = (sem(s) for s in ("k_hi", "v_hi", "v_lo"))
        k_stored = [sem("k_stored0"), sem("k_stored1")]
        v_stored = [sem("v_stored0"), sem("v_stored1")]
        w_in = [sem("w_in0"), sem("w_in1")]
        w_hi, w_lo, zeroed, picked, tan_done, tbo_done = (sem(s) for s in (
            "w_hi", "w_lo", "zeroed", "picked", "tan_done", "tbo_done"))
        x_loaded, mask_loaded, mask_neg, mask_ready = (sem(s) for s in (
            "x_loaded", "mask_loaded", "mask_neg", "mask_ready"))
        ln_stats, ln_aggr, ln_var, ln_rstd, xn_ready, xr_ready = (sem(s) for s in (
            "ln_stats", "ln_aggr", "ln_var", "ln_rstd", "xn_ready", "xr_ready"))
        xt_hi, q_hi, pt_hi, ot_hi = (sem(s) for s in ("xt_hi", "q_hi", "pt_hi", "ot_hi"))
        kblk_loaded, vblk_loaded = sem("kblk_loaded"), sem("vblk_loaded")
        max_done, shifted, exp_done, sum_done, rden_done, p_ready = (sem(s) for s in (
            "max_done", "shifted", "exp_done", "sum_done", "rden_done", "p_ready"))
        router, r_exped = sem("router"), sem("r_exped")
        x2_hi, x2_lo = sem("x2_hi"), sem("x2_lo")
        up_full, up_read, gate_full, gated, h_hi, h_lo, down_done = (sem(s) for s in (
            "up_full", "up_read", "gate_full", "gated", "h_hi", "h_lo", "down_done"))
        ffn_read, fout_full, fout_added = sem("ffn_read"), sem("fout_full"), sem("fout_added")
        xo_loaded, x1_stored, out_stored = sem("xo_loaded"), sem("x1_stored"), sem("out_stored")

        x_v = x.rearrange("(g t p) e -> g p t e", t=TILES, p=P)
        out_v = out.rearrange("(g t p) e -> g p t e", t=TILES, p=P)
        x1_v = x1_scr.rearrange("g p (t e) -> g p t e", t=TILES)
        mask_v = mask.rearrange("(g b) s -> g (b s)", b=BPG)

        def f32(ap):
            return ap.bitcast(F32)

        def bc_mid(ap, k):
            return ap.unsqueeze(1).to_broadcast([ap.shape[0], k, ap.shape[1]])

        def bc_last(ap, k):
            return ap.unsqueeze(2).to_broadcast([ap.shape[0], ap.shape[1], k])

        def bank(u):
            return banks[BANK[u]]

        block = es.enter_context(nc.Block())

        @block.sync
        def _(sp):
            def load_blocks_k(b, filled_by, count):
                if filled_by is not None:
                    sp.wait_ge(zeroed, 5)
                    sp.wait_ge(bank_full[BANK[filled_by]], count)
                for h8 in range(HPC):
                    sp.dma_start(f32(k_blk[D * h8:D * h8 + D, :, :, S * h8:S * h8 + S]).rearrange("p l c s -> p (l c) s"),
                                 k_scr[:, :, D * h8:D * h8 + D, bass.ds(b * S, S)].rearrange("l c p s -> p (l c) s"))\
                        .then_inc(kblk_loaded, 16)

            def load_blocks_v(b, filled_by, count):
                if filled_by is not None:
                    sp.wait_ge(zeroed, 5)
                    sp.wait_ge(bank_full[BANK[filled_by]], count)
                v_b = v_scr[bass.ds(b, 1)].rearrange("o s l e -> (o s) l e")
                for h, s0, n, slot, p0 in V_PIECES:
                    c0 = D * (h % HPC)
                    sp.dma_start(f32(v_blk[p0:p0 + n, :, slot, c0:c0 + D]),
                                 v_b[s0:s0 + n, :, D * h:D * h + D]).then_inc(vblk_loaded, 16)

            sp.dma_start(ctx_raw, ctxT).then_inc(ctx_in, 16)
            sp.dma_start(kv_raw[:, :, :].rearrange("p a n -> p (a n)"), wkvT).then_inc(kv_in, 16)
            sp.dma_start(b_qk[:, :], bqk).then_inc(small_in, 16)
            sp.dma_start(bv_b[:, :], bv.partition_broadcast(P)).then_inc(small_in, 16)
            sp.dma_start(bo_b[:, :], bo.partition_broadcast(P)).then_inc(small_in, 16)
            sp.dma_start(g_raw[:, 0:1], g_x.partition_broadcast(P)).then_inc(small_in, 16)
            sp.dma_start(g_raw[:, 1:2], g_f.partition_broadcast(P)).then_inc(small_in, 16)
            sp.dma_start(x_in[:, :, :], x_v[0]).then_inc(x_loaded, 16)
            sp.dma_start(ident[:, :], ident_c).then_inc(consts_in, 16)
            sp.dma_start(qo_raw[:, :, :].rearrange("p a n -> p (a n)"), wqoT).then_inc(qo_in, 16)
            sp.dma_start(wr_f[:, :], wr).then_inc(small_in, 16)
            sp.dma_start(am[:, :, :], attn_mask.rearrange("(t p) s -> p t s", p=P)).then_inc(small_in, 16)
            sp.dma_start(mask_u[:, :], mask_v[0:1, :].to_broadcast([P, BPG * S])).then_inc(mask_loaded, 16)
            sp.dma_start(pick_f[:, :], pick_c).then_inc(consts_in, 16)
            sp.dma_start(iota[:, :], iota_c).then_inc(consts_in, 16)

            for i, (m, off, w) in enumerate(K_UNITS):
                sp.wait_ge(bank_free[i % NBANK], i // NBANK + 1)
                sp.dma_start(k_scr[:, m, :, off:off + w].rearrange("l p w -> p l w"),
                             f32(k_st[:, :, i % 2, 0:w])).then_inc(k_stored[i % 2], 16)
            for i in range(V_UNITS):
                sp.wait_ge(v_lo, i + 1)
                for j in range(2):
                    sp.dma_start(v_scr[2 * i + j], f32(v_st[0:S, :, i % 2, j * E:(j + 1) * E])).then_inc(v_stored[i % 2], 16)

            def load_w(p):
                if p == 1:
                    sp.wait_ge(qo_lo, 1)
                if p >= 2:
                    sp.wait_ge(w_lo, p - 1)
                sp.dma_start(w_stage[p % 2], wffn[:, p * 2 * 512:(p + 1) * 2 * 512]).then_inc(w_in[p % 2], 16)

            load_w(0)
            load_w(1)
            for k in range(2):
                sp.wait_ge(k_stored[k], 16 * (len(K_UNITS) // 2))
            for k in range(2):
                sp.wait_ge(v_stored[k], 32 * (V_UNITS // 2))
            sp.wait_ge(zeroed, 5)
            load_blocks_k(0, None, 0)
            load_blocks_v(0, None, 0)
            for p in range(2, WP):
                load_w(p)
            load_blocks_k(1, ("S1", QN - 1), full_count(("S1", QN - 1), 0))
            load_blocks_v(1, ("PV0", 0), full_count(("PV0", 0), 0))
            sp.wait_ge(bank_free[BANK[("O", 1)]], full_count(("O", 1), 0))
            sp.dma_start(x1_v[0], x_res[:, :, :]).then_inc(x1_stored, 16)

            def body_head(g, n):
                sp.wait_ge(x1_stored, 16 * g + 16)
                sp.wait_ge(zeroed, 5)
                sp.wait_ge(out_stored, 16 * g + 16)
                sp.dma_start(x_out[:, :, :], x1_v[bass.ds(g, 1)].rearrange("o p t e -> (o p) t e"))\
                    .then_inc(xo_loaded, 16)

            def body_tail(g):
                sp.wait_ge(zeroed, 5)
                sp.wait_ge(fout_added, 2 * g + 4)
                sp.dma_start(out_v[bass.ds(g, 1)].rearrange("o p t e -> (o p) t e"), x_out[:, :, :])\
                    .then_inc(out_stored, 16)

            with sp.Fori(0, G - 1) as g:
                n = g + 1
                sp.wait_ge(xr_ready, n)
                sp.wait_ge(zeroed, 5)
                sp.wait_ge(xn_ready, 8 * n - 4)
                sp.dma_start(x_in[:, :, :], x_v[bass.ds(n, 1)].rearrange("o p t e -> (o p) t e"))\
                    .then_inc(x_loaded, 16)
                sp.wait_ge(zeroed, 5)
                sp.wait_ge(mask_neg, n)
                sp.dma_start(mask_u[:, :], mask_v[bass.ds(n, 1), :].to_broadcast([P, BPG * S]))\
                    .then_inc(mask_loaded, 16)
                body_head(g, n)
                u = ("S3", QN - 1)
                load_blocks_k(2 * n, u, full_count(u, g))
                u = ("PV1", 0)
                load_blocks_v(2 * n, u, full_count(u, g))
                u = ("S1", QN - 1)
                load_blocks_k(2 * n + 1, u, full_count(u, n))
                u = ("PV0", 0)
                load_blocks_v(2 * n + 1, u, full_count(u, n))
                u = ("O", 1)
                sp.wait_ge(zeroed, 5)
                sp.wait_ge(bank_free[BANK[u]], full_count(u, n))
                sp.dma_start(x1_v[bass.ds(n, 1)].rearrange("o p t e -> (o p) t e"), x_res[:, :, :])\
                    .then_inc(x1_stored, 16)
                body_tail(g)
            body_head(G - 1, G)
            body_tail(G - 1)
            sp.wait_ge(out_stored, 16 * G + 16)
            sp.wait_ge(x1_stored, 16 * G)

        @block.scalar
        def _(act):
            act.wait_ge(ctx_in, 16)
            for c in range(C):
                nc.scalar.activation(ctx_t[HI][:, c, :], ctx_raw[:, c, :], ACT.Copy).then_inc(ctx_hi, 1)
            act.wait_ge(kv_in, 16)
            nc.scalar.activation(w_kv[:, HI, :, :].rearrange("p a n -> p (a n)"),
                                 kv_raw[:, :, :].rearrange("p a n -> p (a n)"), ACT.Copy).then_inc(kv_hi, 1)
            act.wait_ge(qo_in, 16)
            nc.scalar.activation(w_qo[:, HI, :, :].rearrange("p a n -> p (a n)"),
                                 qo_raw[:, :, :].rearrange("p a n -> p (a n)"), ACT.Copy).then_inc(qo_hi, 1)
            act.wait_ge(small_in, 7 * 16)
            nc.scalar.activation(w_rt[:, HI, :], wr_f[:, :], ACT.Copy).then_inc(qo_hi, 1)
            nc.scalar.activation(g_tan[:, :], g_raw[:, :], ACT.Tanh).then_inc(tan_done, 1)
            for i, (m, off, w) in enumerate(K_UNITS):
                act.wait_ge(bank_full[i % NBANK], i // NBANK + 1)
                if i >= 2:
                    act.wait_ge(k_stored[i % 2], 16 * (i // 2))
                nc.scalar.activation(k_st[:, HI, i % 2, 0:w], banks[i % NBANK][:, 0:w], ACT.Identity,
                                     bias=b_qk[:, C + m:C + m + 1]).then_inc(k_hi, 1)
            for i in range(V_UNITS):
                k = len(K_UNITS) + i
                act.wait_ge(bank_free[k % NBANK], k // NBANK + 1)
                if i >= 2:
                    act.wait_ge(v_stored[i % 2], 32 * (i // 2))
                nc.scalar.activation(v_st[0:S, HI, i % 2, :],
                                     v_f[0:S, 2 * (i % 2):2 * (i % 2) + 2, :].rearrange("p a n -> p (a n)"),
                                     ACT.Copy).then_inc(v_hi, 1)

            def split_w(p):
                act.wait_ge(w_in[p % 2], 16 * (p // 2 + 1))
                nc.scalar.activation(w_ffn[:, HI, 2 * p:2 * p + 2, :].rearrange("p a n -> p (a n)"), w_stage[p % 2],
                                     ACT.Copy).then_inc(w_hi, 1)

            def take_xt(step, n, k):
                for c in range(C):
                    act.wait_ge(bank_full[BANK[(step, c)]], full_count((step, c), n))
                    nc.scalar.activation(xo_t[:, HI, c, :], bank((step, c))[:, :], ACT.Copy).then_inc(xt_hi, 1)

            def take_q(n):
                for m in range(C):
                    act.wait_ge(bank_full[BANK[("Q", m)]], full_count(("Q", m), n))
                    nc.scalar.activation(q_t[:, HI, m, :], bank(("Q", m))[:, :], ACT.Identity,
                                         bias=b_qk[:, m:m + 1]).then_inc(q_hi, 1)

            def exps(t, n):
                act.wait_ge(shifted, 4 * n + t + 1)
                nc.scalar.activation(scr[:, t % 2, 0:HS], scr[:, t % 2, 0:HS], ACT.Exp).then_inc(exp_done, 1)

            def take_pt(t, n):
                for i in range(3):
                    u = (f"PT{t}", i)
                    k = min(4, NCH - 4 * i)
                    act.wait_ge(bank_full[BANK[u]], full_count(u, n))
                    nc.scalar.activation(p_t[:, HI, 4 * i:4 * i + k, P * (t % 2):P * (t % 2) + P],
                                         bank(u)[:, 0:k * P].rearrange("p (k n) -> p k n", k=k),
                                         ACT.Copy).then_inc(pt_hi, 1)

            def take_o(j, n):
                u = (f"PV{j}", 0)
                act.wait_ge(bank_full[BANK[u]], full_count(u, n))
                nc.scalar.activation(xo_t[:, HI, :, T * j:T * j + T], bank(u)[:, :].rearrange("p (c n) -> p c n", c=C),
                                     ACT.Copy).then_inc(ot_hi, 1)

            def take_logits(n):
                act.wait_ge(bank_full[BANK[("R", 0)]], full_count(("R", 0), n))
                nc.scalar.activation(lg_t, bank(("R", 0))[0:N_ROUTED, :], ACT.Copy)\
                    .then_inc(bank_free[BANK[("R", 0)]], 1)

            def router_exp(n):
                act.wait_ge(bank_free[BANK[("RT", 0)]], full_count(("RT", 0), n))
                nc.scalar.activation(r_exp[:, :, :], r_exp[:, :, :], ACT.Exp).then_inc(r_exped, 1)

            def take_gates(n):
                act.wait_ge(bank_full[BANK[("GT", 0)]], full_count(("GT", 0), n))
                nc.scalar.activation(gate_t[0:2 * N_ROUTED, :], bank(("GT", 0))[0:2 * N_ROUTED, :], ACT.Copy)\
                    .then_inc(bank_free[BANK[("GT", 0)]], 1)

            def attention(e, n):
                if e == SLOT["XT"]:
                    take_xt("XT", n, 0)
                if e == SLOT["Q"]:
                    take_q(n)
                for t in range(TILES):
                    if e == SLOT[f"PT{t}"]:
                        take_pt(t, n)
                    if e == SLOT[f"N{t}"]:
                        exps(t, n)
                    if t % 2 == 0 and e == SLOT[f"PV{t // 2}"]:
                        take_o(t // 2, n)
                if e == SLOT["X2"]:
                    take_xt("X2", n, 1)
                if e == SLOT["R"]:
                    take_logits(n)
                if e == SLOT["GATE"]:
                    router_exp(n)
                if e == SLOT["GT"]:
                    take_gates(n)

            def hand_over(n):
                act.wait_ge(xt_hi, 4 * n + 4)
                nc.scalar.activation(x2_t[:, HI, :, :], f32(xo_t[:, HI, :, :]), ACT.Copy).then_inc(x2_hi, 1)

            def gelu(e, g):
                act.wait_ge(up_full, NE * g + e + 1)
                act.wait_ge(h_lo, NE * g + e + 1)
                nc.scalar.activation(gel[:, e % 2, :], up_ps[e % 2][:, :], ACT.Gelu).then_inc(up_read, 1)

            def hidden_hi(e, g):
                if e < N_SHARED:
                    act.wait_ge(up_read, NE * g + e + 3)
                else:
                    act.wait_ge(gated, N_ROUTED * g + e - N_SHARED + 2)
                act.wait_ge(down_done, NE * g + e + 1)
                nc.scalar.activation(hid[:, e % HB, HI, :], gel[:, e % 2, :], ACT.Copy).then_inc(h_hi, 1)

            def take_ffn(g):
                act.wait_ge(down_done, NE * g + NE + HB)
                for m in range(C):
                    nc.scalar.activation(ffn_t[:, m, :], dn_ps[m][:, :], ACT.Copy, scale=g_tan[:, 1:2])\
                        .then_inc(ffn_read, 1)

            for k in range(2):
                act.wait_ge(k_stored[k], 16 * (len(K_UNITS) // 2))
            for e in range(NE):
                attention(e, 0)
                if e < WP:
                    split_w(e)
            for k in range(2):
                act.wait_ge(v_stored[k], 32 * (V_UNITS // 2))
            hand_over(0)
            with act.Fori(0, G - 1) as g:
                for e in range(NE):
                    gelu(e, g)
                    attention(e, g + 1)
                    hidden_hi(e, g)
                act.wait_ge(up_full, NE * g + NE)
                hand_over(g + 1)
                take_ffn(g)
            for e in range(NE):
                gelu(e, G - 1)
                hidden_hi(e, G - 1)
            take_ffn(G - 1)

        @block.vector
        def _(dve):
            nc.vector.memset(neg_half[:, :], -0.5).then_inc(zeroed, 1)
            nc.vector.memset(f32(k_blk[:, :, :, :]), 0.0).then_inc(zeroed, 1)
            nc.vector.memset(f32(v_blk[:, :, :, :]), 0.0).then_inc(zeroed, 1)
            nc.vector.memset(scr[:, :, HS:HSP], 0.0).then_inc(zeroed, 1)
            nc.vector.memset(f32(gate_t[:, :]), 0.0).then_inc(zeroed, 1)
            for c in range(C):
                dve.wait_ge(ctx_hi, c + 1)
                nc.vector.tensor_tensor(ctx_t[LO][:, c, :], ctx_raw[:, c, :], f32(ctx_t[HI][:, c, :]),
                                        ALU.subtract).then_inc(ctx_lo, 1)
            dve.wait_ge(kv_hi, 1)
            nc.vector.tensor_tensor(w_kv[:, LO, :, :].rearrange("p a n -> p (a n)"),
                                    kv_raw[:, :, :].rearrange("p a n -> p (a n)"),
                                    f32(w_kv[:, HI, :, :]).rearrange("p a n -> p (a n)"),
                                    ALU.subtract).then_inc(kv_lo, 1)
            dve.wait_ge(qo_hi, 2)
            nc.vector.tensor_tensor(w_rt[:, LO, :], wr_f[:, :], f32(w_rt[:, HI, :]), ALU.subtract)
            nc.vector.tensor_tensor(w_qo[:, LO, :, :].rearrange("p a n -> p (a n)"),
                                    qo_raw[:, :, :].rearrange("p a n -> p (a n)"),
                                    f32(w_qo[:, HI, :, :]).rearrange("p a n -> p (a n)"),
                                    ALU.subtract).then_inc(qo_lo, 1)
            dve.wait_ge(tan_done, 1)
            nc.vector.tensor_scalar(bo_b[:, :], bo_b[:, :], g_tan[:, 0:1], None, ALU.mult).then_inc(tbo_done, 1)
            for i, (m, off, w) in enumerate(K_UNITS):
                dve.wait_ge(k_hi, i + 1)
                nc.vector.scalar_tensor_tensor(out=k_st[:, LO, i % 2, 0:w], in0=banks[i % NBANK][:, 0:w],
                                               scalar=b_qk[:, C + m:C + m + 1], in1=f32(k_st[:, HI, i % 2, 0:w]),
                                               op0=ALU.add, op1=ALU.subtract).then_inc(bank_free[i % NBANK], 1)

            def v_split(i):
                dve.wait_ge(v_hi, i + 1)
                nc.vector.tensor_tensor(v_st[0:S, LO, i % 2, :],
                                        v_f[0:S, 2 * (i % 2):2 * (i % 2) + 2, :].rearrange("p a n -> p (a n)"),
                                        f32(v_st[0:S, HI, i % 2, :]), ALU.subtract).then_inc(v_lo, 1)

            for i in range(V_UNITS):
                k = len(K_UNITS) + i
                dve.wait_ge(bank_full[k % NBANK], k // NBANK + 1)
                nc.vector.tensor_tensor(v_f[0:S, 2 * (i % 2):2 * (i % 2) + 2, :],
                                        banks[k % NBANK][0:S, :].rearrange("p (j n) -> p j n", j=2),
                                        bc_mid(bv_b[0:S, :], 2), ALU.add).then_inc(bank_free[k % NBANK], 1)
                v_split(i)

            dve.wait_ge(consts_in, 48)
            nc.vector.tensor_copy(pick[:, :, :], bc_last(pick_f[:, :], P)).then_inc(picked, 1)

            def additive_mask(n):
                dve.wait_ge(mask_loaded, 16 * n + 16)
                nc.vector.tensor_scalar(mask_f[:, :, :].rearrange("p b s -> p (b s)"), mask_u[:, :], -3e38, 3e38,
                                        ALU.mult, ALU.mult).then_inc(mask_neg, 1)
                dve.wait_ge(mask_neg, n + 1)
                for t in range(2):
                    nc.vector.tensor_tensor(am_b[:, :, t, :], mask_f[:, :, :], bc_mid(am[:, t, :], BPG), ALU.add)\
                        .then_inc(mask_ready, 1)

            def carry_wait():
                nc.vector.memset(unused[:, :], 0.0)

            def layer_norm(src, n, k):
                for t in range(TILES):
                    nc.vector.bn_stats(st[:, t, :], src[:, t, :]).then_inc(ln_stats, 1)
                dve.wait_ge(ln_stats, 8 * n + 4 * k + 4)
                carry_wait()
                for t in range(TILES):
                    nc.vector.bn_aggr(mv[:, t, :], st[:, t, :]).then_inc(ln_aggr, 1)
                dve.wait_ge(ln_aggr, 8 * n + 4 * k + 4)
                nc.vector.tensor_scalar(ve[:, :], mv[:, :, 1], LN_EPS, None, ALU.add).then_inc(ln_var, 1)
                dve.wait_ge(ln_rstd, 2 * n + k + 1)
                for t in range(TILES):
                    nc.vector.tensor_scalar(xn[:, t, :], src[:, t, :], mv[:, t, 0:1], rstd[:, t:t + 1],
                                            ALU.subtract, ALU.mult).then_inc(xn_ready, 1)

            def take_xt(step, n, k):
                for c in range(C):
                    dve.wait_ge(xt_hi, 4 * n + 2 * k + c + 1)
                    nc.vector.tensor_tensor(xo_t[:, LO, c, :], bank((step, c))[:, :], f32(xo_t[:, HI, c, :]),
                                            ALU.subtract).then_inc(bank_free[BANK[(step, c)]], 1)

            def take_q(n):
                for m in range(C):
                    dve.wait_ge(q_hi, 2 * n + m + 1)
                    nc.vector.scalar_tensor_tensor(out=q_t[:, LO, m, :], in0=bank(("Q", m))[:, :],
                                                   scalar=b_qk[:, m:m + 1], in1=f32(q_t[:, HI, m, :]),
                                                   op0=ALU.add, op1=ALU.subtract)\
                        .then_inc(bank_free[BANK[("Q", m)]], 1)

            def scores(t, n):
                s = scr[:, t % 2, 0:HS].rearrange("p (h s) -> p h s", h=H)
                dve.wait_ge(mask_ready, 2 * n + 2)
                for i in range(QN):
                    u = (f"S{t}", i)
                    dve.wait_ge(bank_full[BANK[u]], full_count(u, n))
                    nc.vector.scalar_tensor_tensor(out=s[:, QH * i:QH * i + QH, :],
                                                   in0=bank(u)[:, 0:QW].rearrange("p (h s) -> p h s", h=QH),
                                                   scalar=SCALE, in1=bc_mid(am_b[:, t // 2, t % 2, :], QH),
                                                   op0=ALU.mult, op1=ALU.add).then_inc(bank_free[BANK[u]], 1)
                for i in range(QN):
                    u = (f"S{t}", i)
                    dve.wait_ge(bank_free[BANK[u]], full_count(u, n))
                nc.vector.tensor_reduce(mx[:, t % 2, :], s, X, ALU.max).then_inc(max_done, 1)
                dve.wait_ge(max_done, 4 * n + t + 1)
                nc.vector.tensor_tensor(s, s, bc_last(mx[:, t % 2, :], S), ALU.subtract).then_inc(shifted, 1)

            def normal(t, n):
                s = scr[:, t % 2, 0:HS].rearrange("p (h s) -> p h s", h=H)
                dve.wait_ge(exp_done, 4 * n + t + 1)
                nc.vector.tensor_reduce(den[:, t % 2, :], s, X, ALU.add).then_inc(sum_done, 1)
                dve.wait_ge(sum_done, 4 * n + t + 1)
                nc.vector.reciprocal(rden[:, t % 2, :], den[:, t % 2, :]).then_inc(rden_done, 1)

            def take_pt(t, n):
                for i in range(3):
                    u = (f"PT{t}", i)
                    k = min(4, NCH - 4 * i)
                    dve.wait_ge(pt_hi, 12 * n + 3 * t + i + 1)
                    nc.vector.tensor_tensor(p_t[:, LO, 4 * i:4 * i + k, P * (t % 2):P * (t % 2) + P],
                                            bank(u)[:, 0:k * P].rearrange("p (k n) -> p k n", k=k),
                                            f32(p_t[:, HI, 4 * i:4 * i + k, P * (t % 2):P * (t % 2) + P]),
                                            ALU.subtract).then_inc(bank_free[BANK[u]], 1)

            def take_o(j, n):
                u = (f"PV{j}", 0)
                dve.wait_ge(ot_hi, 2 * n + j + 1)
                nc.vector.tensor_tensor(xo_t[:, LO, :, T * j:T * j + T],
                                        bank(u)[:, :].rearrange("p (c n) -> p c n", c=C),
                                        f32(xo_t[:, HI, :, T * j:T * j + T]), ALU.subtract)\
                    .then_inc(bank_free[BANK[u]], 1)

            def residual(n):
                dve.wait_ge(xr_ready, n + 1)
                for i in range(2):
                    u = ("O", i)
                    dve.wait_ge(bank_full[BANK[u]], full_count(u, n))
                    nc.vector.scalar_tensor_tensor(out=x_res[:, 2 * i:2 * i + 2, :],
                                                   in0=bank(u)[:, :].rearrange("p (t n) -> p t n", t=2),
                                                   scalar=g_tan[:, 0:1], in1=x_res[:, 2 * i:2 * i + 2, :],
                                                   op0=ALU.mult, op1=ALU.add).then_inc(bank_free[BANK[u]], 1)
                for i in range(2):
                    dve.wait_ge(bank_free[BANK[("O", i)]], full_count(("O", i), n))

            def gates(n):
                u = ("RT", 0)
                lg = bank(u)[:, :].rearrange("p (t n) -> p t n", t=TILES)[:, :, 0:N_ROUTED]
                base = ROUTER_STEPS * n
                dve.wait_ge(bank_full[BANK[u]], full_count(u, n))
                nc.vector.tensor_reduce(r_max[:, :], lg, X, ALU.max).then_inc(router, 1)
                dve.wait_ge(router, base + 1)
                nc.vector.tensor_tensor(r_exp[:, :, :], lg, bc_last(r_max[:, :], N_ROUTED), ALU.subtract)\
                    .then_inc(bank_free[BANK[u]], 1)
                dve.wait_ge(r_exped, n + 1)
                nc.vector.tensor_reduce(r_sum[:, :], r_exp[:, :, :], X, ALU.add).then_inc(router, 1)
                dve.wait_ge(router, base + 2)
                nc.vector.reciprocal(r_rcp[:, :], r_sum[:, :]).then_inc(router, 1)
                dve.wait_ge(router, base + 3)
                nc.vector.tensor_tensor(r_prob[:, :, :], r_exp[:, :, :], bc_last(r_rcp[:, :], N_ROUTED), ALU.mult)\
                    .then_inc(router, 1)
                dve.wait_ge(router, base + 4)
                carry_wait()
                for t in range(TILES):
                    nc.vector.max(r_top[:, t, :], r_prob[:, t, :]).then_inc(router, 1)
                dve.wait_ge(router, base + 8)
                carry_wait()
                for t in range(TILES):
                    nc.vector.max_index(r_idx[:, t, :], r_top[:, t, :], r_prob[:, t, :]).then_inc(router, 1)
                dve.wait_ge(router, base + 12)
                nc.vector.tensor_copy(r_idf[:, :, :], r_idx[:, :, :]).then_inc(router, 1)
                dve.wait_ge(router, base + 13)
                for t in range(TILES):
                    eq = nc.vector.tensor_tensor(r_eq[:, t, :, :], bc_last(iota[:, :], TOP_K),
                                                 bc_mid(r_idf[:, t, 0:TOP_K], N_ROUTED), ALU.is_equal)
                eq.then_inc(router, 1)
                dve.wait_ge(router, base + 14)
                nc.vector.tensor_reduce(r_sel[:, :, :], r_eq[:, :, :, :], X, ALU.max).then_inc(router, 1)
                dve.wait_ge(router, base + 15)
                nc.vector.tensor_tensor(r_prob[:, :, :], r_prob[:, :, :], r_sel[:, :, :], ALU.mult)\
                    .then_inc(router, 1)
                dve.wait_ge(router, base + 16)
                nc.vector.tensor_copy(gate2[:, :, 0:N_ROUTED].bitcast(FR), r_prob[:, :, :]).then_inc(router, 1)
                dve.wait_ge(router, base + 17)
                nc.vector.tensor_tensor(gate2[:, :, N_ROUTED:2 * N_ROUTED], r_prob[:, :, :],
                                        gate2[:, :, 0:N_ROUTED], ALU.subtract).then_inc(router, 1)

            def attention(e, n):
                if e == SLOT["LN1"]:
                    additive_mask(n)
                    dve.wait_ge(x_loaded, 16 * n + 16)
                    layer_norm(x_in, n, 0)
                if e == SLOT["XT"]:
                    take_xt("XT", n, 0)
                if e == SLOT["Q"]:
                    take_q(n)
                for t in range(TILES):
                    if e == SLOT[f"PT{t}"]:
                        take_pt(t, n)
                    if t % 2 == 0 and e == SLOT[f"PV{t // 2}"]:
                        take_o(t // 2, n)
                for t in range(TILES):
                    if e == SLOT[f"N{t}"]:
                        normal(t, n)
                    if e == SLOT[f"S{t}"]:
                        scores(t, n)
                if e == SLOT["O"]:
                    residual(n)
                    layer_norm(x_res, n, 1)
                if e == SLOT["X2"]:
                    take_xt("X2", n, 1)
                if e == SLOT["GATE"]:
                    gates(n)

            def hand_over(n):
                for c in range(C):
                    dve.wait_ge(bank_free[BANK[("X2", c)]], full_count(("X2", c), n))
                nc.vector.tensor_copy(x2_t[:, LO, :, :], f32(xo_t[:, LO, :, :])).then_inc(x2_lo, 1)

            def gate(e, g):
                if e >= N_SHARED:
                    dve.wait_ge(up_read, NE * g + e + 3)
                    dve.wait_ge(gate_full, N_ROUTED * g + e - N_SHARED + 1)
                    nc.vector.tensor_tensor(gel[:, e % 2, :], gel[:, e % 2, :], gt_ps[:, :], ALU.mult)\
                        .then_inc(gated, 1)

            def add_ffn(g):
                dve.wait_ge(xo_loaded, 16 * g + 16)
                for i in range(2):
                    dve.wait_ge(fout_full, 2 * g + i + 1)
                    nc.vector.tensor_tensor(x_out[:, 2 * i:2 * i + 2, :], x_out[:, 2 * i:2 * i + 2, :],
                                            dn_ps[i][:, :].rearrange("p (t n) -> p t n", t=2), ALU.add)\
                        .then_inc(fout_added, 1)

            for e in range(NE):
                attention(e, 0)
            for k in range(2):
                dve.wait_ge(v_stored[k], 32 * (V_UNITS // 2))
            hand_over(0)
            with dve.Fori(0, G - 1) as g:
                for e in range(NE):
                    gate(e, g)
                    attention(e, g + 1)
                dve.wait_ge(up_full, NE * g + NE)
                hand_over(g + 1)
                add_ffn(g)
            for e in range(NE):
                gate(e, G - 1)
            add_ffn(G - 1)

        @block.gpsimd
        def _(pool):
            pool.sem_inc(up_read, 2)
            pool.sem_inc(h_lo, 2)
            pool.sem_inc(down_done, HB)
            pool.sem_inc(fout_added, 2)
            pool.sem_inc(gated, 1)
            pool.sem_inc(out_stored, 16)

            def split_w(p):
                pool.wait_ge(w_hi, p + 1)
                nc.gpsimd.tensor_tensor(w_ffn[:, LO, 2 * p:2 * p + 2, :].rearrange("p a n -> p (a n)"), w_stage[p % 2],
                                        f32(w_ffn[:, HI, 2 * p:2 * p + 2, :]).rearrange("p a n -> p (a n)"),
                                        ALU.subtract).then_inc(w_lo, 1)

            def root(n, k):
                pool.wait_ge(ln_var, 2 * n + k + 1)
                nc.gpsimd.tensor_tensor(rstd[:, :], ve[:, :], neg_half[:, :], ALU.pow).then_inc(ln_rstd, 1)

            def rows(n):
                pool.wait_ge(x_loaded, 16 * n + 16)
                if not isinstance(n, int):
                    pool.wait_ge(x1_stored, 16 * n)
                    pool.wait_ge(xn_ready, 8 * n)
                nc.gpsimd.tensor_tensor(x_res[:, :, :], x_in[:, :, :], bc_mid(bo_b[:, :], TILES), ALU.add)\
                    .then_inc(xr_ready, 1)

            def probabilities(t, n):
                s = scr[:, t % 2, 0:HS].rearrange("p (h s) -> p h s", h=H)
                pool.wait_ge(rden_done, 4 * n + t + 1)
                nc.gpsimd.tensor_tensor(s, s, bc_last(rden[:, t % 2, :], S), ALU.mult).then_inc(p_ready, 1)

            def attention(e, n):
                if e == SLOT["LN1"]:
                    root(n, 0)
                    rows(n)
                for t in range(TILES):
                    if e == SLOT[f"N{t}"]:
                        probabilities(t, n)
                if e == SLOT["LN2"]:
                    root(n, 1)

            def hidden_lo(e, g):
                pool.wait_ge(h_hi, NE * g + e + 1)
                nc.gpsimd.tensor_tensor(hid[:, e % HB, LO, :], gel[:, e % 2, :], f32(hid[:, e % HB, HI, :]),
                                        ALU.subtract).then_inc(h_lo, 1)

            pool.wait_ge(zeroed, 1)
            pool.wait_ge(tbo_done, 1)
            pool.wait_ge(kv_lo, 1)
            for e in range(NE):
                attention(e, 0)
                if e < WP:
                    split_w(e)
            with pool.Fori(0, G - 1) as g:
                for e in range(NE):
                    attention(e, g + 1)
                    hidden_lo(e, g)
            for e in range(NE):
                hidden_lo(e, G - 1)

        @block.tensor
        def _(pe):
            def product(dst, pairs, first=True, last=True):
                k = 0
                for lhs, rhs in pairs:
                    for a, b in PASSES:
                        mm = nc.tensor.matmul(dst, lhs(a), rhs(b), start=first and k == 0,
                                              stop=last and k == 3 * len(pairs) - 1)
                        k += 1
                return mm

            def w_half(w, which, c, m0, m1):
                return lambda l: w[:, l, which, c * E + m0:c * E + m1]

            kv = w_kv[:, :, :, :]
            pe.wait_ge(ctx_lo, 2)
            pe.wait_ge(kv_lo, 1)
            for i, (m, off, w) in enumerate(K_UNITS):
                if i >= NBANK:
                    pe.wait_ge(bank_free[i % NBANK], i // NBANK)
                product(banks[i % NBANK][:, 0:w],
                        [(w_half(kv, 0, c, m * P, m * P + P),
                          lambda l, c=c: ctx_t[l][:, c, off:off + w]) for c in range(C)])\
                    .then_inc(bank_full[i % NBANK], 1)
            for i in range(V_UNITS):
                k = len(K_UNITS) + i
                pe.wait_ge(bank_free[k % NBANK], k // NBANK)
                for j in range(2):
                    b = 2 * i + j
                    mm = product(banks[k % NBANK][0:S, j * E:(j + 1) * E],
                                 [(lambda l, c=c: ctx_t[l][:, c, b * S:(b + 1) * S],
                                   w_half(kv, 1, c, 0, E)) for c in range(C)])
                mm.then_inc(bank_full[k % NBANK], 1)

            def refill(u, n):
                pe.wait_ge(bank_free[BANK[u]], full_count(u, n) - 1)

            def read(u, n):
                pe.wait_ge(bank_free[BANK[u]], full_count(u, n))

            def transpose_rows(step, n, k):
                pe.wait_ge(xn_ready, 8 * n + 4 * k + 4)
                for c in range(C):
                    u = (step, c)
                    refill(u, n)
                    for t in range(TILES):
                        mm = nc.tensor.transpose(bank(u)[:, t * P:(t + 1) * P], xn[:, t, c * P:(c + 1) * P],
                                                 ident[:, :])
                    mm.then_inc(bank_full[BANK[u]], 1)

            def queries(n):
                read(("XT", 0), n)
                read(("XT", 1), n)
                for m in range(C):
                    u = ("Q", m)
                    refill(u, n)
                    product(bank(u)[:, :], [(w_half(w_qo, 0, c, m * P, m * P + P),
                                             lambda l, c=c: xo_t[:, l, c, :]) for c in range(C)])\
                        .then_inc(bank_full[BANK[u]], 1)

            def scores(t, n):
                pe.wait_ge(kblk_loaded, (2 * n + t // 2 + 1) * (HPC * 16))
                if t == 0:
                    read(("Q", 0), n)
                    read(("Q", 1), n)
                for i in range(QN):
                    u = (f"S{t}", i)
                    c, o = i // (QN // C), QW * (i % (QN // C))
                    refill(u, n)
                    product(bank(u)[:, 0:QW], [(lambda l: q_t[:, l, c, t * P:(t + 1) * P],
                                                lambda l: k_blk[:, l, c, o:o + QW])])\
                        .then_inc(bank_full[BANK[u]], 1)

            def transpose_p(t, n):
                pe.wait_ge(p_ready, 4 * n + t + 1)
                for i in range(3):
                    u = (f"PT{t}", i)
                    refill(u, n)
                    for k in range(4 * i, min(4 * i + 4, NCH)):
                        mm = nc.tensor.transpose(bank(u)[:, (k - 4 * i) * P:(k - 4 * i + 1) * P],
                                                 scr[:, t % 2, k * P:(k + 1) * P], ident[:, :])
                    mm.then_inc(bank_full[BANK[u]], 1)

            def head_outputs(j, n):
                u = (f"PV{j}", 0)
                pe.wait_ge(vblk_loaded, (2 * n + j + 1) * (len(V_PIECES) * 16))
                for i in range(3):
                    read((f"PT{2 * j + 1}", i), n)
                refill(u, n)
                product(bank(u)[:, 0:T], [(lambda l, k=k: v_blk[:, l, k, :], lambda l, k=k: p_t[:, l, k, :])
                                          for k in range(SPLIT)])
                product(bank(u)[:, T:2 * T], [(lambda l, k=k: v_blk[:, l, SPLIT + k - FIRST2, :],
                                               lambda l, k=k: p_t[:, l, k, :]) for k in range(FIRST2, NCH)])\
                    .then_inc(bank_full[BANK[u]], 1)

            def project(n):
                read(("PV0", 0), n)
                read(("PV1", 0), n)
                for i in range(2):
                    u = ("O", i)
                    refill(u, n)
                    for t in (2 * i, 2 * i + 1):
                        mm = product(bank(u)[:, (t % 2) * E:(t % 2 + 1) * E],
                                     [(lambda l, c=c, t=t: xo_t[:, l, c, t * P:(t + 1) * P],
                                       w_half(w_qo, 1, c, 0, E)) for c in range(C)])
                    mm.then_inc(bank_full[BANK[u]], 1)

            def logits(n):
                read(("X2", 0), n)
                read(("X2", 1), n)
                u = ("R", 0)
                refill(u, n)
                product(bank(u)[0:N_ROUTED, :],
                        [(lambda l, c=c: w_rt[:, l, c * N_ROUTED:(c + 1) * N_ROUTED],
                          lambda l, c=c: xo_t[:, l, c, :]) for c in range(C)]).then_inc(bank_full[BANK[u]], 1)

            def logits_rows(n):
                u = ("RT", 0)
                read(("R", 0), n)
                refill(u, n)
                for t in range(TILES):
                    mm = nc.tensor.transpose(bank(u)[:, t * P:(t + 1) * P], scr[:, 1, t * P:(t + 1) * P], ident[:, :])
                mm.then_inc(bank_full[BANK[u]], 1)

            def gate_columns(n):
                u = ("GT", 0)
                pe.wait_ge(router, ROUTER_STEPS * n + ROUTER_STEPS)
                refill(u, n)
                for t in range(TILES):
                    mm = nc.tensor.transpose(bank(u)[0:2 * N_ROUTED, t * P:(t + 1) * P], gate2[:, t, :], ident[:, :])
                mm.then_inc(bank_full[BANK[u]], 1)

            def attention(e, n):
                if e == SLOT["XT"]:
                    transpose_rows("XT", n, 0)
                if e == SLOT["Q"]:
                    queries(n)
                for t in range(TILES):
                    if e == SLOT[f"PT{t}"]:
                        transpose_p(t, n)
                    if t % 2 == 0 and e == SLOT[f"PV{t // 2}"]:
                        head_outputs(t // 2, n)
                for t in range(TILES):
                    if e == SLOT[f"S{t}"]:
                        scores(t, n)
                if e == SLOT["O"]:
                    project(n)
                if e == SLOT["X2"]:
                    transpose_rows("X2", n, 1)
                if e == SLOT["R"]:
                    logits(n)
                if e == SLOT["RT"]:
                    logits_rows(n)
                if e == SLOT["GT"]:
                    gate_columns(n)

            def up(e, g):
                if e == 0:
                    pe.wait_ge(x2_hi, g + 1)
                    pe.wait_ge(x2_lo, g + 1)
                pe.wait_ge(up_read, NE * g + e + 1)
                product(up_ps[e % 2][:, :], [(lambda l, c=c: w_ffn[:, l, e, c * P:(c + 1) * P],
                                              lambda l, c=c: x2_t[:, l, c, :]) for c in range(C)])\
                    .then_inc(up_full, 1)

            def spread_gate(e, g):
                r = e - N_SHARED
                if r == 0:
                    pe.wait_ge(bank_free[BANK[("GT", 0)]], full_count(("GT", 0), g))
                pe.wait_ge(gated, N_ROUTED * g + r + 1)
                nc.tensor.matmul(gt_ps[:, :], pick[:, r, :], gate_t[:, :], start=True, stop=True)\
                    .then_inc(gate_full, 1)

            def down(e, g):
                if e == 0:
                    pe.wait_ge(fout_added, 2 * g + 2)
                pe.wait_ge(h_lo, NE * g + e + 3)
                for m in range(C):
                    mm = product(dn_ps[m][:, :], [(lambda l: w_ffn[:, l, e, 2 * P + m * P:2 * P + (m + 1) * P],
                                                   lambda l: hid[:, e % HB, l, :])],
                                 first=e == 0, last=e == NE - 1)
                mm.then_inc(down_done, 1)

            def ffn_rows(g):
                pe.wait_ge(ffn_read, 2 * g + 2)
                for i in range(2):
                    for t in (2 * i, 2 * i + 1):
                        for m in range(C):
                            mm = nc.tensor.transpose(dn_ps[i][:, (t % 2) * E + m * P:(t % 2) * E + (m + 1) * P],
                                                     ffn_t[:, m, t * P:(t + 1) * P], ident[:, :])
                    mm.then_inc(fout_full, 1)

            for e in range(NE):
                attention(e, 0)
            pe.wait_ge(w_lo, WP)
            pe.wait_ge(picked, 1)
            with pe.Fori(0, G - 1) as g:
                for e in range(NE):
                    up(e, g)
                    if e >= N_SHARED:
                        spread_gate(e, g)
                    attention(e, g + 1)
                    if e >= LAG:
                        down(e - LAG, g)
                for e in range(NE - LAG, NE):
                    down(e, g)
                ffn_rows(g)
            for e in range(NE):
                up(e, G - 1)
                if e >= N_SHARED:
                    spread_gate(e, G - 1)
                if e >= LAG:
                    down(e - LAG, G - 1)
            for e in range(NE - LAG, NE):
                down(e, G - 1)
            ffn_rows(G - 1)


def kernel(x, ctx_1024, fside_Bx16xSxS2_0, fside_SxS2_0, mask_BxS2_bf0, g_xattn, g_ffn, L0_xattn_Wq, L0_xattn_bq,
           L0_xattn_Wk, L0_xattn_bk, L0_xattn_Wv, L0_xattn_bv, L0_xattn_Wo, L0_xattn_bo, L0_ffn_shared_up,
           L0_ffn_shared_down, L0_ffn_routed_up, L0_ffn_routed_down, L0_ffn_router_w):
    import numpy as np
    import concourse.bacc as bacc
    from concourse.bass_utils import run_bass_kernel_spmd

    def by_half(w):
        w = np.asarray(w)
        return w.T.reshape(C, P, w.shape[0]).transpose(1, 0, 2).reshape(P, C * w.shape[0])

    def column(b):
        return np.asarray(b).reshape(C, P).T

    ups = np.concatenate([np.asarray(L0_ffn_shared_up), np.asarray(L0_ffn_routed_up)])
    downs = np.concatenate([np.asarray(L0_ffn_shared_down), np.asarray(L0_ffn_routed_down)])
    up_t = ups.reshape(NE, HID, C, P).transpose(3, 0, 2, 1)
    down_t = downs.transpose(2, 0, 1).reshape(HID, NE, C, P)
    arrays = {
        "x": np.asarray(x).reshape(B * T, E),
        "ctxT": np.asarray(ctx_1024).reshape(CTX, E).T.reshape(C, P, CTX).transpose(1, 0, 2),
        "mask": np.asarray(mask_BxS2_bf0),
        "attn_mask": np.asarray(fside_SxS2_0),
        "g_x": np.asarray(g_xattn).reshape(1, 1),
        "g_f": np.asarray(g_ffn).reshape(1, 1),
        "wkvT": np.concatenate([by_half(L0_xattn_Wk), by_half(L0_xattn_Wv)], axis=1),
        "wqoT": np.concatenate([by_half(L0_xattn_Wq), by_half(L0_xattn_Wo)], axis=1),
        "bqk": np.concatenate([column(L0_xattn_bq), column(L0_xattn_bk)], axis=1),
        "bo": np.asarray(L0_xattn_bo).reshape(1, E),
        "bv": np.asarray(L0_xattn_bv).reshape(1, E),
        "wffn": np.concatenate([up_t.reshape(P, NE, C * P), down_t.reshape(P, NE, C * P)], axis=2).reshape(P, -1),
        "wr": by_half(L0_ffn_router_w),
        "ident": np.eye(P, dtype=np.float32),
        "pick": np.concatenate([np.eye(N_ROUTED), np.eye(N_ROUTED), np.zeros((P - 2 * N_ROUTED, N_ROUTED))])
        .astype(np.float32),
        "iota": np.tile(np.arange(N_ROUTED, dtype=np.float32), (P, 1)),
    }
    arrays = {f"in_{k}": np.ascontiguousarray(v) for k, v in arrays.items()}
    nc = bacc.Bacc("TRN2", target_bir_lowering=False, num_devices=1)
    args = [nc.dram_tensor(k, v.shape, mybir.dt.from_np(v.dtype), kind="ExternalInput").ap()
            for k, v in arrays.items()]
    out = nc.dram_tensor("out_rows", (B * T, E), F32, kind="ExternalOutput").ap()
    block_program(nc, *args, out)
    r = run_bass_kernel_spmd(nc, [arrays], core_ids=[0])
    return r.results[0]["out_rows"].reshape(B, T, E)
```

```python
from contextlib import ExitStack

import concourse.bass as bass
from concourse import mybir

F32 = mybir.dt.float32
FR = mybir.dt.float32r
U8 = mybir.dt.uint8
U32 = mybir.dt.uint32
ALU = mybir.AluOpType
ACT = mybir.ActivationFunctionType
X = mybir.AxisListType.X

B, T, E = 16, 256, 256
H, D, S = 16, 16, 77
N_SHARED, N_ROUTED, TOP_K, HID = 2, 16, 4, 128
NE = N_SHARED + N_ROUTED
LN_EPS = 1e-5
SCALE = D ** -0.5
P = 128

TOK = 512
G = B * T // TOK
TILES = TOK // P
BPG = TOK // T
C = E // P
HPC = H // C
QH = 4
QN = H // QH
QW = QH * S
HS = H * S
NCH = -(-HS // P)
HSP = NCH * P
SPLIT = -(-HPC * S // P)
FIRST2 = HPC * S // P
NSLOT = SPLIT + NCH - FIRST2
HB = 3
LAG = 2
CTX = B * S

HI, LO = 0, 1
PASSES = ((HI, HI), (HI, LO), (LO, HI))

SLOTS = range(LAG, NE + LAG)
AT = {'S0': 2, 'M0': 2.5, 'SH0': 3, 'E0': 3.5, 'N0': 3.5, 'PT0': 5, 'S1': 4, 'M1': 4.5, 'SH1': 5, 'E1': 5.5, 'N1': 6, 'PT1': 7, 'PV0': 8, 'S2': 6, 'M2': 6.5, 'SH2': 7.5, 'E2': 7.5, 'N2': 8, 'PT2': 9, 'S3': 8, 'M3': 8.5, 'SH3': 9, 'E3': 9.5, 'N3': 9.5, 'PT3': 11, 'PV1': 12, 'O': 13.5, 'LN2': 14, 'LN2B': 14.25, 'X2': 15.5, 'R': 16, 'RT': 16.5, 'GATE': 16.75, 'GEXP': 17, 'PICK': 17.5, 'HAND': 17, 'GT': 18.5}
AHEAD = {'LN1': 16.5, 'LN1B': 17.75, 'MASK': 17.5, 'XT': 18.5, 'Q': 19}

NBANK = 3
N_UNITS = {"XT": 2, "Q": 2, "S0": QN, "S1": QN, "PT0": 3, "S2": QN, "PT1": 3, "PV0": 1, "S3": QN, "PT2": 3, "PT3": 3,
           "PV1": 1, "O": 2, "X2": 2, "R": 1, "RT": 1, "GT": 1}


PER_HALF = {"S": 2, "PT": 2, "O": 1, "Q": 1}


def units_at(pos, table, taken=False):
    out = []
    for step in N_UNITS:
        if step in table:
            per = PER_HALF.get(step.rstrip("0123"), N_UNITS[step])
            late = 0.5 if taken and step[:2] == "PV" else 0
            out += [(step, i) for i in range(N_UNITS[step]) if table[step] + late + 0.5 * (i // per) == pos]
    return out


QUARTERS = (0, 0.25, 0.5, 0.75)
POSITIONS = [e + q for e in SLOTS for q in QUARTERS]


def place_units():
    bank_of, use_of, used, last, held = {}, {}, [0] * NBANK, list(range(NBANK)), {}
    for table in (AHEAD, AT):
        for pos in POSITIONS:
            for u in units_at(pos, table):
                k = min((b for b in range(NBANK) if held.get(b, 0) < pos), key=lambda b: last[b])
                bank_of[u], use_of[u] = k, used[k]
                used[k] += 1
                last[k] = NBANK + sum(used)
                if u[0][:2] == "PV":
                    held[k] = pos + 0.5
    return bank_of, use_of, used


BANK, USE, USES = place_units()


def full_count(u, n):
    return n * USES[BANK[u]] + (USE[u] + 1)


def last_in_banks(units):
    return [u for u in units if all(BANK[v] != BANK[u] or USE[v] <= USE[u] for v in units)]


KW = [412, 410, 410]
K_UNITS = [(m, sum(KW[:i]), KW[i]) for i in range(len(KW)) for m in range(C)]
V_UNITS = B // 2

V_PIECES = []
for _h in range(H):
    _r = _h * S
    while _r < (_h + 1) * S:
        _k = _r // P
        _n = min((_h + 1) * S, (_k + 1) * P) - _r
        _slot = _k if _h < HPC else SPLIT + _k - FIRST2
        V_PIECES.append((_h, _r - _h * S, _n, _slot, _r % P))
        _r += _n

WP = NE // 2
ROUTER_STEPS = 18

K_AT = {1: 3.5, 2: 5}
V_AT = {1: 2.75, 2: 3.5, 3: 4, 4: 5.75, 5: 6, 6: 7.25, 7: 7.5}
W_AT = {0: 3, 1: 4.75, 2: 5.75, 3: 6.75, 4: 8, 5: 9.5, 6: 10.5, 7: 11.5, 8: 12.5}
KV_ORDER = [("K", 0), ("K", 1), ("V", 0)]
for _pos in POSITIONS:
    KV_ORDER += [("K", C * j + m) for j in K_AT if K_AT[j] == _pos for m in range(C)]
    KV_ORDER += [("V", i) for i in V_AT if V_AT[i] == _pos]


def full_kv(what, i):
    return KV_ORDER.index((what, i)) + 1


def block_program(nc, x, ctxT, mask, attn_mask, g_x, g_f, wkvT, wqoT, bqk, bo, bv, wffn, wr, ident_c, pick_c, iota_c,
                  out):
    with ExitStack() as es:
        def sb(name, shape, dt=F32):
            return es.enter_context(nc.sbuf_tensor(name, shape, dt))

        def sem(name):
            return es.enter_context(nc.semaphore(name))

        def f32(ap):
            return ap.bitcast(F32)

        k_scr = nc.dram_tensor("k_scr", [2, C, P, CTX], F32, kind="Internal").ap()
        v_scr = nc.dram_tensor("v_scr", [V_UNITS, S, 2, 2 * E], F32, kind="Internal").ap()
        x1_scr = nc.dram_tensor("x1_scr", [G, P, TILES * E], F32, kind="Internal").ap()

        w_ffn = sb("w_ffn", [P, 2, NE, 4 * P], FR)
        w_qo = sb("w_qo", [P, 2, 2, C * E], FR)
        w_rt = sb("w_rt", [P, 2, C * N_ROUTED], FR)
        pick = sb("pick", [P, N_ROUTED, P], FR)
        k_blk = sb("k_blk", [P, 2, C, HPC * S], FR)
        v_blk = sb("v_blk", [P, 2, NSLOT, P], FR)
        p_t = sb("p_t", [P, 2, NCH, 2 * P], FR)
        scr = sb("scr", [P, 2, HSP])
        xo_t = sb("xo_t", [P, 2, C, TOK], FR)
        q_t = sb("q_t", [P, 2, C, TOK], FR)
        x2_t = sb("x2_t", [P, 2, C, TOK], FR)
        gel = sb("gel", [P, 2, TOK])
        hid = sb("hid", [P, HB, 2, TOK], FR)
        gate_t = sb("gate_t", [P, TOK], FR)
        xn = sb("xn", [P, TILES, E])
        x_in = sb("x_in", [P, TILES, E])
        x_res = sb("x_res", [P, TILES, E])
        x_out = sb("x_out", [P, TILES, E])
        ident = sb("ident", [P, P])
        pick_f = sb("pick_f", [P, N_ROUTED])
        iota = sb("iota", [P, N_ROUTED])
        am = sb("am", [P, 2, S])
        mask_u = sb("mask_u", [P, BPG * S], U8)
        mask_f = sb("mask_f", [P, BPG, S])
        am_b = sb("am_b", [P, BPG, 2, S])
        b_qk = sb("b_qk", [P, 2 * C])
        bo_b = sb("bo_b", [P, E])
        bv_b = sb("bv_b", [P, E])
        wr_f = sb("wr_f", [P, C * N_ROUTED])
        g_raw = sb("g_raw", [P, 2])
        g_tan = sb("g_tan", [P, 2])
        neg_half = sb("neg_half", [P, TILES])
        unused = sb("unused", [P, 1])
        st = sb("st", [P, TILES, 6])
        mv = sb("mv", [P, TILES, 2])
        ve = sb("ve", [P, TILES])
        rstd = sb("rstd", [P, TILES])
        mx = sb("mx", [P, 2, H])
        den = sb("den", [P, 2, H])
        rden = sb("rden", [P, 2, H])
        r_max = sb("r_max", [P, TILES])
        r_sum = sb("r_sum", [P, TILES])
        r_rcp = sb("r_rcp", [P, TILES])
        r_exp = sb("r_exp", [P, TILES, N_ROUTED])
        r_prob = sb("r_prob", [P, TILES, N_ROUTED])
        r_top = sb("r_top", [P, TILES, 8])
        r_idx = sb("r_idx", [P, TILES, 8], U32)
        r_idf = sb("r_idf", [P, TILES, 8])
        r_eq = sb("r_eq", [P, TILES, N_ROUTED, TOP_K])
        r_sel = sb("r_sel", [P, TILES, N_ROUTED])
        gate2 = sb("gate2", [P, TILES, 2 * N_ROUTED])

        ctx_raw = scr[:, :, 0:CTX]
        late = 13
        ctx_t = [w_ffn[:, l, late:, :].rearrange("p k n -> p (k n)")[:, 0:C * CTX].rearrange("p (c n) -> p c n", c=C)
                 for l in (HI, LO)]
        v_st = w_ffn[:, :, late - 2:late, :]
        w_kv = hid[:, 0:2, :, :]
        k_st = x2_t
        v_f = x_res[:, :, :].rearrange("p (i j) n -> p i (j n)", i=2)
        kv_raw = x_res
        qo_raw = x_out
        lg_t = scr[0:N_ROUTED, 1, 0:TOK]
        ffn_t = scr[:, 0, 0:C * TOK].rearrange("p (c n) -> p c n", c=C)
        w_stage = [gel[:, :, :].rearrange("p a n -> p (a n)"), x_out[:, :, :].rearrange("p a n -> p (a n)")]

        banks = [es.enter_context(nc.psum_tensor(f"bank{k}", [P, 512], F32)) for k in range(NBANK)]
        up_ps = [es.enter_context(nc.psum_tensor(f"up_ps{k}", [P, 512], F32)) for k in range(2)]
        dn_ps = [es.enter_context(nc.psum_tensor(f"dn_ps{k}", [P, 512], F32)) for k in range(C)]
        gt_ps = es.enter_context(nc.psum_tensor("gt_ps", [P, 512], F32))
        kv_ps = up_ps + dn_ps

        bank_full = [sem(f"bank_full{k}") for k in range(NBANK)]
        bank_free = [sem(f"bank_free{k}") for k in range(NBANK)]
        bias_in, am_in = sem("bias_in"), sem("am_in")
        ident_in, consts_in, ctx_in, kv_in, qo_in, small_in = (sem(s) for s in (
            "ident_in", "consts_in", "ctx_in", "kv_in", "qo_in", "small_in"))
        ctx_rest_in, ctx_rest_lo, kv_full, kv_free = (sem(s) for s in (
            "ctx_rest_in", "ctx_rest_lo", "kv_full", "kv_free"))
        ctx_hi, ctx_lo, kv_hi, kv_lo, qo_hi, qo_lo = (sem(s) for s in (
            "ctx_hi", "ctx_lo", "kv_hi", "kv_lo", "qo_hi", "qo_lo"))
        k_hi, v_hi, v_lo = (sem(s) for s in ("k_hi", "v_hi", "v_lo"))
        k_stored = sem("k_stored")
        v_stored = [sem("v_stored0"), sem("v_stored1")]
        w_in = [sem("w_in0"), sem("w_in1")]
        w_hi, w_lo, zeroed, picked, tan_done, tbo_done = (sem(s) for s in (
            "w_hi", "w_lo", "zeroed", "picked", "tan_done", "tbo_done"))
        x_loaded, mask_loaded, mask_neg, mask_ready = (sem(s) for s in (
            "x_loaded", "mask_loaded", "mask_neg", "mask_ready"))
        ln_stats, ln_aggr, ln_var, ln_rstd, xn_ready, xr_ready = (sem(s) for s in (
            "ln_stats", "ln_aggr", "ln_var", "ln_rstd", "xn_ready", "xr_ready"))
        xt_hi, q_hi, pt_hi, ot_hi = (sem(s) for s in ("xt_hi", "q_hi", "pt_hi", "ot_hi"))
        kblk_loaded, vblk_loaded = sem("kblk_loaded"), sem("vblk_loaded")
        heads_half = sem("heads_half")
        max_done, shifted, exp_done, sum_done, rden_done, p_ready = (sem(s) for s in (
            "max_done", "shifted", "exp_done", "sum_done", "rden_done", "p_ready"))
        router, r_exped = sem("router"), sem("r_exped")
        x2_hi, x2_lo = sem("x2_hi"), sem("x2_lo")
        up_full, up_read, gate_full, gated, h_hi, h_lo, down_done = (sem(s) for s in (
            "up_full", "up_read", "gate_full", "gated", "h_hi", "h_lo", "down_done"))
        ffn_read, fout_full, fout_added = sem("ffn_read"), sem("fout_full"), sem("fout_added")
        xo_loaded, x1_stored, out_stored = sem("xo_loaded"), sem("x1_stored"), sem("out_stored")

        x_v = x.rearrange("(g t p) e -> g p t e", t=TILES, p=P)
        out_v = out.rearrange("(g t p) e -> g p t e", t=TILES, p=P)
        x1_v = x1_scr.rearrange("g p (t e) -> g p t e", t=TILES)
        mask_v = mask.rearrange("(g b) s -> g (b s)", b=BPG)

        def bc_mid(ap, k):
            return ap.unsqueeze(1).to_broadcast([ap.shape[0], k, ap.shape[1]])

        def bc_last(ap, k):
            return ap.unsqueeze(2).to_broadcast([ap.shape[0], ap.shape[1], k])

        def bank(u):
            return banks[BANK[u]]

        def before_all(g):
            return isinstance(g, int) and g < 0

        def kv_bank(what, i):
            return kv_ps[(full_kv(what, i) - 1) % len(kv_ps)]

        block = es.enter_context(nc.Block())

        @block.sync
        def _(sp):
            def load_blocks_k(b):
                for h8 in range(HPC):
                    sp.dma_start(f32(k_blk[D * h8:D * h8 + D, :, :, S * h8:S * h8 + S]).rearrange("p l c s -> p (l c) s"),
                                 k_scr[:, :, D * h8:D * h8 + D, bass.ds(b * S, S)].rearrange("l c p s -> p (l c) s"))\
                        .then_inc(kblk_loaded, 16)

            def load_blocks_v(i, j, before, u, n):
                sp.wait_ge(zeroed, 5)
                sp.wait_ge(heads_half, before)
                v_b = v_scr[bass.ds(i, 1)].rearrange("o s l e -> (o s) l e")
                for h, s0, rows, slot, p0 in V_PIECES:
                    c0 = D * (h % HPC)
                    if h == HPC and s0 == 0:
                        sp.wait_ge(zeroed, 5)
                        sp.wait_ge(bank_full[BANK[u]], full_count(u, n))
                    sp.dma_start(f32(v_blk[p0:p0 + rows, :, slot, c0:c0 + D]),
                                 v_b[s0:s0 + rows, :, j * E + D * h:j * E + D * h + D]).then_inc(vblk_loaded, 16)

            def first_blocks():
                sp.wait_ge(zeroed, 5)
                sp.wait_ge(kv_free, 2)
                for h8 in range(HPC):
                    sp.dma_start(f32(k_blk[D * h8:D * h8 + D, :, :, S * h8:S * h8 + S]).rearrange("p l c s -> p (l c) s"),
                                 f32(k_st[D * h8:D * h8 + D, :, :, 0:S]).rearrange("p l c s -> p (l c) s"))\
                        .then_inc(kblk_loaded, 16)
                off, w = 0, KW[0]
                sp.dma_start(k_scr[:, :, :, off:off + w].rearrange("l c p w -> p (l c) w"),
                             f32(k_st[:, :, :, 0:w]).rearrange("p l c w -> p (l c) w")).then_inc(k_stored, 16)
                sp.wait_ge(v_lo, 1)
                for h, s0, n, slot, p0 in V_PIECES:
                    c0 = D * (h % HPC)
                    sp.dma_start(f32(v_blk[p0:p0 + n, :, slot, c0:c0 + D]),
                                 f32(v_st[s0:s0 + n, :, 0, D * h:D * h + D])).then_inc(vblk_loaded, 16)
                sp.dma_start(v_scr[0], f32(v_st[0:S, :, 0, :])).then_inc(v_stored[0], 16)

            sp.dma_start(kv_raw[:, :, :].rearrange("p a n -> p (a n)"), wkvT).then_inc(kv_in, 16)
            sp.dma_start(ctx_raw[:, :, 0:KW[0]], ctxT[:, :, 0:KW[0]]).then_inc(ctx_in, 16)
            sp.dma_start(x_in[:, :, :], x_v[0]).then_inc(x_loaded, 16)
            sp.dma_start(b_qk[:, :], bqk).then_inc(bias_in, 16)
            sp.dma_start(bv_b[:, :], bv.partition_broadcast(P)).then_inc(bias_in, 16)
            sp.dma_start(ident[:, :], ident_c).then_inc(ident_in, 16)
            sp.dma_start(qo_raw[:, :, :].rearrange("p a n -> p (a n)"), wqoT).then_inc(qo_in, 16)
            sp.dma_start(ctx_raw[:, :, KW[0]:], ctxT[:, :, KW[0]:]).then_inc(ctx_rest_in, 16)
            sp.dma_start(am[:, :, :], attn_mask.rearrange("(t p) s -> p t s", p=P)).then_inc(am_in, 16)
            sp.dma_start(mask_u[:, :], mask_v[0:1, :].to_broadcast([P, BPG * S])).then_inc(mask_loaded, 16)
            sp.dma_start(bo_b[:, :], bo.partition_broadcast(P)).then_inc(small_in, 16)
            sp.dma_start(g_raw[:, 0:1], g_x.partition_broadcast(P)).then_inc(small_in, 16)
            sp.dma_start(g_raw[:, 1:2], g_f.partition_broadcast(P)).then_inc(small_in, 16)
            sp.dma_start(wr_f[:, :], wr).then_inc(small_in, 16)
            first_blocks()
            sp.dma_start(pick_f[:, :], pick_c).then_inc(consts_in, 16)
            sp.dma_start(iota[:, :], iota_c).then_inc(consts_in, 16)

            def body(g, n, ffn=True, ahead=True):
                for pos in POSITIONS:
                    if pos == AT["S1"] + 0.5:
                        u = ("S1", QN - 1)
                        sp.wait_ge(zeroed, 5)
                        sp.wait_ge(bank_full[BANK[u]], full_count(u, n))
                        if before_all(g):
                            sp.wait_ge(k_stored, 16)
                        load_blocks_k(2 * n + 1)
                        if ffn:
                            sp.wait_ge(x1_stored, 16 * g + 16)
                            sp.wait_ge(zeroed, 5)
                            sp.wait_ge(out_stored, 16 * g + 16)
                            sp.dma_start(x_out[:, :, :], x1_v[bass.ds(g, 1)].rearrange("o p t e -> (o p) t e"))\
                                .then_inc(xo_loaded, 16)
                    if pos == AT["PV0"]:
                        if before_all(g):
                            sp.wait_ge(v_stored[0], 16)
                        load_blocks_v(n, 1, 2 * n + 1, ("PV0", 0), n)
                    if pos == AT["S3"] + 0.5 and ahead:
                        u = ("S3", QN - 1)
                        sp.wait_ge(zeroed, 5)
                        sp.wait_ge(bank_full[BANK[u]], full_count(u, n))
                        load_blocks_k(2 * n + 2)
                    if pos == AT["PV1"] and ahead:
                        sp.wait_ge(zeroed, 5)
                        sp.wait_ge(xr_ready, n + 1)
                        sp.wait_ge(zeroed, 5)
                        sp.wait_ge(xn_ready, 8 * n + 4)
                        sp.dma_start(x_in[:, :, :], x_v[bass.ds(n + 1, 1)].rearrange("o p t e -> (o p) t e"))\
                            .then_inc(x_loaded, 16)
                        sp.wait_ge(zeroed, 5)
                        sp.wait_ge(mask_neg, n + 1)
                        sp.dma_start(mask_u[:, :], mask_v[bass.ds(n + 1, 1), :].to_broadcast([P, BPG * S]))\
                            .then_inc(mask_loaded, 16)
                        if before_all(g):
                            sp.wait_ge(v_stored[1], 16)
                        load_blocks_v(n + 1, 0, 2 * n + 2, ("PV1", 0), n)
                    if pos == AT["O"] + 0.5:
                        u = ("O", 1)
                        sp.wait_ge(zeroed, 5)
                        sp.wait_ge(bank_free[BANK[u]], full_count(u, n))
                        sp.dma_start(x1_v[bass.ds(n, 1)].rearrange("o p t e -> (o p) t e"), x_res[:, :, :])\
                            .then_inc(x1_stored, 16)
                if ffn:
                    store_rows(g)

            def store_rows(g):
                sp.wait_ge(zeroed, 5)
                sp.wait_ge(fout_added, 2 * g + 4)
                sp.dma_start(out_v[bass.ds(g, 1)].rearrange("o p t e -> (o p) t e"), x_out[:, :, :])\
                    .then_inc(out_stored, 16)

            body(-1, 0, ffn=False)
            sp.wait_ge(k_stored, 16 * len(KW))
            for k in range(2):
                sp.wait_ge(v_stored[k], 16 * (V_UNITS // 2))
            with sp.Fori(0, G - 2) as g:
                body(g, g + 1)
            body(G - 2, G - 1, ahead=False)
            sp.wait_ge(x1_stored, 16 * G)
            sp.wait_ge(out_stored, 16 * G)
            sp.dma_start(x_out[:, :, :], x1_v[G - 1]).then_inc(xo_loaded, 16)
            store_rows(G - 1)
            sp.wait_ge(out_stored, 16 * G + 16)

        @block.scalar
        def _(act):
            act.wait_ge(kv_in, 16)
            nc.scalar.activation(w_kv[:, HI, :, :].rearrange("p a n -> p (a n)"),
                                 kv_raw[:, :, :].rearrange("p a n -> p (a n)"), ACT.Copy).then_inc(kv_hi, 1)
            act.wait_ge(ctx_in, 16)
            nc.scalar.activation(ctx_t[HI][:, :, 0:KW[0]], ctx_raw[:, :, 0:KW[0]], ACT.Copy).then_inc(ctx_hi, 1)

            def keys_hi(j):
                for i, (m, off, w) in enumerate(K_UNITS[C * j:C * j + C], C * j):
                    act.wait_ge(kv_full, full_kv("K", i))
                    if m == 0 and j == 1:
                        act.wait_ge(kblk_loaded, 16 * HPC)
                    if m == 0 and j > 0:
                        act.wait_ge(k_stored, 16 * j)
                    nc.scalar.activation(k_st[:, HI, m, 0:w], kv_bank("K", i)[:, 0:w], ACT.Identity,
                                         bias=b_qk[:, C + m:C + m + 1]).then_inc(k_hi, 1)

            def values_hi(i):
                act.wait_ge(kv_free, full_kv("V", i))
                if i == 2:
                    act.wait_ge(vblk_loaded, 16 * len(V_PIECES))
                if i >= 2:
                    act.wait_ge(v_stored[i % 2], 16 * (i // 2))
                nc.scalar.activation(v_st[0:S, HI, i % 2, :], v_f[0:S, i % 2, :], ACT.Copy).then_inc(v_hi, 1)

            def store_k(i):
                off, w = sum(KW[:i]), KW[i]
                act.wait_ge(kv_free, full_kv("K", C * i + C - 1))
                nc.scalar.dma_start(k_scr[:, :, :, off:off + w].rearrange("l c p w -> p (l c) w"),
                             f32(k_st[:, :, :, 0:w]).rearrange("p l c w -> p (l c) w")).then_inc(k_stored, 16)

            def store_v(i):
                act.wait_ge(v_lo, i + 1)
                nc.scalar.dma_start(v_scr[i], f32(v_st[0:S, :, i % 2, :])).then_inc(v_stored[i % 2], 16)

            def load_w(p):
                if p == 1:
                    act.wait_ge(qo_lo, 1)
                if p >= 2:
                    act.wait_ge(w_lo, p - 1)
                nc.scalar.dma_start(w_stage[p % 2], wffn[:, p * 2 * 512:(p + 1) * 2 * 512]).then_inc(w_in[p % 2], 16)

            def split_w(p):
                if p == 5:
                    act.wait_ge(v_stored[0], 16 * (V_UNITS // 2))
                    act.wait_ge(v_stored[1], 16 * (V_UNITS // 2))
                if p == 6:
                    act.wait_ge(kv_full, len(K_UNITS) + V_UNITS)
                act.wait_ge(w_in[p % 2], 16 * (p // 2 + 1))
                nc.scalar.activation(w_ffn[:, HI, 2 * p:2 * p + 2, :].rearrange("p a n -> p (a n)"), w_stage[p % 2],
                                     ACT.Copy).then_inc(w_hi, 1)
                if p + 1 < WP and p >= 1:
                    load_w(p + 1)

            def take_xt(u, n):
                act.wait_ge(bank_full[BANK[u]], full_count(u, n))
                nc.scalar.activation(xo_t[:, HI, u[1], :], bank(u)[:, :], ACT.Copy).then_inc(xt_hi, 1)

            def take_q(u, n):
                act.wait_ge(bank_full[BANK[u]], full_count(u, n))
                nc.scalar.activation(q_t[:, HI, u[1], :], bank(u)[:, :], ACT.Identity,
                                     bias=b_qk[:, u[1]:u[1] + 1]).then_inc(q_hi, 1)

            def exps(t, n):
                act.wait_ge(shifted, 4 * n + t + 1)
                nc.scalar.activation(scr[:, t % 2, 0:HS], scr[:, t % 2, 0:HS], ACT.Exp).then_inc(exp_done, 1)

            def take_pt(u, n):
                t, i = int(u[0][2]), u[1]
                k = min(4, NCH - 4 * i)
                act.wait_ge(bank_full[BANK[u]], full_count(u, n))
                nc.scalar.activation(p_t[:, HI, 4 * i:4 * i + k, P * (t % 2):P * (t % 2) + P],
                                     bank(u)[:, 0:k * P].rearrange("p (k n) -> p k n", k=k),
                                     ACT.Copy).then_inc(pt_hi, 1)

            def take_o(u, n):
                j = int(u[0][2])
                act.wait_ge(bank_full[BANK[u]], full_count(u, n))
                nc.scalar.activation(xo_t[:, HI, :, T * j:T * j + T], bank(u)[:, :].rearrange("p (c n) -> p c n", c=C),
                                     ACT.Copy).then_inc(ot_hi, 1)

            def take_logits(u, n):
                act.wait_ge(bank_full[BANK[u]], full_count(u, n))
                nc.scalar.activation(lg_t, bank(u)[0:N_ROUTED, :], ACT.Copy).then_inc(bank_free[BANK[u]], 1)

            def router_exp(n):
                act.wait_ge(bank_free[BANK[("RT", 0)]], full_count(("RT", 0), n))
                nc.scalar.activation(r_exp[:, :, :], r_exp[:, :, :], ACT.Exp).then_inc(r_exped, 1)

            def take_gates(u, n):
                act.wait_ge(bank_full[BANK[u]], full_count(u, n))
                nc.scalar.activation(gate_t[0:2 * N_ROUTED, :], bank(u)[0:2 * N_ROUTED, :], ACT.Copy)\
                    .then_inc(bank_free[BANK[u]], 1)

            def take(u, n):
                if u[0] in ("XT", "X2"):
                    take_xt(u, n)
                elif u[0] == "Q":
                    take_q(u, n)
                elif u[0][:2] == "PT":
                    take_pt(u, n)
                elif u[0][:2] == "PV":
                    take_o(u, n)
                elif u[0] == "R":
                    take_logits(u, n)
                elif u[0] == "GT":
                    take_gates(u, n)

            def attention(pos, n):
                for u in units_at(pos, AT, taken=True):
                    take(u, n)
                for t in range(TILES):
                    if pos == AT[f"E{t}"]:
                        exps(t, n)
                if pos == AT["GEXP"]:
                    router_exp(n)
                if pos == AT["HAND"]:
                    hand_over(n)

            def next_attention(pos, n):
                for u in units_at(pos, AHEAD):
                    take(u, n)

            def hand_over(n):
                if before_all(n - 1):
                    act.wait_ge(k_stored, 16 * len(KW))
                else:
                    act.wait_ge(up_full, NE * n)
                act.wait_ge(xt_hi, 4 * n + 4)
                nc.scalar.activation(x2_t[:, HI, :, :], f32(xo_t[:, HI, :, :]), ACT.Copy).then_inc(x2_hi, 1)

            def gelu(e, g):
                act.wait_ge(up_full, NE * g + e + 1)
                act.wait_ge(h_lo, NE * g + e + 1)
                nc.scalar.activation(gel[:, e % 2, :], up_ps[e % 2][:, :], ACT.Gelu).then_inc(up_read, 1)

            def hidden_hi(e, g):
                if e % NE < N_SHARED:
                    act.wait_ge(up_read, NE * g + e + 3)
                else:
                    act.wait_ge(gated, N_ROUTED * g + e - N_SHARED + 2)
                act.wait_ge(down_done, NE * g + e + 1)
                nc.scalar.activation(hid[:, e % HB, HI, :], gel[:, e % 2, :], ACT.Copy).then_inc(h_hi, 1)

            def take_ffn(g):
                act.wait_ge(down_done, NE * g + NE + HB)
                for m in range(C):
                    nc.scalar.activation(ffn_t[:, m, :], dn_ps[m][:, :], ACT.Copy, scale=g_tan[:, 1:2])\
                        .then_inc(ffn_read, 1)

            def body(g, n, ffn=True, attend=True, ahead=True):
                for e in SLOTS:
                    if ffn and e == SLOTS[-1]:
                        take_ffn(g)
                    if (ffn and e < NE) or (attend and e >= NE):
                        gelu(e, g)
                    for pos in (e + q for q in QUARTERS):
                        if pos == e + 0.5 and ((ffn and e <= NE) or (attend and e > NE)):
                            hidden_hi(e - 1, g)
                        if attend:
                            attention(pos, n)
                        if ahead:
                            next_attention(pos, n + 1)
                        if before_all(g):
                            context_and_weights(pos)

            def context_and_weights(pos):
                for j in K_AT:
                    if pos == K_AT[j]:
                        keys_hi(j)
                    if pos == K_AT[j] + 1:
                        store_k(j)
                for i in V_AT:
                    if pos == V_AT[i]:
                        values_hi(i)
                    if pos == V_AT[i] + 0.75:
                        store_v(i)
                for p in W_AT:
                    if pos == W_AT[p]:
                        split_w(p)

            act.wait_ge(qo_in, 16)
            nc.scalar.activation(w_qo[:, HI, :, :].rearrange("p a n -> p (a n)"),
                                 qo_raw[:, :, :].rearrange("p a n -> p (a n)"), ACT.Copy).then_inc(qo_hi, 1)
            act.wait_ge(bias_in, 32)
            keys_hi(0)
            values_hi(0)
            for c in range(C):
                take(("XT", c), 0)
            act.wait_ge(ctx_rest_in, 16)
            nc.scalar.activation(ctx_t[HI][:, :, KW[0]:], ctx_raw[:, :, KW[0]:], ACT.Copy).then_inc(ctx_hi, 1)
            for m in range(C):
                take(("Q", m), 0)
            load_w(0)
            act.wait_ge(small_in, 4 * 16)
            nc.scalar.activation(w_rt[:, HI, :], wr_f[:, :], ACT.Copy).then_inc(qo_hi, 1)
            nc.scalar.activation(g_tan[:, :], g_raw[:, :], ACT.Tanh).then_inc(tan_done, 1)
            load_w(1)
            body(-1, 0, ffn=False)
            with act.Fori(0, G - 2) as g:
                body(g, g + 1)
            body(G - 2, G - 1, ahead=False)
            body(G - 1, G, attend=False, ahead=False)

        @block.vector
        def _(dve):
            nc.vector.memset(neg_half[:, :], -0.5).then_inc(zeroed, 1)
            nc.vector.memset(scr[:, :, HS:HSP], 0.0).then_inc(zeroed, 1)
            nc.vector.memset(f32(gate_t[:, :]), 0.0).then_inc(zeroed, 1)
            dve.wait_ge(kv_hi, 1)
            nc.vector.tensor_tensor(w_kv[:, LO, :, :].rearrange("p a n -> p (a n)"),
                                    kv_raw[:, :, :].rearrange("p a n -> p (a n)"),
                                    f32(w_kv[:, HI, :, :]).rearrange("p a n -> p (a n)"),
                                    ALU.subtract).then_inc(kv_lo, 1)
            dve.wait_ge(ctx_hi, 1)
            nc.vector.tensor_tensor(ctx_t[LO][:, :, 0:KW[0]], ctx_raw[:, :, 0:KW[0]], f32(ctx_t[HI][:, :, 0:KW[0]]),
                                    ALU.subtract).then_inc(ctx_lo, 1)

            def keys_lo(j):
                for i, (m, off, w) in enumerate(K_UNITS[C * j:C * j + C], C * j):
                    dve.wait_ge(k_hi, i + 1)
                    nc.vector.scalar_tensor_tensor(out=k_st[:, LO, m, 0:w], in0=kv_bank("K", i)[:, 0:w],
                                                   scalar=b_qk[:, C + m:C + m + 1], in1=f32(k_st[:, HI, m, 0:w]),
                                                   op0=ALU.add, op1=ALU.subtract).then_inc(kv_free, 1)

            def values(i):
                dve.wait_ge(kv_full, full_kv("V", i))
                if i >= 2:
                    dve.wait_ge(v_lo, i - 1)
                nc.vector.tensor_tensor(v_f[0:S, i % 2, :].rearrange("p (j n) -> p j n", j=2),
                                        kv_bank("V", i)[0:S, :].rearrange("p (j n) -> p j n", j=2),
                                        bc_mid(bv_b[0:S, :], 2), ALU.add).then_inc(kv_free, 1)

            def additive_mask(n):
                dve.wait_ge(mask_loaded, 16 * n + 16)
                nc.vector.tensor_scalar(mask_f[:, :, :].rearrange("p b s -> p (b s)"), mask_u[:, :], -3e38, 3e38,
                                        ALU.mult, ALU.mult).then_inc(mask_neg, 1)
                dve.wait_ge(mask_neg, n + 1)
                for t in range(2):
                    nc.vector.tensor_tensor(am_b[:, :, t, :], mask_f[:, :, :], bc_mid(am[:, t, :], BPG), ALU.add)\
                        .then_inc(mask_ready, 1)

            def carry_wait():
                nc.vector.memset(unused[:, :], 0.0)

            def norm_stats(src, n, k):
                for t in range(TILES):
                    nc.vector.bn_stats(st[:, t, :], src[:, t, :]).then_inc(ln_stats, 1)
                dve.wait_ge(ln_stats, 8 * n + 4 * k + 4)
                carry_wait()
                for t in range(TILES):
                    nc.vector.bn_aggr(mv[:, t, :], st[:, t, :]).then_inc(ln_aggr, 1)
                dve.wait_ge(ln_aggr, 8 * n + 4 * k + 4)
                nc.vector.tensor_scalar(ve[:, :], mv[:, :, 1], LN_EPS, None, ALU.add).then_inc(ln_var, 1)

            def norm_rows(src, n, k):
                dve.wait_ge(ln_rstd, 2 * n + k + 1)
                for t in range(TILES):
                    nc.vector.tensor_scalar(xn[:, t, :], src[:, t, :], mv[:, t, 0:1], rstd[:, t:t + 1],
                                            ALU.subtract, ALU.mult).then_inc(xn_ready, 1)

            def take_xt(u, n):
                dve.wait_ge(xt_hi, 4 * n + (2 if u[0] == "X2" else 0) + u[1] + 1)
                nc.vector.tensor_tensor(xo_t[:, LO, u[1], :], bank(u)[:, :], f32(xo_t[:, HI, u[1], :]),
                                        ALU.subtract).then_inc(bank_free[BANK[u]], 1)

            def take_q(u, n):
                m = u[1]
                dve.wait_ge(q_hi, 2 * n + m + 1)
                nc.vector.scalar_tensor_tensor(out=q_t[:, LO, m, :], in0=bank(u)[:, :], scalar=b_qk[:, m:m + 1],
                                               in1=f32(q_t[:, HI, m, :]), op0=ALU.add, op1=ALU.subtract)\
                    .then_inc(bank_free[BANK[u]], 1)

            def take_scores(u, n):
                t, i = int(u[0][1]), u[1]
                s = scr[:, t % 2, 0:HS].rearrange("p (h s) -> p h s", h=H)
                if t == 0 and i == 0:
                    dve.wait_ge(mask_ready, 2 * n + 2)
                dve.wait_ge(bank_full[BANK[u]], full_count(u, n))
                nc.vector.scalar_tensor_tensor(out=s[:, QH * i:QH * i + QH, :],
                                               in0=bank(u)[:, 0:QW].rearrange("p (h s) -> p h s", h=QH),
                                               scalar=SCALE, in1=bc_mid(am_b[:, t // 2, t % 2, :], QH),
                                               op0=ALU.mult, op1=ALU.add).then_inc(bank_free[BANK[u]], 1)

            def maximum(t, n):
                s = scr[:, t % 2, 0:HS].rearrange("p (h s) -> p h s", h=H)
                for u in last_in_banks([(f"S{t}", i) for i in range(QN)]):
                    dve.wait_ge(bank_free[BANK[u]], full_count(u, n))
                nc.vector.tensor_reduce(mx[:, t % 2, :], s, X, ALU.max).then_inc(max_done, 1)

            def shift(t, n):
                s = scr[:, t % 2, 0:HS].rearrange("p (h s) -> p h s", h=H)
                dve.wait_ge(max_done, 4 * n + t + 1)
                nc.vector.tensor_tensor(s, s, bc_last(mx[:, t % 2, :], S), ALU.subtract).then_inc(shifted, 1)

            def normal(t, n):
                s = scr[:, t % 2, 0:HS].rearrange("p (h s) -> p h s", h=H)
                dve.wait_ge(exp_done, 4 * n + t + 1)
                nc.vector.tensor_reduce(den[:, t % 2, :], s, X, ALU.add).then_inc(sum_done, 1)
                dve.wait_ge(sum_done, 4 * n + t + 1)
                nc.vector.reciprocal(rden[:, t % 2, :], den[:, t % 2, :]).then_inc(rden_done, 1)

            def take_pt(u, n):
                t, i = int(u[0][2]), u[1]
                k = min(4, NCH - 4 * i)
                dve.wait_ge(pt_hi, 12 * n + 3 * t + i + 1)
                nc.vector.tensor_tensor(p_t[:, LO, 4 * i:4 * i + k, P * (t % 2):P * (t % 2) + P],
                                        bank(u)[:, 0:k * P].rearrange("p (k n) -> p k n", k=k),
                                        f32(p_t[:, HI, 4 * i:4 * i + k, P * (t % 2):P * (t % 2) + P]),
                                        ALU.subtract).then_inc(bank_free[BANK[u]], 1)

            def take_o(u, n):
                j = int(u[0][2])
                dve.wait_ge(ot_hi, 2 * n + j + 1)
                nc.vector.tensor_tensor(xo_t[:, LO, :, T * j:T * j + T],
                                        bank(u)[:, :].rearrange("p (c n) -> p c n", c=C),
                                        f32(xo_t[:, HI, :, T * j:T * j + T]), ALU.subtract)\
                    .then_inc(bank_free[BANK[u]], 1)

            def residual(u, n):
                i = u[1]
                dve.wait_ge(xr_ready, n + 1)
                dve.wait_ge(bank_full[BANK[u]], full_count(u, n))
                nc.vector.scalar_tensor_tensor(out=x_res[:, 2 * i:2 * i + 2, :],
                                               in0=bank(u)[:, :].rearrange("p (t n) -> p t n", t=2),
                                               scalar=g_tan[:, 0:1], in1=x_res[:, 2 * i:2 * i + 2, :],
                                               op0=ALU.mult, op1=ALU.add).then_inc(bank_free[BANK[u]], 1)

            def shift_logits(n):
                u = ("RT", 0)
                lg = bank(u)[:, :].rearrange("p (t n) -> p t n", t=TILES)[:, :, 0:N_ROUTED]
                base = ROUTER_STEPS * n
                dve.wait_ge(bank_full[BANK[u]], full_count(u, n))
                nc.vector.tensor_reduce(r_max[:, :], lg, X, ALU.max).then_inc(router, 1)
                dve.wait_ge(router, base + 1)
                nc.vector.tensor_tensor(r_exp[:, :, :], lg, bc_last(r_max[:, :], N_ROUTED), ALU.subtract)\
                    .then_inc(bank_free[BANK[u]], 1)

            def gates(n):
                base = ROUTER_STEPS * n
                dve.wait_ge(r_exped, n + 1)
                nc.vector.tensor_reduce(r_sum[:, :], r_exp[:, :, :], X, ALU.add).then_inc(router, 1)
                dve.wait_ge(router, base + 2)
                nc.vector.reciprocal(r_rcp[:, :], r_sum[:, :]).then_inc(router, 1)
                dve.wait_ge(router, base + 3)
                nc.vector.tensor_tensor(r_prob[:, :, :], r_exp[:, :, :], bc_last(r_rcp[:, :], N_ROUTED), ALU.mult)\
                    .then_inc(router, 1)
                dve.wait_ge(router, base + 4)
                carry_wait()
                for t in range(TILES):
                    nc.vector.max(r_top[:, t, :], r_prob[:, t, :]).then_inc(router, 1)
                dve.wait_ge(router, base + 8)
                carry_wait()
                for t in range(TILES):
                    nc.vector.max_index(r_idx[:, t, :], r_top[:, t, :], r_prob[:, t, :]).then_inc(router, 1)
                dve.wait_ge(router, base + 12)
                nc.vector.tensor_copy(r_idf[:, :, :], r_idx[:, :, :]).then_inc(router, 1)
                dve.wait_ge(router, base + 13)
                for t in range(TILES):
                    eq = nc.vector.tensor_tensor(r_eq[:, t, :, :], bc_last(iota[:, :], TOP_K),
                                                 bc_mid(r_idf[:, t, 0:TOP_K], N_ROUTED), ALU.is_equal)
                eq.then_inc(router, 1)
                dve.wait_ge(router, base + 14)
                nc.vector.tensor_reduce(r_sel[:, :, :], r_eq[:, :, :, :], X, ALU.max).then_inc(router, 1)
                dve.wait_ge(router, base + 15)
                nc.vector.tensor_tensor(r_prob[:, :, :], r_prob[:, :, :], r_sel[:, :, :], ALU.mult)\
                    .then_inc(router, 1)
                dve.wait_ge(router, base + 16)
                nc.vector.tensor_copy(gate2[:, :, 0:N_ROUTED].bitcast(FR), r_prob[:, :, :]).then_inc(router, 1)
                dve.wait_ge(router, base + 17)
                nc.vector.tensor_tensor(gate2[:, :, N_ROUTED:2 * N_ROUTED], r_prob[:, :, :],
                                        gate2[:, :, 0:N_ROUTED], ALU.subtract).then_inc(router, 1)

            def take(u, n):
                if u[0] in ("XT", "X2"):
                    take_xt(u, n)
                elif u[0] == "Q":
                    take_q(u, n)
                elif u[0][:2] == "PT":
                    take_pt(u, n)
                elif u[0][:2] == "PV":
                    take_o(u, n)
                elif u[0][0] == "S":
                    take_scores(u, n)
                elif u[0] == "O":
                    residual(u, n)

            def attention(pos, n):
                for u in units_at(pos, AT, taken=True):
                    take(u, n)
                for t in range(TILES):
                    if pos == AT[f"SH{t}"]:
                        shift(t, n)
                    if pos == AT[f"N{t}"]:
                        normal(t, n)
                    if pos == AT[f"M{t}"]:
                        maximum(t, n)
                if pos == AT["LN2"]:
                    for u in last_in_banks([("O", 0), ("O", 1)]):
                        dve.wait_ge(bank_free[BANK[u]], full_count(u, n))
                    norm_stats(x_res, n, 1)
                if pos == AT["LN2B"]:
                    norm_rows(x_res, n, 1)
                if pos == AT["GATE"]:
                    shift_logits(n)
                if pos == AT["PICK"]:
                    gates(n)
                if pos == AT["HAND"]:
                    hand_over(n)

            def next_attention(pos, n):
                if pos == AHEAD["LN1"]:
                    dve.wait_ge(x_loaded, 16 * n + 16)
                    norm_stats(x_in, n, 0)
                if pos == AHEAD["LN1B"]:
                    norm_rows(x_in, n, 0)
                if pos == AHEAD["MASK"]:
                    additive_mask(n)
                for u in units_at(pos, AHEAD):
                    take(u, n)

            def hand_over(n):
                if before_all(n - 1):
                    dve.wait_ge(k_stored, 16 * len(KW))
                else:
                    dve.wait_ge(up_full, NE * n)
                for u in last_in_banks([("X2", c) for c in range(C)]):
                    dve.wait_ge(bank_free[BANK[u]], full_count(u, n))
                nc.vector.tensor_copy(x2_t[:, LO, :, :], f32(xo_t[:, LO, :, :])).then_inc(x2_lo, 1)

            def gate(e, g):
                if e >= N_SHARED:
                    dve.wait_ge(up_read, NE * g + e + 3)
                    dve.wait_ge(gate_full, N_ROUTED * g + e - N_SHARED + 1)
                    nc.vector.tensor_tensor(gel[:, e % 2, :], gel[:, e % 2, :], gt_ps[:, :], ALU.mult)\
                        .then_inc(gated, 1)

            def add_ffn(g):
                dve.wait_ge(xo_loaded, 16 * g + 16)
                for i in range(2):
                    dve.wait_ge(fout_full, 2 * g + i + 1)
                    nc.vector.tensor_tensor(x_out[:, 2 * i:2 * i + 2, :], x_out[:, 2 * i:2 * i + 2, :],
                                            dn_ps[i][:, :].rearrange("p (t n) -> p t n", t=2), ALU.add)\
                        .then_inc(fout_added, 1)

            def body(g, n, ffn=True, attend=True, ahead=True):
                for e in SLOTS:
                    for pos in (e + q for q in QUARTERS):
                        if pos == e + 0.25 and ffn and e < NE:
                            gate(e, g)
                        if attend:
                            attention(pos, n)
                        if ahead:
                            next_attention(pos, n + 1)
                        if before_all(g):
                            context(pos)
                if ffn:
                    add_ffn(g)

            def context(pos):
                for j in K_AT:
                    if pos == K_AT[j]:
                        keys_lo(j)
                for i in V_AT:
                    if pos == V_AT[i]:
                        values(i)

            dve.wait_ge(x_loaded, 16)
            norm_stats(x_in, 0, 0)
            dve.wait_ge(bias_in, 32)
            keys_lo(0)
            norm_rows(x_in, 0, 0)
            values(0)
            for step in ("XT", "Q"):
                for i in range(C):
                    take((step, i), 0)
            dve.wait_ge(am_in, 16)
            additive_mask(0)
            dve.wait_ge(tan_done, 1)
            nc.vector.tensor_scalar(bo_b[:, :], bo_b[:, :], g_tan[:, 0:1], None, ALU.mult).then_inc(tbo_done, 1)
            dve.wait_ge(ctx_rest_lo, 1)
            body(-1, 0, ffn=False)
            with dve.Fori(0, G - 2) as g:
                body(g, g + 1)
            body(G - 2, G - 1, ahead=False)
            body(G - 1, G, attend=False, ahead=False)

        @block.gpsimd
        def _(pool):
            nc.gpsimd.memset(f32(k_blk[:, :, :, :]), 0.0).then_inc(zeroed, 1)
            nc.gpsimd.memset(f32(v_blk[:, :, :, :]), 0.0).then_inc(zeroed, 1)
            pool.sem_inc(up_read, 2)
            pool.sem_inc(h_lo, 2)
            pool.sem_inc(down_done, HB)
            pool.sem_inc(fout_added, 2)
            pool.sem_inc(gated, 1)
            pool.sem_inc(out_stored, 16)

            def split_w(p):
                pool.wait_ge(w_hi, p + 1)
                nc.gpsimd.tensor_tensor(w_ffn[:, LO, 2 * p:2 * p + 2, :].rearrange("p a n -> p (a n)"), w_stage[p % 2],
                                        f32(w_ffn[:, HI, 2 * p:2 * p + 2, :]).rearrange("p a n -> p (a n)"),
                                        ALU.subtract).then_inc(w_lo, 1)

            def values_lo(i):
                pool.wait_ge(v_hi, i + 1)
                if i == 2:
                    pool.wait_ge(vblk_loaded, 16 * len(V_PIECES))
                if i >= 2:
                    pool.wait_ge(v_stored[i % 2], 16 * (i // 2))
                nc.gpsimd.tensor_tensor(v_st[0:S, LO, i % 2, :], v_f[0:S, i % 2, :], f32(v_st[0:S, HI, i % 2, :]),
                                        ALU.subtract).then_inc(v_lo, 1)

            def root(n, k):
                pool.wait_ge(ln_var, 2 * n + k + 1)
                nc.gpsimd.tensor_tensor(rstd[:, :], ve[:, :], neg_half[:, :], ALU.pow).then_inc(ln_rstd, 1)

            def rows(n):
                pool.wait_ge(x_loaded, 16 * n + 16)
                if before_all(n - 1):
                    pool.wait_ge(v_lo, V_UNITS)
                else:
                    pool.wait_ge(x1_stored, 16 * n)
                    pool.wait_ge(xn_ready, 8 * n)
                nc.gpsimd.tensor_tensor(x_res[:, :, :], x_in[:, :, :], bc_mid(bo_b[:, :], TILES), ALU.add)\
                    .then_inc(xr_ready, 1)

            def probabilities(t, n):
                s = scr[:, t % 2, 0:HS].rearrange("p (h s) -> p h s", h=H)
                pool.wait_ge(rden_done, 4 * n + t + 1)
                nc.gpsimd.tensor_tensor(s, s, bc_last(rden[:, t % 2, :], S), ALU.mult).then_inc(p_ready, 1)

            def attention(pos, n):
                if pos == (max(V_AT.values()) + 0.5 if before_all(n - 1) else SLOTS[0]):
                    rows(n)
                for t in range(TILES):
                    if pos == AT[f"N{t}"]:
                        probabilities(t, n)
                if pos == AT["LN2"]:
                    root(n, 1)

            def next_attention(pos, n):
                if pos == AHEAD["LN1"]:
                    root(n, 0)

            def hidden_lo(e, g):
                pool.wait_ge(h_hi, NE * g + e + 1)
                nc.gpsimd.tensor_tensor(hid[:, e % HB, LO, :], gel[:, e % 2, :], f32(hid[:, e % HB, HI, :]),
                                        ALU.subtract).then_inc(h_lo, 1)

            def body(g, n, ffn=True, attend=True, ahead=True):
                for e in SLOTS:
                    for pos in (e + q for q in QUARTERS):
                        if pos == e + 0.5 and ((ffn and e <= NE) or (attend and e > NE)):
                            hidden_lo(e - 1, g)
                        if attend:
                            attention(pos, n)
                        if ahead:
                            next_attention(pos, n + 1)
                        if before_all(g):
                            context_and_weights(pos)

            def context_and_weights(pos):
                for i in V_AT:
                    if pos == V_AT[i]:
                        values_lo(i)
                for p in W_AT:
                    if pos == W_AT[p]:
                        split_w(p)
                if pos == AT["X2"]:
                    pool.wait_ge(consts_in, 32)
                    nc.gpsimd.tensor_copy(pick[:, :, :], bc_last(pick_f[:, :], P)).then_inc(picked, 1)

            pool.wait_ge(zeroed, 5)
            root(0, 0)
            pool.wait_ge(qo_hi, 1)
            nc.gpsimd.tensor_tensor(w_qo[:, LO, :, :].rearrange("p a n -> p (a n)"),
                                    qo_raw[:, :, :].rearrange("p a n -> p (a n)"),
                                    f32(w_qo[:, HI, :, :]).rearrange("p a n -> p (a n)"),
                                    ALU.subtract).then_inc(qo_lo, 1)
            values_lo(0)
            pool.wait_ge(ctx_hi, 2)
            nc.gpsimd.tensor_tensor(ctx_t[LO][:, :, KW[0]:], ctx_raw[:, :, KW[0]:],
                                    f32(ctx_t[HI][:, :, KW[0]:]), ALU.subtract).then_inc(ctx_rest_lo, 1)
            pool.wait_ge(qo_hi, 2)
            nc.gpsimd.tensor_tensor(w_rt[:, LO, :], wr_f[:, :], f32(w_rt[:, HI, :]), ALU.subtract).then_inc(qo_lo, 1)
            pool.wait_ge(tbo_done, 1)
            pool.wait_ge(kv_lo, 1)
            body(-1, 0, ffn=False)
            with pool.Fori(0, G - 2) as g:
                body(g, g + 1)
            body(G - 2, G - 1, ahead=False)
            body(G - 1, G, attend=False, ahead=False)

        @block.tensor
        def _(pe):
            def product(dst, pairs, first=True, last=True):
                k = 0
                for lhs, rhs in pairs:
                    for a, b in PASSES:
                        mm = nc.tensor.matmul(dst, lhs(a), rhs(b), start=first and k == 0,
                                              stop=last and k == 3 * len(pairs) - 1)
                        k += 1
                return mm

            def w_half(w, which, c, m0, m1):
                return lambda l: w[:, l, which, c * E + m0:c * E + m1]

            def keys(j):
                if j > 0:
                    pe.wait_ge(ctx_rest_lo, 1)
                for i, (m, off, w) in enumerate(K_UNITS[C * j:C * j + C], C * j):
                    if full_kv("K", i) > len(kv_ps):
                        pe.wait_ge(kv_free, full_kv("K", i) - len(kv_ps))
                    product(kv_bank("K", i)[:, 0:w],
                            [(w_half(w_kv, 0, c, m * P, m * P + P),
                              lambda l, c=c: ctx_t[l][:, c, off:off + w]) for c in range(C)]).then_inc(kv_full, 1)

            def values(i):
                if full_kv("V", i) > len(kv_ps):
                    pe.wait_ge(kv_free, full_kv("V", i) - len(kv_ps))
                for j in range(2):
                    b = 2 * i + j
                    mm = product(kv_bank("V", i)[0:S, j * E:(j + 1) * E],
                                 [(lambda l, c=c: ctx_t[l][:, c, b * S:(b + 1) * S],
                                   w_half(w_kv, 1, c, 0, E)) for c in range(C)])
                mm.then_inc(kv_full, 1)

            def refill(u, n, after=()):
                for v in last_in_banks(after):
                    if BANK[v] != BANK[u]:
                        pe.wait_ge(bank_free[BANK[v]], full_count(v, n))
                pe.wait_ge(bank_free[BANK[u]], full_count(u, n) - 1)

            def transpose_rows(u, n):
                pe.wait_ge(xn_ready, 8 * n + (8 if u[0] == "X2" else 4))
                refill(u, n)
                for t in range(TILES):
                    mm = nc.tensor.transpose(bank(u)[:, t * P:(t + 1) * P], xn[:, t, u[1] * P:(u[1] + 1) * P],
                                             ident[:, :])
                mm.then_inc(bank_full[BANK[u]], 1)

            def queries(u, n):
                m = u[1]
                refill(u, n, after=[("XT", 0), ("XT", 1)])
                product(bank(u)[:, :], [(w_half(w_qo, 0, c, m * P, m * P + P),
                                         lambda l, c=c: xo_t[:, l, c, :]) for c in range(C)])\
                    .then_inc(bank_full[BANK[u]], 1)

            def scores(u, n):
                t, i = int(u[0][1]), u[1]
                if i == 0:
                    pe.wait_ge(kblk_loaded, (2 * n + t // 2 + 1) * (HPC * 16))
                c, o = i // (QN // C), QW * (i % (QN // C))
                refill(u, n, after=[("Q", 0), ("Q", 1)] if t == 0 and i == 0 else [])
                product(bank(u)[:, 0:QW], [(lambda l: q_t[:, l, c, t * P:(t + 1) * P],
                                            lambda l: k_blk[:, l, c, o:o + QW])]).then_inc(bank_full[BANK[u]], 1)

            def transpose_p(u, n):
                t, i = int(u[0][2]), u[1]
                if i == 0:
                    pe.wait_ge(p_ready, 4 * n + t + 1)
                refill(u, n)
                for k in range(4 * i, min(4 * i + 4, NCH)):
                    mm = nc.tensor.transpose(bank(u)[:, (k - 4 * i) * P:(k - 4 * i + 1) * P],
                                             scr[:, t % 2, k * P:(k + 1) * P], ident[:, :])
                mm.then_inc(bank_full[BANK[u]], 1)

            def head_outputs(u, n):
                j = int(u[0][2])
                pe.wait_ge(vblk_loaded, (2 * n + j + 1) * (len(V_PIECES) * 16))
                refill(u, n, after=[(f"PT{2 * j + 1}", i) for i in range(3)])
                product(bank(u)[:, 0:T], [(lambda l, k=k: v_blk[:, l, k, :], lambda l, k=k: p_t[:, l, k, :])
                                          for k in range(SPLIT)]).then_inc(heads_half, 1)

            def head_outputs_2(j):
                u = (f"PV{j}", 0)
                product(bank(u)[:, T:2 * T], [(lambda l, k=k: v_blk[:, l, SPLIT + k - FIRST2, :],
                                               lambda l, k=k: p_t[:, l, k, :]) for k in range(FIRST2, NCH)])\
                    .then_inc(bank_full[BANK[u]], 1)

            def project(u, n):
                refill(u, n, after=[("PV0", 0), ("PV1", 0)])
                for t in (2 * u[1], 2 * u[1] + 1):
                    mm = product(bank(u)[:, (t % 2) * E:(t % 2 + 1) * E],
                                 [(lambda l, c=c, t=t: xo_t[:, l, c, t * P:(t + 1) * P],
                                   w_half(w_qo, 1, c, 0, E)) for c in range(C)])
                mm.then_inc(bank_full[BANK[u]], 1)

            def logits(n):
                u = ("R", 0)
                if before_all(n - 1):
                    pe.wait_ge(qo_lo, 2)
                refill(u, n, after=[("X2", 0), ("X2", 1)])
                product(bank(u)[0:N_ROUTED, :],
                        [(lambda l, c=c: w_rt[:, l, c * N_ROUTED:(c + 1) * N_ROUTED],
                          lambda l, c=c: xo_t[:, l, c, :]) for c in range(C)]).then_inc(bank_full[BANK[u]], 1)

            def logits_rows(n):
                u = ("RT", 0)
                refill(u, n, after=[("R", 0)])
                for t in range(TILES):
                    mm = nc.tensor.transpose(bank(u)[:, t * P:(t + 1) * P], scr[:, 1, t * P:(t + 1) * P], ident[:, :])
                mm.then_inc(bank_full[BANK[u]], 1)

            def gate_columns(n):
                u = ("GT", 0)
                pe.wait_ge(router, ROUTER_STEPS * n + ROUTER_STEPS)
                refill(u, n)
                for t in range(TILES):
                    mm = nc.tensor.transpose(bank(u)[0:2 * N_ROUTED, t * P:(t + 1) * P], gate2[:, t, :], ident[:, :])
                mm.then_inc(bank_full[BANK[u]], 1)

            def fill(u, n):
                if u[0] in ("XT", "X2"):
                    transpose_rows(u, n)
                elif u[0] == "Q":
                    queries(u, n)
                elif u[0][0] == "S":
                    scores(u, n)
                elif u[0][:2] == "PT":
                    transpose_p(u, n)
                elif u[0][:2] == "PV":
                    head_outputs(u, n)
                elif u[0] == "O":
                    project(u, n)
                elif u[0] == "R":
                    logits(n)
                elif u[0] == "RT":
                    logits_rows(n)
                elif u[0] == "GT":
                    gate_columns(n)

            def up(e, g):
                if e == NE:
                    if before_all(g):
                        pe.wait_ge(w_lo, WP)
                    pe.wait_ge(x2_hi, g + 2)
                    pe.wait_ge(x2_lo, g + 2)
                pe.wait_ge(up_read, NE * g + e + 1)
                w = e % NE
                product(up_ps[e % 2][:, :], [(lambda l, c=c: w_ffn[:, l, w, c * P:(c + 1) * P],
                                              lambda l, c=c: x2_t[:, l, c, :]) for c in range(C)])\
                    .then_inc(up_full, 1)

            def spread_gate(e, g):
                r = e - N_SHARED
                if r == 0:
                    pe.wait_ge(picked, 1)
                    pe.wait_ge(bank_free[BANK[("GT", 0)]], full_count(("GT", 0), g))
                pe.wait_ge(gated, N_ROUTED * g + r + 1)
                nc.tensor.matmul(gt_ps[:, :], pick[:, r, :], gate_t[:, :], start=True, stop=True)\
                    .then_inc(gate_full, 1)

            def down(e, g):
                if e == 0:
                    pe.wait_ge(fout_added, 2 * g + 2)
                pe.wait_ge(h_lo, NE * g + e + 3)
                for m in range(C):
                    mm = product(dn_ps[m][:, :], [(lambda l: w_ffn[:, l, e, 2 * P + m * P:2 * P + (m + 1) * P],
                                                   lambda l: hid[:, e % HB, l, :])],
                                 first=e == 0, last=e == NE - 1)
                mm.then_inc(down_done, 1)

            def ffn_rows(g):
                pe.wait_ge(ffn_read, 2 * g + 2)
                for i in range(2):
                    for t in (2 * i, 2 * i + 1):
                        for m in range(C):
                            mm = nc.tensor.transpose(dn_ps[i][:, (t % 2) * E + m * P:(t % 2) * E + (m + 1) * P],
                                                     ffn_t[:, m, t * P:(t + 1) * P], ident[:, :])
                    mm.then_inc(fout_full, 1)

            def body(g, n, ffn=True, attend=True, ahead=True):
                for e in SLOTS:
                    if ffn and e == SLOTS[-1]:
                        down(e - LAG, g)
                    if (ffn and e < NE) or (attend and e >= NE):
                        up(e, g)
                    for pos in (e + q for q in QUARTERS):
                        if pos == e + 0.5 and ffn and e < SLOTS[-1]:
                            if e < NE:
                                spread_gate(e, g)
                            down(e - LAG, g)
                        if attend:
                            for j in range(2):
                                if pos == AT[f"PV{j}"] + 0.5:
                                    head_outputs_2(j)
                            for u in units_at(pos, AT):
                                fill(u, n)
                        if ahead:
                            for u in units_at(pos, AHEAD):
                                fill(u, n + 1)
                        if before_all(g):
                            context(pos)
                if ffn:
                    ffn_rows(g)

            def context(pos):
                for j in K_AT:
                    if pos == K_AT[j]:
                        keys(j)
                for i in V_AT:
                    if pos == V_AT[i]:
                        values(i)

            pe.wait_ge(ctx_lo, 1)
            pe.wait_ge(kv_lo, 1)
            keys(0)
            values(0)
            pe.wait_ge(ident_in, 16)
            fill(("XT", 0), 0)
            fill(("XT", 1), 0)
            pe.wait_ge(qo_lo, 1)
            fill(("Q", 0), 0)
            fill(("Q", 1), 0)
            body(-1, 0, ffn=False)
            with pe.Fori(0, G - 2) as g:
                body(g, g + 1)
            body(G - 2, G - 1, ahead=False)
            body(G - 1, G, attend=False, ahead=False)


def kernel(x, ctx_1024, fside_Bx16xSxS2_0, fside_SxS2_0, mask_BxS2_bf0, g_xattn, g_ffn, L0_xattn_Wq, L0_xattn_bq,
           L0_xattn_Wk, L0_xattn_bk, L0_xattn_Wv, L0_xattn_bv, L0_xattn_Wo, L0_xattn_bo, L0_ffn_shared_up,
           L0_ffn_shared_down, L0_ffn_routed_up, L0_ffn_routed_down, L0_ffn_router_w):
    import numpy as np
    import concourse.bacc as bacc
    from concourse.bass_utils import run_bass_kernel_spmd

    def by_half(w):
        w = np.asarray(w)
        return w.T.reshape(C, P, w.shape[0]).transpose(1, 0, 2).reshape(P, C * w.shape[0])

    def column(b):
        return np.asarray(b).reshape(C, P).T

    ups = np.concatenate([np.asarray(L0_ffn_shared_up), np.asarray(L0_ffn_routed_up)])
    downs = np.concatenate([np.asarray(L0_ffn_shared_down), np.asarray(L0_ffn_routed_down)])
    up_t = ups.reshape(NE, HID, C, P).transpose(3, 0, 2, 1)
    down_t = downs.transpose(2, 0, 1).reshape(HID, NE, C, P)
    arrays = {
        "x": np.asarray(x).reshape(B * T, E),
        "ctxT": np.asarray(ctx_1024).reshape(CTX, E).T.reshape(C, P, CTX).transpose(1, 0, 2),
        "mask": np.asarray(mask_BxS2_bf0),
        "attn_mask": np.asarray(fside_SxS2_0),
        "g_x": np.asarray(g_xattn).reshape(1, 1),
        "g_f": np.asarray(g_ffn).reshape(1, 1),
        "wkvT": np.concatenate([by_half(L0_xattn_Wk), by_half(L0_xattn_Wv)], axis=1),
        "wqoT": np.concatenate([by_half(L0_xattn_Wq), by_half(L0_xattn_Wo)], axis=1),
        "bqk": np.concatenate([column(L0_xattn_bq), column(L0_xattn_bk)], axis=1),
        "bo": np.asarray(L0_xattn_bo).reshape(1, E),
        "bv": np.asarray(L0_xattn_bv).reshape(1, E),
        "wffn": np.concatenate([up_t.reshape(P, NE, C * P), down_t.reshape(P, NE, C * P)], axis=2).reshape(P, -1),
        "wr": by_half(L0_ffn_router_w),
        "ident": np.eye(P, dtype=np.float32),
        "pick": np.concatenate([np.eye(N_ROUTED), np.eye(N_ROUTED), np.zeros((P - 2 * N_ROUTED, N_ROUTED))])
        .astype(np.float32),
        "iota": np.tile(np.arange(N_ROUTED, dtype=np.float32), (P, 1)),
    }
    arrays = {f"in_{k}": np.ascontiguousarray(v) for k, v in arrays.items()}
    nc = bacc.Bacc("TRN2", target_bir_lowering=False, num_devices=1)
    args = [nc.dram_tensor(k, v.shape, mybir.dt.from_np(v.dtype), kind="ExternalInput").ap()
            for k, v in arrays.items()]
    out = nc.dram_tensor("out_rows", (B * T, E), F32, kind="ExternalOutput").ap()
    block_program(nc, *args, out)
    r = run_bass_kernel_spmd(nc, [arrays], core_ids=[0])
    return r.results[0]["out_rows"].reshape(B, T, E)
```

```python
from contextlib import ExitStack

import concourse.bass as bass
from concourse import mybir

F32 = mybir.dt.float32
FR = mybir.dt.float32r
U8 = mybir.dt.uint8
U32 = mybir.dt.uint32
ALU = mybir.AluOpType
ACT = mybir.ActivationFunctionType
X = mybir.AxisListType.X

B, T, E = 16, 256, 256
H, D, S = 16, 16, 77
N_SHARED, N_ROUTED, TOP_K, HID = 2, 16, 4, 128
NE = N_SHARED + N_ROUTED
LN_EPS = 1e-5
SCALE = D ** -0.5
P = 128

TOK = 512
G = B * T // TOK
TILES = TOK // P
BPG = TOK // T
C = E // P
HPC = H // C
QH = 4
QN = H // QH
QW = QH * S
HS = H * S
NCH = -(-HS // P)
HSP = NCH * P
SPLIT = -(-HPC * S // P)
FIRST2 = HPC * S // P
NSLOT = SPLIT + NCH - FIRST2
HB = 3
LAG = 2
CTX = B * S
POOL_HEADS = 8

HI, LO = 0, 1
PASSES = ((HI, HI), (HI, LO), (LO, HI))

SLOTS = range(LAG, NE + LAG)
AT = {"S0": 2, "M0": 2.5, "SH0": 3, "E0": 3.5, "S1": 3.5, "N0": 3.75, "M1": 4.25, "SH1": 4.75, "PT0": 5, "E1": 5.5,
      "N1": 6, "S2": 6, "PT1": 6.5, "M2": 6.75, "SH2": 7.5, "E2": 7.75, "PV0": 8, "N2": 8, "S3": 8, "M3": 8.5,
      "SH3": 9, "E3": 9.5, "N3": 9.5, "O0": 9.5, "PT2": 10, "LN20": 10.5, "PT3": 11, "LN20B": 11.25, "PV1": 12,
      "X20": 12.5, "O1": 13, "LN21": 14, "LN21B": 14.5, "X21": 15, "R": 16, "RT": 16.5, "GEXP": 16.5, "GATE": 16.75,
      "HAND": 17, "PICK": 17.5, "GT": 18.5}
AHEAD = {"LN1": 15.5, "LN1B": 16.75, "XT": 17.5, "MASK": 18.5, "Q": 18.5}

FIRST_AT = {"M0": 2.75, "SH0": 3, "E0": 3.25, "N0": 3.75, "M1": 4, "SH1": 4.75, "E1": 4.75, "N1": 6, "M2": 6.5,
            "SH2": 7.25, "E2": 7.25, "N2": 8.25, "M3": 8.5, "SH3": 8.75, "N3": 9.25, "E3": 9.75, "LN20": 10.5,
            "LN20B": 11, "LN21": 14.25, "LN21B": 14.75, "HAND": 15.75, "GEXP": 16, "GATE": 17.25, "PICK": 17.5}
FIRST = {**AT, **FIRST_AT}

NBANK = 3
N_UNITS = {"XT": 2, "Q": 2, "S0": QN, "S1": QN, "PT0": 3, "S2": QN, "PT1": 3, "PV0": 1, "S3": QN, "PT2": 3, "PT3": 3,
           "PV1": 1, "O0": 1, "O1": 1, "X20": 1, "X21": 1, "R": 1, "RT": 1, "GT": 1}


PER_HALF = {"S": 2, "PT": 2, "Q": 1}


def units_at(pos, table, taken=False):
    out = []
    for step in N_UNITS:
        if step in table:
            per = PER_HALF.get(step.rstrip("0123"), N_UNITS[step])
            late = 0.5 if taken and step[:2] == "PV" else 0
            out += [(step, i) for i in range(N_UNITS[step]) if table[step] + late + 0.5 * (i // per) == pos]
    return out


QUARTERS = (0, 0.25, 0.5, 0.75)
POSITIONS = [e + q for e in SLOTS for q in QUARTERS]


def place_units():
    bank_of, use_of, used, last, held = {}, {}, [0] * NBANK, list(range(NBANK)), {}
    for table in (AHEAD, AT):
        for pos in POSITIONS:
            for u in units_at(pos, table):
                k = min((b for b in range(NBANK) if held.get(b, 0) < pos), key=lambda b: last[b])
                bank_of[u], use_of[u] = k, used[k]
                used[k] += 1
                last[k] = NBANK + sum(used)
                if u[0][:2] == "PV":
                    held[k] = pos + 0.5
    return bank_of, use_of, used


BANK, USE, USES = place_units()


def full_count(u, n):
    return n * USES[BANK[u]] + (USE[u] + 1)


def last_in_banks(units):
    return [u for u in units if all(BANK[v] != BANK[u] or USE[v] <= USE[u] for v in units)]


KW = [412, 410, 410]
K_UNITS = [(m, sum(KW[:i]), KW[i]) for i in range(len(KW)) for m in range(C)]
V_UNITS = B // 2
VB = 3

V_PIECES = []
for _h in range(H):
    _r = _h * S
    while _r < (_h + 1) * S:
        _k = _r // P
        _n = min((_h + 1) * S, (_k + 1) * P) - _r
        _slot = _k if _h < HPC else SPLIT + _k - FIRST2
        V_PIECES.append((_h, _r - _h * S, _n, _slot, _r % P))
        _r += _n
V_LOADS = [sum(1 for p in V_PIECES if p[0] // HPC == c) for c in range(C)]

WP = NE // 2
ROUTER_STEPS = 18

NORMS = [range(TILES), range(0, 2), range(2, 4)]

K_AT = {1: 3, 2: 5}
V_AT = {1: 2.75, 2: 4.25, 3: 6, 4: 6, 5: 6.75, 6: 7, 7: 7.5}
W_AT = {0: 3.5, 1: 5, 2: 5.5, 3: 7, 4: 8.5, 5: 10.25, 6: 10.75, 7: 11.5, 8: 12.25}
V_LO_AT = {1: 3.25, 2: 4.25, 3: 6, 4: 6.5, 5: 7.5, 6: 7.5, 7: 8.75}
W_LO_AT = {0: 3.25, 1: 5.5, 2: 7, 3: 7.5, 4: 8.75, 5: 9.75, 6: 12, 7: 12.25, 8: 12.75}
KV_ORDER = [("K", 0), ("K", 1), ("V", 0)]
for _pos in POSITIONS:
    KV_ORDER += [("K", C * j + m) for j in K_AT if K_AT[j] == _pos for m in range(C)]
    KV_ORDER += [("V", i) for i in V_AT if V_AT[i] == _pos]


def full_kv(what, i):
    return KV_ORDER.index((what, i)) + 1


def block_program(nc, x, ctxT, mask, attn_mask, g_x, g_f, wkvT, wqoT, bqk, bo, bv, wffn, wr, ident_c, pick_c, iota_c,
                  out):
    with ExitStack() as es:
        def sb(name, shape, dt=F32):
            return es.enter_context(nc.sbuf_tensor(name, shape, dt))

        def sem(name):
            return es.enter_context(nc.semaphore(name))

        def f32(ap):
            return ap.bitcast(F32)

        k_scr = nc.dram_tensor("k_scr", [2, C, P, CTX], F32, kind="Internal").ap()
        v_scr = nc.dram_tensor("v_scr", [V_UNITS, S, 2, 2 * E], F32, kind="Internal").ap()
        x1_scr = nc.dram_tensor("x1_scr", [G, P, TILES * E], F32, kind="Internal").ap()

        w_ffn = sb("w_ffn", [P, 2, NE, 4 * P], FR)
        w_qo = sb("w_qo", [P, 2, 2, C * E], FR)
        w_rt = sb("w_rt", [P, 2, C * N_ROUTED], FR)
        pick = sb("pick", [P, N_ROUTED, P], FR)
        k_blk = sb("k_blk", [P, 2, C, HPC * S], FR)
        v_blk = sb("v_blk", [P, 2, NSLOT, P], FR)
        p_t = sb("p_t", [P, 2, NCH, 2 * P], FR)
        scr = sb("scr", [P, 2, HSP])
        xo_t = sb("xo_t", [P, 2, C, TOK], FR)
        q_t = sb("q_t", [P, 2, C, TOK], FR)
        x2_t = sb("x2_t", [P, 2, C, TOK], FR)
        gel = sb("gel", [P, 2, TOK])
        hid = sb("hid", [P, HB, 2, TOK], FR)
        gate_t = sb("gate_t", [P, TOK], FR)
        xn = sb("xn", [P, TILES, E])
        x_in = sb("x_in", [P, TILES, E])
        x_res = sb("x_res", [P, TILES, E])
        x_out = sb("x_out", [P, TILES, E])
        ident = sb("ident", [P, P])
        pick_f = sb("pick_f", [P, N_ROUTED])
        iota = sb("iota", [P, N_ROUTED])
        am = sb("am", [P, 2, S])
        mask_u = sb("mask_u", [P, BPG * S], U8)
        mask_f = sb("mask_f", [P, BPG, S])
        am_b = sb("am_b", [P, BPG, 2, S])
        b_qk = sb("b_qk", [P, 2 * C])
        bo_b = sb("bo_b", [P, E])
        bv_b = sb("bv_b", [P, E])
        wr_f = sb("wr_f", [P, C * N_ROUTED])
        g_raw = sb("g_raw", [P, 2])
        g_tan = sb("g_tan", [P, 2])
        neg_half = sb("neg_half", [P, TILES])
        unused = sb("unused", [P, 1])
        st = sb("st", [P, TILES, 6])
        mv = sb("mv", [P, TILES, 2])
        ve = sb("ve", [P, TILES])
        rstd = sb("rstd", [P, TILES])
        mx = sb("mx", [P, 2, H])
        den = sb("den", [P, 2, H])
        rden = sb("rden", [P, 2, H])
        r_max = sb("r_max", [P, TILES])
        r_sum = sb("r_sum", [P, TILES])
        r_rcp = sb("r_rcp", [P, TILES])
        r_exp = sb("r_exp", [P, TILES, N_ROUTED])
        r_prob = sb("r_prob", [P, TILES, N_ROUTED])
        r_top = sb("r_top", [P, TILES, 8])
        r_idx = sb("r_idx", [P, TILES, 8], U32)
        r_idf = sb("r_idf", [P, TILES, 8])
        r_eq = sb("r_eq", [P, TILES, N_ROUTED, TOP_K])
        r_sel = sb("r_sel", [P, TILES, N_ROUTED])
        gate2 = sb("gate2", [P, TILES, 2 * N_ROUTED])

        ctx_raw = scr[:, :, 0:CTX]
        late = 13
        ctx_t = [w_ffn[:, l, late:, :].rearrange("p k n -> p (k n)")[:, 0:C * CTX].rearrange("p (c n) -> p c n", c=C)
                 for l in (HI, LO)]
        v_st = w_ffn[:, :, late - VB:late, :]
        w_kv = hid[:, 0:2, :, :]
        k_st = x2_t
        v_f = x_res[:, :, :].rearrange("p (i j) n -> p i (j n)", i=2)
        kv_raw = x_res
        qo_raw = x_out
        lg_t = scr[0:N_ROUTED, 1, 0:TOK]
        ffn_t = scr[:, 0, 0:C * TOK].rearrange("p (c n) -> p c n", c=C)
        w_stage = [gel[:, :, :].rearrange("p a n -> p (a n)"), x_out[:, :, :].rearrange("p a n -> p (a n)")]

        banks = [es.enter_context(nc.psum_tensor(f"bank{k}", [P, 512], F32)) for k in range(NBANK)]
        up_ps = [es.enter_context(nc.psum_tensor(f"up_ps{k}", [P, 512], F32)) for k in range(2)]
        dn_ps = [es.enter_context(nc.psum_tensor(f"dn_ps{k}", [P, 512], F32)) for k in range(C)]
        gt_ps = es.enter_context(nc.psum_tensor("gt_ps", [P, 512], F32))
        kv_ps = up_ps + dn_ps

        bank_full = [sem(f"bank_full{k}") for k in range(NBANK)]
        bank_free = [sem(f"bank_free{k}") for k in range(NBANK)]
        bias_in, am_in = sem("bias_in"), sem("am_in")
        ident_in, consts_in, ctx_in, kv_in, qo_in, small_in = (sem(s) for s in (
            "ident_in", "consts_in", "ctx_in", "kv_in", "qo_in", "small_in"))
        ctx_rest_in, ctx_rest_lo, kv_full, kv_free = (sem(s) for s in (
            "ctx_rest_in", "ctx_rest_lo", "kv_full", "kv_free"))
        ctx_hi, ctx_lo, kv_hi, kv_lo, qo_hi, qo_lo = (sem(s) for s in (
            "ctx_hi", "ctx_lo", "kv_hi", "kv_lo", "qo_hi", "qo_lo"))
        k_hi, v_hi, v_lo = (sem(s) for s in ("k_hi", "v_hi", "v_lo"))
        k_stored = sem("k_stored")
        v_stored = [sem(f"v_stored{k}") for k in range(VB)]
        w_in = [sem("w_in0"), sem("w_in1")]
        w_hi, w_lo, zeroed, picked, tan_done, tbo_done = (sem(s) for s in (
            "w_hi", "w_lo", "zeroed", "picked", "tan_done", "tbo_done"))
        x_loaded, mask_loaded, mask_neg, mask_ready = (sem(s) for s in (
            "x_loaded", "mask_loaded", "mask_neg", "mask_ready"))
        ln_stats, ln_aggr, ln_var, ln_rstd, xn_ready, xr_ready = (sem(s) for s in (
            "ln_stats", "ln_aggr", "ln_var", "ln_rstd", "xn_ready", "xr_ready"))
        xt_hi, q_hi, pt_hi, ot_hi = (sem(s) for s in ("xt_hi", "q_hi", "pt_hi", "ot_hi"))
        kblk_loaded, vblk_loaded = sem("kblk_loaded"), [sem("vblk_loaded0"), sem("vblk_loaded1")]
        heads_half = sem("heads_half")
        max_done, shifted, exp_done, sum_done, rden_done, p_ready = (sem(s) for s in (
            "max_done", "shifted", "exp_done", "sum_done", "rden_done", "p_ready"))
        router, r_exped = sem("router"), sem("r_exped")
        x2_hi, x2_lo = sem("x2_hi"), sem("x2_lo")
        up_full, up_read, gate_full, gated, h_hi, h_lo, down_done = (sem(s) for s in (
            "up_full", "up_read", "gate_full", "gated", "h_hi", "h_lo", "down_done"))
        ffn_read, fout_full, fout_added = sem("ffn_read"), sem("fout_full"), sem("fout_added")
        xo_loaded, x1_stored, out_stored = sem("xo_loaded"), sem("x1_stored"), sem("out_stored")

        x_v = x.rearrange("(g t p) e -> g p t e", t=TILES, p=P)
        out_v = out.rearrange("(g t p) e -> g p t e", t=TILES, p=P)
        x1_v = x1_scr.rearrange("g p (t e) -> g p t e", t=TILES)
        mask_v = mask.rearrange("(g b) s -> g (b s)", b=BPG)

        def bc_mid(ap, k):
            return ap.unsqueeze(1).to_broadcast([ap.shape[0], k, ap.shape[1]])

        def bc_last(ap, k):
            return ap.unsqueeze(2).to_broadcast([ap.shape[0], ap.shape[1], k])

        def bank(u):
            return banks[BANK[u]]

        def before_all(g):
            return isinstance(g, int) and g < 0

        def kv_bank(what, i):
            return kv_ps[(full_kv(what, i) - 1) % len(kv_ps)]

        block = es.enter_context(nc.Block())

        @block.sync
        def _(sp):
            def load_blocks_k(b):
                for h8 in range(HPC):
                    sp.dma_start(f32(k_blk[D * h8:D * h8 + D, :, :, S * h8:S * h8 + S])
                                 .rearrange("p l c s -> p (l c) s"),
                                 k_scr[:, :, D * h8:D * h8 + D, bass.ds(b * S, S)].rearrange("l c p s -> p (l c) s"))\
                        .then_inc(kblk_loaded, 16)

            def load_blocks_v(i, j, before, u, n):
                sp.wait_ge(zeroed, 5)
                sp.wait_ge(heads_half, before)
                v_b = v_scr[bass.ds(i, 1)].rearrange("o s l e -> (o s) l e")
                for h, s0, rows, slot, p0 in V_PIECES:
                    c0 = D * (h % HPC)
                    if h == HPC and s0 == 0:
                        sp.wait_ge(zeroed, 5)
                        sp.wait_ge(bank_full[BANK[u]], full_count(u, n))
                    sp.dma_start(f32(v_blk[p0:p0 + rows, :, slot, c0:c0 + D]),
                                 v_b[s0:s0 + rows, :, j * E + D * h:j * E + D * h + D])\
                        .then_inc(vblk_loaded[h // HPC], 16)

            def first_blocks():
                sp.wait_ge(zeroed, 5)
                sp.wait_ge(kv_free, 2)
                for h8 in range(HPC):
                    sp.dma_start(f32(k_blk[D * h8:D * h8 + D, :, :, S * h8:S * h8 + S])
                                 .rearrange("p l c s -> p (l c) s"),
                                 f32(k_st[D * h8:D * h8 + D, :, :, 0:S]).rearrange("p l c s -> p (l c) s"))\
                        .then_inc(kblk_loaded, 16)
                off, w = 0, KW[0]
                sp.dma_start(k_scr[:, :, :, off:off + w].rearrange("l c p w -> p (l c) w"),
                             f32(k_st[:, :, :, 0:w]).rearrange("p l c w -> p (l c) w")).then_inc(k_stored, 16)
                sp.wait_ge(v_lo, 1)
                for h, s0, n, slot, p0 in V_PIECES:
                    c0 = D * (h % HPC)
                    if h == HPC and s0 == 0:
                        sp.wait_ge(bank_full[BANK[("S1", QN - 1)]], full_count(("S1", QN - 1), 0))
                        sp.wait_ge(k_stored, 16)
                        load_blocks_k(1)
                    sp.dma_start(f32(v_blk[p0:p0 + n, :, slot, c0:c0 + D]),
                                 f32(v_st[s0:s0 + n, :, 0, D * h:D * h + D])).then_inc(vblk_loaded[h // HPC], 16)
                sp.dma_start(v_scr[0], f32(v_st[0:S, :, 0, :])).then_inc(v_stored[0], 16)

            sp.dma_start(kv_raw[:, :, :].rearrange("p a n -> p (a n)"), wkvT).then_inc(kv_in, 16)
            sp.dma_start(ctx_raw[:, :, 0:KW[0]], ctxT[:, :, 0:KW[0]]).then_inc(ctx_in, 16)
            sp.dma_start(x_in[:, :, :], x_v[0]).then_inc(x_loaded, 16)
            sp.dma_start(b_qk[:, :], bqk).then_inc(bias_in, 16)
            sp.dma_start(bv_b[:, :], bv.partition_broadcast(P)).then_inc(bias_in, 16)
            sp.dma_start(ident[:, :], ident_c).then_inc(ident_in, 16)
            sp.dma_start(qo_raw[:, :, :].rearrange("p a n -> p (a n)"), wqoT).then_inc(qo_in, 16)
            sp.dma_start(ctx_raw[:, :, KW[0]:], ctxT[:, :, KW[0]:]).then_inc(ctx_rest_in, 16)
            sp.dma_start(am[:, :, :], attn_mask.rearrange("(t p) s -> p t s", p=P)).then_inc(am_in, 16)
            sp.dma_start(mask_u[:, :], mask_v[0:1, :].to_broadcast([P, BPG * S])).then_inc(mask_loaded, 16)
            sp.dma_start(bo_b[:, :], bo.partition_broadcast(P)).then_inc(small_in, 16)
            sp.dma_start(g_raw[:, 0:1], g_x.partition_broadcast(P)).then_inc(small_in, 16)
            sp.dma_start(g_raw[:, 1:2], g_f.partition_broadcast(P)).then_inc(small_in, 16)
            sp.dma_start(wr_f[:, :], wr).then_inc(small_in, 16)
            first_blocks()
            sp.dma_start(pick_f[:, :], pick_c).then_inc(consts_in, 16)
            sp.dma_start(iota[:, :], iota_c).then_inc(consts_in, 16)

            def body(g, n, ffn=True, ahead=True):
                for pos in POSITIONS:
                    if pos == AT["S1"] + 0.5 and not before_all(g):
                        u = ("S1", QN - 1)
                        sp.wait_ge(zeroed, 5)
                        sp.wait_ge(bank_full[BANK[u]], full_count(u, n))
                        load_blocks_k(2 * n + 1)
                        if ffn:
                            sp.wait_ge(x1_stored, 16 * g + 16)
                            sp.wait_ge(zeroed, 5)
                            sp.wait_ge(out_stored, 16 * g + 16)
                            sp.dma_start(x_out[:, :, :], x1_v[bass.ds(g, 1)].rearrange("o p t e -> (o p) t e"))\
                                .then_inc(xo_loaded, 16)
                    if pos == AT["PV0"]:
                        if before_all(g):
                            sp.wait_ge(v_stored[0], 16)
                        load_blocks_v(n, 1, 2 * n + 1, ("PV0", 0), n)
                    if pos == AT["S3"] + 0.5 and ahead:
                        u = ("S3", QN - 1)
                        sp.wait_ge(zeroed, 5)
                        sp.wait_ge(bank_full[BANK[u]], full_count(u, n))
                        load_blocks_k(2 * n + 2)
                    if pos == AT["PV1"] and ahead:
                        sp.wait_ge(zeroed, 5)
                        sp.wait_ge(xr_ready, n + 1)
                        sp.wait_ge(zeroed, 5)
                        sp.wait_ge(xn_ready, 8 * n + 4)
                        sp.dma_start(x_in[:, :, :], x_v[bass.ds(n + 1, 1)].rearrange("o p t e -> (o p) t e"))\
                            .then_inc(x_loaded, 16)
                        sp.wait_ge(zeroed, 5)
                        sp.wait_ge(mask_neg, n + 1)
                        sp.dma_start(mask_u[:, :], mask_v[bass.ds(n + 1, 1), :].to_broadcast([P, BPG * S]))\
                            .then_inc(mask_loaded, 16)
                        if before_all(g):
                            sp.wait_ge(v_stored[1], 16)
                        load_blocks_v(n + 1, 0, 2 * n + 2, ("PV1", 0), n)
                    if pos == AT["O1"]:
                        u = ("O1", 0)
                        sp.wait_ge(zeroed, 5)
                        sp.wait_ge(bank_free[BANK[u]], full_count(u, n))
                        sp.dma_start(x1_v[bass.ds(n, 1)].rearrange("o p t e -> (o p) t e"), x_res[:, :, :])\
                            .then_inc(x1_stored, 16)
                if ffn:
                    store_rows(g)

            def store_rows(g):
                sp.wait_ge(zeroed, 5)
                sp.wait_ge(fout_added, 2 * g + 4)
                sp.dma_start(out_v[bass.ds(g, 1)].rearrange("o p t e -> (o p) t e"), x_out[:, :, :])\
                    .then_inc(out_stored, 16)

            body(-1, 0, ffn=False)
            sp.wait_ge(k_stored, 16 * len(KW))
            for k in range(VB):
                sp.wait_ge(v_stored[k], 16 * len(range(k, V_UNITS, VB)))
            with sp.Fori(0, G - 2) as g:
                body(g, g + 1)
            body(G - 2, G - 1, ahead=False)
            sp.wait_ge(x1_stored, 16 * G)
            sp.wait_ge(out_stored, 16 * G)
            sp.dma_start(x_out[:, :, :], x1_v[G - 1]).then_inc(xo_loaded, 16)
            store_rows(G - 1)
            sp.wait_ge(out_stored, 16 * G + 16)

        @block.scalar
        def _(act):
            act.wait_ge(kv_in, 16)
            nc.scalar.activation(w_kv[:, HI, :, :].rearrange("p a n -> p (a n)"),
                                 kv_raw[:, :, :].rearrange("p a n -> p (a n)"), ACT.Copy).then_inc(kv_hi, 1)
            act.wait_ge(ctx_in, 16)
            nc.scalar.activation(ctx_t[HI][:, :, 0:KW[0]], ctx_raw[:, :, 0:KW[0]], ACT.Copy).then_inc(ctx_hi, 1)

            def keys_hi(j):
                for i, (m, off, w) in enumerate(K_UNITS[C * j:C * j + C], C * j):
                    act.wait_ge(kv_full, full_kv("K", i))
                    if m == 0 and j == 1:
                        act.wait_ge(kblk_loaded, 16 * HPC)
                    if m == 0 and j > 0:
                        act.wait_ge(k_stored, 16 * j)
                    nc.scalar.activation(k_st[:, HI, m, 0:w], kv_bank("K", i)[:, 0:w], ACT.Identity,
                                         bias=b_qk[:, C + m:C + m + 1]).then_inc(k_hi, 1)

            def values_hi(i):
                act.wait_ge(kv_free, full_kv("V", i))
                if i == VB:
                    for c in range(C):
                        act.wait_ge(vblk_loaded[c], 16 * V_LOADS[c])
                if i >= VB:
                    act.wait_ge(v_stored[i % VB], 16 * (i // VB))
                nc.scalar.activation(v_st[0:S, HI, i % VB, :], v_f[0:S, i % 2, :], ACT.Copy).then_inc(v_hi, 1)

            def store_k(i):
                off, w = sum(KW[:i]), KW[i]
                act.wait_ge(kv_free, full_kv("K", C * i + C - 1))
                nc.scalar.dma_start(k_scr[:, :, :, off:off + w].rearrange("l c p w -> p (l c) w"),
                             f32(k_st[:, :, :, 0:w]).rearrange("p l c w -> p (l c) w")).then_inc(k_stored, 16)

            def store_v(i):
                act.wait_ge(v_lo, i + 1)
                nc.scalar.dma_start(v_scr[i], f32(v_st[0:S, :, i % VB, :])).then_inc(v_stored[i % VB], 16)

            def load_w(p):
                if p == 1:
                    act.wait_ge(qo_lo, 1)
                if p >= 2:
                    act.wait_ge(w_lo, p - 1)
                nc.scalar.dma_start(w_stage[p % 2], wffn[:, p * 2 * 512:(p + 1) * 2 * 512]).then_inc(w_in[p % 2], 16)

            def split_w(p):
                if p == 5:
                    for k in range(VB):
                        act.wait_ge(v_stored[k], 16 * len(range(k, V_UNITS, VB)))
                if p == 6:
                    act.wait_ge(kv_full, len(K_UNITS) + V_UNITS)
                act.wait_ge(w_in[p % 2], 16 * (p // 2 + 1))
                nc.scalar.activation(w_ffn[:, HI, 2 * p:2 * p + 2, :].rearrange("p a n -> p (a n)"), w_stage[p % 2],
                                     ACT.Copy).then_inc(w_hi, 1)
                if p + 1 < WP and p >= 1:
                    load_w(p + 1)

            def take_xt(u, n):
                if u[0] == "XT" and not before_all(n - 1):
                    act.wait_ge(x2_hi, n)
                act.wait_ge(bank_full[BANK[u]], full_count(u, n))
                nc.scalar.activation(xo_t[:, HI, u[1], :], bank(u)[:, :], ACT.Copy).then_inc(xt_hi, 1)

            def take_x2(u, n):
                j = int(u[0][2])
                act.wait_ge(bank_full[BANK[u]], full_count(u, n))
                nc.scalar.activation(xo_t[:, HI, :, T * j:T * j + T], bank(u)[:, :].rearrange("p (c n) -> p c n", c=C),
                                     ACT.Copy).then_inc(xt_hi, 1)

            def take_q(u, n):
                act.wait_ge(bank_full[BANK[u]], full_count(u, n))
                nc.scalar.activation(q_t[:, HI, u[1], :], bank(u)[:, :], ACT.Identity,
                                     bias=b_qk[:, u[1]:u[1] + 1]).then_inc(q_hi, 1)

            def exps(t, n):
                act.wait_ge(shifted, 4 * n + t + 1)
                nc.scalar.activation(scr[:, t % 2, 0:HS], scr[:, t % 2, 0:HS], ACT.Exp).then_inc(exp_done, 1)

            def take_pt(u, n):
                t, i = int(u[0][2]), u[1]
                k = min(4, NCH - 4 * i)
                act.wait_ge(bank_full[BANK[u]], full_count(u, n))
                nc.scalar.activation(p_t[:, HI, 4 * i:4 * i + k, P * (t % 2):P * (t % 2) + P],
                                     bank(u)[:, 0:k * P].rearrange("p (k n) -> p k n", k=k),
                                     ACT.Copy).then_inc(pt_hi, 1)

            def take_o(u, n):
                j = int(u[0][2])
                act.wait_ge(bank_full[BANK[u]], full_count(u, n))
                nc.scalar.activation(xo_t[:, HI, :, T * j:T * j + T], bank(u)[:, :].rearrange("p (c n) -> p c n", c=C),
                                     ACT.Copy).then_inc(ot_hi, 1)

            def take_logits(u, n):
                act.wait_ge(bank_full[BANK[u]], full_count(u, n))
                nc.scalar.activation(lg_t, bank(u)[0:N_ROUTED, :], ACT.Copy).then_inc(bank_free[BANK[u]], 1)

            def router_exp(n):
                act.wait_ge(bank_free[BANK[("RT", 0)]], full_count(("RT", 0), n))
                nc.scalar.activation(r_exp[:, :, :], r_exp[:, :, :], ACT.Exp).then_inc(r_exped, 1)

            def take_gates(u, n):
                act.wait_ge(bank_full[BANK[u]], full_count(u, n))
                nc.scalar.activation(gate_t[0:2 * N_ROUTED, :], bank(u)[0:2 * N_ROUTED, :], ACT.Copy)\
                    .then_inc(bank_free[BANK[u]], 1)

            def take(u, n):
                if u[0] == "XT":
                    take_xt(u, n)
                elif u[0][:2] == "X2":
                    take_x2(u, n)
                elif u[0] == "Q":
                    take_q(u, n)
                elif u[0][:2] == "PT":
                    take_pt(u, n)
                elif u[0][:2] == "PV":
                    take_o(u, n)
                elif u[0] == "R":
                    take_logits(u, n)
                elif u[0] == "GT":
                    take_gates(u, n)

            def attention(pos, n):
                at = FIRST if before_all(n - 1) else AT
                for u in units_at(pos, AT, taken=True):
                    take(u, n)
                for t in range(TILES):
                    if pos == at[f"E{t}"]:
                        exps(t, n)
                if pos == at["GEXP"]:
                    router_exp(n)
                if pos == at["HAND"]:
                    hand_over(n)

            def next_attention(pos, n):
                for u in units_at(pos, AHEAD):
                    take(u, n)

            def hand_over(n):
                if before_all(n - 1):
                    act.wait_ge(k_stored, 16 * len(KW))
                else:
                    act.wait_ge(up_full, NE * n)
                act.wait_ge(xt_hi, 4 * n + 4)
                nc.scalar.activation(x2_t[:, HI, :, :], f32(xo_t[:, HI, :, :]), ACT.Copy).then_inc(x2_hi, 1)

            def gelu(e, g):
                act.wait_ge(up_full, NE * g + e + 1)
                act.wait_ge(h_lo, NE * g + e + 1)
                nc.scalar.activation(gel[:, e % 2, :], up_ps[e % 2][:, :], ACT.Gelu).then_inc(up_read, 1)

            def hidden_hi(e, g):
                if e % NE < N_SHARED:
                    act.wait_ge(up_read, NE * g + e + 3)
                else:
                    act.wait_ge(gated, N_ROUTED * g + e - N_SHARED + 2)
                act.wait_ge(down_done, NE * g + e + 1)
                nc.scalar.activation(hid[:, e % HB, HI, :], gel[:, e % 2, :], ACT.Copy).then_inc(h_hi, 1)

            def take_ffn(g):
                act.wait_ge(down_done, NE * g + NE + HB)
                for m in range(C):
                    nc.scalar.activation(ffn_t[:, m, :], dn_ps[m][:, :], ACT.Copy, scale=g_tan[:, 1:2])\
                        .then_inc(ffn_read, 1)

            def body(g, n, ffn=True, attend=True, ahead=True):
                for e in SLOTS:
                    if ffn and e == SLOTS[-1]:
                        take_ffn(g)
                    if (ffn and e < NE) or (attend and e >= NE):
                        gelu(e, g)
                    for pos in (e + q for q in QUARTERS):
                        if pos == e + 0.5 and ((ffn and e <= NE) or (attend and e > NE)):
                            hidden_hi(e - 1, g)
                        if attend:
                            attention(pos, n)
                        if ahead:
                            next_attention(pos, n + 1)
                        if before_all(g):
                            context_and_weights(pos)

            def context_and_weights(pos):
                for j in K_AT:
                    if pos == K_AT[j]:
                        keys_hi(j)
                    if pos == K_AT[j] + 1:
                        store_k(j)
                for i in V_AT:
                    if pos == V_AT[i]:
                        values_hi(i)
                    if pos == V_LO_AT[i] + 0.5:
                        store_v(i)
                for p in W_AT:
                    if pos == W_AT[p]:
                        split_w(p)

            act.wait_ge(qo_in, 16)
            nc.scalar.activation(w_qo[:, HI, :, :].rearrange("p a n -> p (a n)"),
                                 qo_raw[:, :, :].rearrange("p a n -> p (a n)"), ACT.Copy).then_inc(qo_hi, 1)
            act.wait_ge(bias_in, 32)
            keys_hi(0)
            values_hi(0)
            for c in range(C):
                take(("XT", c), 0)
            act.wait_ge(ctx_rest_in, 16)
            nc.scalar.activation(ctx_t[HI][:, :, KW[0]:], ctx_raw[:, :, KW[0]:], ACT.Copy).then_inc(ctx_hi, 1)
            for m in range(C):
                take(("Q", m), 0)
            load_w(0)
            act.wait_ge(small_in, 4 * 16)
            nc.scalar.activation(w_rt[:, HI, :], wr_f[:, :], ACT.Copy).then_inc(qo_hi, 1)
            nc.scalar.activation(g_tan[:, :], g_raw[:, :], ACT.Tanh).then_inc(tan_done, 1)
            load_w(1)
            body(-1, 0, ffn=False)
            with act.Fori(0, G - 2) as g:
                body(g, g + 1)
            body(G - 2, G - 1, ahead=False)
            body(G - 1, G, attend=False, ahead=False)

        @block.vector
        def _(dve):
            nc.vector.memset(neg_half[:, :], -0.5).then_inc(zeroed, 1)
            nc.vector.memset(scr[:, :, HS:HSP], 0.0).then_inc(zeroed, 1)
            nc.vector.memset(f32(gate_t[:, :]), 0.0).then_inc(zeroed, 1)
            dve.wait_ge(kv_hi, 1)
            nc.vector.tensor_tensor(w_kv[:, LO, :, :].rearrange("p a n -> p (a n)"),
                                    kv_raw[:, :, :].rearrange("p a n -> p (a n)"),
                                    f32(w_kv[:, HI, :, :]).rearrange("p a n -> p (a n)"),
                                    ALU.subtract).then_inc(kv_lo, 1)
            dve.wait_ge(ctx_hi, 1)
            nc.vector.tensor_tensor(ctx_t[LO][:, :, 0:KW[0]], ctx_raw[:, :, 0:KW[0]], f32(ctx_t[HI][:, :, 0:KW[0]]),
                                    ALU.subtract).then_inc(ctx_lo, 1)

            def keys_lo(j):
                for i, (m, off, w) in enumerate(K_UNITS[C * j:C * j + C], C * j):
                    dve.wait_ge(k_hi, i + 1)
                    nc.vector.scalar_tensor_tensor(out=k_st[:, LO, m, 0:w], in0=kv_bank("K", i)[:, 0:w],
                                                   scalar=b_qk[:, C + m:C + m + 1], in1=f32(k_st[:, HI, m, 0:w]),
                                                   op0=ALU.add, op1=ALU.subtract).then_inc(kv_free, 1)

            def values(i):
                dve.wait_ge(kv_full, full_kv("V", i))
                if i >= 2:
                    dve.wait_ge(v_lo, i - 1)
                nc.vector.tensor_tensor(v_f[0:S, i % 2, :].rearrange("p (j n) -> p j n", j=2),
                                        kv_bank("V", i)[0:S, :].rearrange("p (j n) -> p j n", j=2),
                                        bc_mid(bv_b[0:S, :], 2), ALU.add).then_inc(kv_free, 1)

            def additive_mask(n):
                dve.wait_ge(mask_loaded, 16 * n + 16)
                nc.vector.tensor_scalar(mask_f[:, :, :].rearrange("p b s -> p (b s)"), mask_u[:, :], -3e38, 3e38,
                                        ALU.mult, ALU.mult).then_inc(mask_neg, 1)
                dve.wait_ge(mask_neg, n + 1)
                for t in range(2):
                    nc.vector.tensor_tensor(am_b[:, :, t, :], mask_f[:, :, :], bc_mid(am[:, t, :], BPG), ALU.add)\
                        .then_inc(mask_ready, 1)

            def carry_wait():
                nc.vector.memset(unused[:, :], 0.0)

            def tile_stats(src, tiles):
                for t in tiles:
                    nc.vector.bn_stats(st[:, t, :], src[:, t, :]).then_inc(ln_stats, 1)

            def norm_stats(n, k):
                tiles = NORMS[k]
                done = 8 * n + (4 if k > 0 else 0) + tiles[-1] + 1
                dve.wait_ge(ln_stats, done)
                carry_wait()
                for t in tiles:
                    nc.vector.bn_aggr(mv[:, t, :], st[:, t, :]).then_inc(ln_aggr, 1)
                dve.wait_ge(ln_aggr, done)
                nc.vector.tensor_scalar(ve[:, tiles[0]:tiles[-1] + 1], mv[:, tiles[0]:tiles[-1] + 1, 1], LN_EPS, None,
                                        ALU.add).then_inc(ln_var, 1)

            def norm_rows(src, n, k):
                dve.wait_ge(ln_rstd, len(NORMS) * n + k + 1)
                for t in NORMS[k]:
                    nc.vector.tensor_scalar(xn[:, t, :], src[:, t, :], mv[:, t, 0:1], rstd[:, t:t + 1],
                                            ALU.subtract, ALU.mult).then_inc(xn_ready, 1)

            def take_xt(u, n):
                if u[0] == "XT" and not before_all(n - 1):
                    dve.wait_ge(x2_lo, n)
                dve.wait_ge(xt_hi, 4 * n + u[1] + 1)
                nc.vector.tensor_tensor(xo_t[:, LO, u[1], :], bank(u)[:, :], f32(xo_t[:, HI, u[1], :]),
                                        ALU.subtract).then_inc(bank_free[BANK[u]], 1)

            def take_x2(u, n):
                j = int(u[0][2])
                dve.wait_ge(xt_hi, 4 * n + 2 + j + 1)
                nc.vector.tensor_tensor(xo_t[:, LO, :, T * j:T * j + T],
                                        bank(u)[:, :].rearrange("p (c n) -> p c n", c=C),
                                        f32(xo_t[:, HI, :, T * j:T * j + T]), ALU.subtract)\
                    .then_inc(bank_free[BANK[u]], 1)

            def take_q(u, n):
                m = u[1]
                dve.wait_ge(q_hi, 2 * n + m + 1)
                nc.vector.scalar_tensor_tensor(out=q_t[:, LO, m, :], in0=bank(u)[:, :], scalar=b_qk[:, m:m + 1],
                                               in1=f32(q_t[:, HI, m, :]), op0=ALU.add, op1=ALU.subtract)\
                    .then_inc(bank_free[BANK[u]], 1)

            def take_scores(u, n):
                t, i = int(u[0][1]), u[1]
                s = scr[:, t % 2, 0:HS].rearrange("p (h s) -> p h s", h=H)
                if t == 0 and i == 0:
                    dve.wait_ge(mask_ready, 2 * n + 2)
                dve.wait_ge(bank_full[BANK[u]], full_count(u, n))
                nc.vector.scalar_tensor_tensor(out=s[:, QH * i:QH * i + QH, :],
                                               in0=bank(u)[:, 0:QW].rearrange("p (h s) -> p h s", h=QH),
                                               scalar=SCALE, in1=bc_mid(am_b[:, t // 2, t % 2, :], QH),
                                               op0=ALU.mult, op1=ALU.add).then_inc(bank_free[BANK[u]], 1)

            def maximum(t, n):
                s = scr[:, t % 2, 0:HS].rearrange("p (h s) -> p h s", h=H)
                for u in last_in_banks([(f"S{t}", i) for i in range(QN)]):
                    dve.wait_ge(bank_free[BANK[u]], full_count(u, n))
                nc.vector.tensor_reduce(mx[:, t % 2, :], s, X, ALU.max).then_inc(max_done, 1)

            def shift(t, n):
                s = scr[:, t % 2, 0:HS].rearrange("p (h s) -> p h s", h=H)
                dve.wait_ge(max_done, 4 * n + t + 1)
                nc.vector.tensor_tensor(s, s, bc_last(mx[:, t % 2, :], S), ALU.subtract).then_inc(shifted, 1)

            def normal(t, n):
                s = scr[:, t % 2, 0:HS].rearrange("p (h s) -> p h s", h=H)
                dve.wait_ge(exp_done, 4 * n + t + 1)
                nc.vector.tensor_reduce(den[:, t % 2, :], s, X, ALU.add).then_inc(sum_done, 1)
                dve.wait_ge(sum_done, 4 * n + t + 1)
                nc.vector.reciprocal(rden[:, t % 2, :], den[:, t % 2, :]).then_inc(rden_done, 1)
                dve.wait_ge(rden_done, 4 * n + t + 1)
                nc.vector.tensor_tensor(s[:, POOL_HEADS:, :], s[:, POOL_HEADS:, :],
                                        bc_last(rden[:, t % 2, POOL_HEADS:], S), ALU.mult).then_inc(p_ready, 1)

            def take_pt(u, n):
                t, i = int(u[0][2]), u[1]
                k = min(4, NCH - 4 * i)
                dve.wait_ge(pt_hi, 12 * n + 3 * t + i + 1)
                nc.vector.tensor_tensor(p_t[:, LO, 4 * i:4 * i + k, P * (t % 2):P * (t % 2) + P],
                                        bank(u)[:, 0:k * P].rearrange("p (k n) -> p k n", k=k),
                                        f32(p_t[:, HI, 4 * i:4 * i + k, P * (t % 2):P * (t % 2) + P]),
                                        ALU.subtract).then_inc(bank_free[BANK[u]], 1)

            def take_o(u, n):
                j = int(u[0][2])
                dve.wait_ge(ot_hi, 2 * n + j + 1)
                nc.vector.tensor_tensor(xo_t[:, LO, :, T * j:T * j + T],
                                        bank(u)[:, :].rearrange("p (c n) -> p c n", c=C),
                                        f32(xo_t[:, HI, :, T * j:T * j + T]), ALU.subtract)\
                    .then_inc(bank_free[BANK[u]], 1)

            def residual(u, n):
                i = int(u[0][1])
                dve.wait_ge(xr_ready, n + 1)
                dve.wait_ge(bank_full[BANK[u]], full_count(u, n))
                nc.vector.scalar_tensor_tensor(out=x_res[:, 2 * i:2 * i + 2, :],
                                               in0=bank(u)[:, :].rearrange("p (t n) -> p t n", t=2),
                                               scalar=g_tan[:, 0:1], in1=x_res[:, 2 * i:2 * i + 2, :],
                                               op0=ALU.mult, op1=ALU.add).then_inc(bank_free[BANK[u]], 1)
                dve.wait_ge(bank_free[BANK[u]], full_count(u, n))
                tile_stats(x_res, (2 * i, 2 * i + 1))

            def shift_logits(n):
                u = ("RT", 0)
                lg = bank(u)[:, :].rearrange("p (t n) -> p t n", t=TILES)[:, :, 0:N_ROUTED]
                base = ROUTER_STEPS * n
                dve.wait_ge(bank_full[BANK[u]], full_count(u, n))
                nc.vector.tensor_reduce(r_max[:, :], lg, X, ALU.max).then_inc(router, 1)
                dve.wait_ge(router, base + 1)
                nc.vector.tensor_tensor(r_exp[:, :, :], lg, bc_last(r_max[:, :], N_ROUTED), ALU.subtract)\
                    .then_inc(bank_free[BANK[u]], 1)

            def gates(n):
                base = ROUTER_STEPS * n
                dve.wait_ge(r_exped, n + 1)
                nc.vector.tensor_reduce(r_sum[:, :], r_exp[:, :, :], X, ALU.add).then_inc(router, 1)
                dve.wait_ge(router, base + 2)
                nc.vector.reciprocal(r_rcp[:, :], r_sum[:, :]).then_inc(router, 1)
                dve.wait_ge(router, base + 3)
                nc.vector.tensor_tensor(r_prob[:, :, :], r_exp[:, :, :], bc_last(r_rcp[:, :], N_ROUTED), ALU.mult)\
                    .then_inc(router, 1)
                dve.wait_ge(router, base + 4)
                carry_wait()
                for t in range(TILES):
                    nc.vector.max(r_top[:, t, :], r_prob[:, t, :]).then_inc(router, 1)
                dve.wait_ge(router, base + 8)
                carry_wait()
                for t in range(TILES):
                    nc.vector.max_index(r_idx[:, t, :], r_top[:, t, :], r_prob[:, t, :]).then_inc(router, 1)
                dve.wait_ge(router, base + 12)
                nc.vector.tensor_copy(r_idf[:, :, :], r_idx[:, :, :]).then_inc(router, 1)
                dve.wait_ge(router, base + 13)
                for t in range(TILES):
                    eq = nc.vector.tensor_tensor(r_eq[:, t, :, :], bc_last(iota[:, :], TOP_K),
                                                 bc_mid(r_idf[:, t, 0:TOP_K], N_ROUTED), ALU.is_equal)
                eq.then_inc(router, 1)
                dve.wait_ge(router, base + 14)
                nc.vector.tensor_reduce(r_sel[:, :, :], r_eq[:, :, :, :], X, ALU.max).then_inc(router, 1)
                dve.wait_ge(router, base + 15)
                nc.vector.tensor_tensor(r_prob[:, :, :], r_prob[:, :, :], r_sel[:, :, :], ALU.mult)\
                    .then_inc(router, 1)
                dve.wait_ge(router, base + 16)
                nc.vector.tensor_copy(gate2[:, :, 0:N_ROUTED].bitcast(FR), r_prob[:, :, :]).then_inc(router, 1)
                dve.wait_ge(router, base + 17)
                nc.vector.tensor_tensor(gate2[:, :, N_ROUTED:2 * N_ROUTED], r_prob[:, :, :],
                                        gate2[:, :, 0:N_ROUTED], ALU.subtract).then_inc(router, 1)

            def take(u, n):
                if u[0] == "XT":
                    take_xt(u, n)
                elif u[0][:2] == "X2":
                    take_x2(u, n)
                elif u[0] == "Q":
                    take_q(u, n)
                elif u[0][:2] == "PT":
                    take_pt(u, n)
                elif u[0][:2] == "PV":
                    take_o(u, n)
                elif u[0][0] == "S":
                    take_scores(u, n)
                elif u[0][0] == "O":
                    residual(u, n)

            def attention(pos, n):
                at = FIRST if before_all(n - 1) else AT
                for u in units_at(pos, AT, taken=True):
                    take(u, n)
                for t in range(TILES):
                    if pos == at[f"SH{t}"]:
                        shift(t, n)
                    if pos == at[f"N{t}"]:
                        normal(t, n)
                    if pos == at[f"M{t}"]:
                        maximum(t, n)
                for j in range(BPG):
                    if pos == at[f"LN2{j}"]:
                        norm_stats(n, 1 + j)
                    if pos == at[f"LN2{j}B"]:
                        norm_rows(x_res, n, 1 + j)
                if pos == at["GATE"]:
                    shift_logits(n)
                if pos == at["PICK"]:
                    gates(n)
                if pos == at["HAND"]:
                    hand_over(n)

            def next_attention(pos, n):
                if pos == AHEAD["LN1"]:
                    dve.wait_ge(x_loaded, 16 * n + 16)
                    tile_stats(x_in, range(TILES))
                    norm_stats(n, 0)
                if pos == AHEAD["LN1B"]:
                    norm_rows(x_in, n, 0)
                if pos == AHEAD["MASK"]:
                    additive_mask(n)
                for u in units_at(pos, AHEAD):
                    take(u, n)

            def hand_over(n):
                if before_all(n - 1):
                    dve.wait_ge(k_stored, 16 * len(KW))
                else:
                    dve.wait_ge(up_full, NE * n)
                for u in last_in_banks([(f"X2{j}", 0) for j in range(BPG)]):
                    dve.wait_ge(bank_free[BANK[u]], full_count(u, n))
                nc.vector.tensor_copy(x2_t[:, LO, :, :], f32(xo_t[:, LO, :, :])).then_inc(x2_lo, 1)

            def gate(e, g):
                if e >= N_SHARED:
                    dve.wait_ge(up_read, NE * g + e + 3)
                    dve.wait_ge(gate_full, N_ROUTED * g + e - N_SHARED + 1)
                    nc.vector.tensor_tensor(gel[:, e % 2, :], gel[:, e % 2, :], gt_ps[:, :], ALU.mult)\
                        .then_inc(gated, 1)

            def add_ffn(g):
                dve.wait_ge(xo_loaded, 16 * g + 16)
                for i in range(2):
                    dve.wait_ge(fout_full, 2 * g + i + 1)
                    nc.vector.tensor_tensor(x_out[:, 2 * i:2 * i + 2, :], x_out[:, 2 * i:2 * i + 2, :],
                                            dn_ps[i][:, :].rearrange("p (t n) -> p t n", t=2), ALU.add)\
                        .then_inc(fout_added, 1)

            def body(g, n, ffn=True, attend=True, ahead=True):
                for e in SLOTS:
                    for pos in (e + q for q in QUARTERS):
                        if pos == e + 0.25 and ffn and e < NE:
                            gate(e, g)
                        if attend:
                            attention(pos, n)
                        if ahead:
                            next_attention(pos, n + 1)
                        if before_all(g):
                            context(pos)
                if ffn:
                    add_ffn(g)

            def context(pos):
                for j in K_AT:
                    if pos == K_AT[j]:
                        keys_lo(j)
                for i in V_AT:
                    if pos == V_AT[i]:
                        values(i)

            dve.wait_ge(x_loaded, 16)
            tile_stats(x_in, range(TILES))
            norm_stats(0, 0)
            dve.wait_ge(bias_in, 32)
            keys_lo(0)
            norm_rows(x_in, 0, 0)
            values(0)
            for step in ("XT", "Q"):
                for i in range(C):
                    take((step, i), 0)
            dve.wait_ge(am_in, 16)
            additive_mask(0)
            dve.wait_ge(tan_done, 1)
            nc.vector.tensor_scalar(bo_b[:, :], bo_b[:, :], g_tan[:, 0:1], None, ALU.mult).then_inc(tbo_done, 1)
            dve.wait_ge(ctx_rest_lo, 1)
            body(-1, 0, ffn=False)
            with dve.Fori(0, G - 2) as g:
                body(g, g + 1)
            body(G - 2, G - 1, ahead=False)
            body(G - 1, G, attend=False, ahead=False)

        @block.gpsimd
        def _(pool):
            nc.gpsimd.memset(f32(k_blk[:, :, :, :]), 0.0).then_inc(zeroed, 1)
            nc.gpsimd.memset(f32(v_blk[:, :, :, :]), 0.0).then_inc(zeroed, 1)
            pool.sem_inc(up_read, 2)
            pool.sem_inc(h_lo, 2)
            pool.sem_inc(down_done, HB)
            pool.sem_inc(fout_added, 2)
            pool.sem_inc(gated, 1)
            pool.sem_inc(out_stored, 16)

            def split_w(p):
                pool.wait_ge(w_hi, p + 1)
                nc.gpsimd.tensor_tensor(w_ffn[:, LO, 2 * p:2 * p + 2, :].rearrange("p a n -> p (a n)"), w_stage[p % 2],
                                        f32(w_ffn[:, HI, 2 * p:2 * p + 2, :]).rearrange("p a n -> p (a n)"),
                                        ALU.subtract).then_inc(w_lo, 1)

            def values_lo(i):
                pool.wait_ge(v_hi, i + 1)
                if i == VB:
                    for c in range(C):
                        pool.wait_ge(vblk_loaded[c], 16 * V_LOADS[c])
                if i >= VB:
                    pool.wait_ge(v_stored[i % VB], 16 * (i // VB))
                nc.gpsimd.tensor_tensor(v_st[0:S, LO, i % VB, :], v_f[0:S, i % 2, :], f32(v_st[0:S, HI, i % VB, :]),
                                        ALU.subtract).then_inc(v_lo, 1)

            def root(n, k):
                t0, t1 = NORMS[k][0], NORMS[k][-1] + 1
                pool.wait_ge(ln_var, len(NORMS) * n + k + 1)
                nc.gpsimd.tensor_tensor(rstd[:, t0:t1], ve[:, t0:t1], neg_half[:, t0:t1], ALU.pow).then_inc(ln_rstd, 1)

            def rows(n):
                pool.wait_ge(x_loaded, 16 * n + 16)
                if before_all(n - 1):
                    pool.wait_ge(v_lo, V_UNITS)
                else:
                    pool.wait_ge(x1_stored, 16 * n)
                    pool.wait_ge(xn_ready, 8 * n)
                nc.gpsimd.tensor_tensor(x_res[:, :, :], x_in[:, :, :], bc_mid(bo_b[:, :], TILES), ALU.add)\
                    .then_inc(xr_ready, 1)

            def probabilities(t, n):
                s = scr[:, t % 2, 0:HS].rearrange("p (h s) -> p h s", h=H)
                pool.wait_ge(rden_done, 4 * n + t + 1)
                nc.gpsimd.tensor_tensor(s[:, 0:POOL_HEADS, :], s[:, 0:POOL_HEADS, :],
                                        bc_last(rden[:, t % 2, 0:POOL_HEADS], S), ALU.mult).then_inc(p_ready, 1)

            def attention(pos, n):
                at = FIRST if before_all(n - 1) else AT
                if pos == (max(V_LO_AT.values()) + 0.5 if before_all(n - 1) else SLOTS[0]):
                    rows(n)
                for t in range(TILES):
                    if pos == at[f"N{t}"]:
                        probabilities(t, n)
                for j in range(BPG):
                    if pos == at[f"LN2{j}"]:
                        root(n, 1 + j)

            def next_attention(pos, n):
                if pos == AHEAD["LN1"]:
                    root(n, 0)

            def hidden_lo(e, g):
                pool.wait_ge(h_hi, NE * g + e + 1)
                nc.gpsimd.tensor_tensor(hid[:, e % HB, LO, :], gel[:, e % 2, :], f32(hid[:, e % HB, HI, :]),
                                        ALU.subtract).then_inc(h_lo, 1)

            def body(g, n, ffn=True, attend=True, ahead=True):
                for e in SLOTS:
                    for pos in (e + q for q in QUARTERS):
                        if pos == e + 0.5 and ((ffn and e <= NE) or (attend and e > NE)):
                            hidden_lo(e - 1, g)
                        if attend:
                            attention(pos, n)
                        if ahead:
                            next_attention(pos, n + 1)
                        if before_all(g):
                            context_and_weights(pos)

            def context_and_weights(pos):
                for i in V_LO_AT:
                    if pos == V_LO_AT[i]:
                        values_lo(i)
                for p in W_LO_AT:
                    if pos == W_LO_AT[p]:
                        split_w(p)
                if pos == W_LO_AT[7]:
                    pool.wait_ge(consts_in, 32)
                    nc.gpsimd.tensor_copy(pick[:, :, :], bc_last(pick_f[:, :], P)).then_inc(picked, 1)

            pool.wait_ge(zeroed, 5)
            root(0, 0)
            pool.wait_ge(qo_hi, 1)
            nc.gpsimd.tensor_tensor(w_qo[:, LO, :, :].rearrange("p a n -> p (a n)"),
                                    qo_raw[:, :, :].rearrange("p a n -> p (a n)"),
                                    f32(w_qo[:, HI, :, :]).rearrange("p a n -> p (a n)"),
                                    ALU.subtract).then_inc(qo_lo, 1)
            values_lo(0)
            pool.wait_ge(ctx_hi, 2)
            nc.gpsimd.tensor_tensor(ctx_t[LO][:, :, KW[0]:], ctx_raw[:, :, KW[0]:],
                                    f32(ctx_t[HI][:, :, KW[0]:]), ALU.subtract).then_inc(ctx_rest_lo, 1)
            pool.wait_ge(qo_hi, 2)
            nc.gpsimd.tensor_tensor(w_rt[:, LO, :], wr_f[:, :], f32(w_rt[:, HI, :]), ALU.subtract).then_inc(qo_lo, 1)
            pool.wait_ge(tbo_done, 1)
            pool.wait_ge(kv_lo, 1)
            body(-1, 0, ffn=False)
            with pool.Fori(0, G - 2) as g:
                body(g, g + 1)
            body(G - 2, G - 1, ahead=False)
            body(G - 1, G, attend=False, ahead=False)

        @block.tensor
        def _(pe):
            def product(dst, pairs, first=True, last=True):
                k = 0
                for lhs, rhs in pairs:
                    for a, b in PASSES:
                        mm = nc.tensor.matmul(dst, lhs(a), rhs(b), start=first and k == 0,
                                              stop=last and k == 3 * len(pairs) - 1)
                        k += 1
                return mm

            def w_half(w, which, c, m0, m1):
                return lambda l: w[:, l, which, c * E + m0:c * E + m1]

            def keys(j):
                if j > 0:
                    pe.wait_ge(ctx_rest_lo, 1)
                for i, (m, off, w) in enumerate(K_UNITS[C * j:C * j + C], C * j):
                    if full_kv("K", i) > len(kv_ps):
                        pe.wait_ge(kv_free, full_kv("K", i) - len(kv_ps))
                    product(kv_bank("K", i)[:, 0:w],
                            [(w_half(w_kv, 0, c, m * P, m * P + P),
                              lambda l, c=c: ctx_t[l][:, c, off:off + w]) for c in range(C)]).then_inc(kv_full, 1)

            def values(i):
                if full_kv("V", i) > len(kv_ps):
                    pe.wait_ge(kv_free, full_kv("V", i) - len(kv_ps))
                for j in range(2):
                    b = 2 * i + j
                    mm = product(kv_bank("V", i)[0:S, j * E:(j + 1) * E],
                                 [(lambda l, c=c: ctx_t[l][:, c, b * S:(b + 1) * S],
                                   w_half(w_kv, 1, c, 0, E)) for c in range(C)])
                mm.then_inc(kv_full, 1)

            def refill(u, n, after=()):
                for v in last_in_banks(after):
                    if BANK[v] != BANK[u]:
                        pe.wait_ge(bank_free[BANK[v]], full_count(v, n))
                pe.wait_ge(bank_free[BANK[u]], full_count(u, n) - 1)

            def transpose_rows(u, n):
                refill(u, n)
                for t in range(TILES):
                    if u[1] == 0:
                        pe.wait_ge(xn_ready, 8 * n + t + 1)
                    mm = nc.tensor.transpose(bank(u)[:, t * P:(t + 1) * P], xn[:, t, u[1] * P:(u[1] + 1) * P],
                                             ident[:, :])
                mm.then_inc(bank_full[BANK[u]], 1)

            def transpose_batch(u, n):
                j = int(u[0][2])
                refill(u, n)
                for t in (2 * j, 2 * j + 1):
                    pe.wait_ge(xn_ready, 8 * n + 4 + t + 1)
                    for c in range(C):
                        mm = nc.tensor.transpose(bank(u)[:, c * T + (t % 2) * P:c * T + (t % 2 + 1) * P],
                                                 xn[:, t, c * P:(c + 1) * P], ident[:, :])
                mm.then_inc(bank_full[BANK[u]], 1)

            def queries(u, n):
                m = u[1]
                refill(u, n, after=[("XT", 0), ("XT", 1)])
                product(bank(u)[:, :], [(w_half(w_qo, 0, c, m * P, m * P + P),
                                         lambda l, c=c: xo_t[:, l, c, :]) for c in range(C)])\
                    .then_inc(bank_full[BANK[u]], 1)

            def scores(u, n):
                t, i = int(u[0][1]), u[1]
                if i == 0:
                    pe.wait_ge(kblk_loaded, (2 * n + t // 2 + 1) * (HPC * 16))
                c, o = i // (QN // C), QW * (i % (QN // C))
                refill(u, n, after=[("Q", 0), ("Q", 1)] if t == 0 and i == 0 else [])
                product(bank(u)[:, 0:QW], [(lambda l: q_t[:, l, c, t * P:(t + 1) * P],
                                            lambda l: k_blk[:, l, c, o:o + QW])]).then_inc(bank_full[BANK[u]], 1)

            def transpose_p(u, n):
                t, i = int(u[0][2]), u[1]
                if i == 0:
                    pe.wait_ge(p_ready, 8 * n + 2 * t + 2)
                refill(u, n)
                for k in range(4 * i, min(4 * i + 4, NCH)):
                    mm = nc.tensor.transpose(bank(u)[:, (k - 4 * i) * P:(k - 4 * i + 1) * P],
                                             scr[:, t % 2, k * P:(k + 1) * P], ident[:, :])
                mm.then_inc(bank_full[BANK[u]], 1)

            def head_outputs(u, n):
                j = int(u[0][2])
                pe.wait_ge(vblk_loaded[0], (2 * n + j + 1) * (16 * V_LOADS[0]))
                refill(u, n, after=[(f"PT{2 * j + 1}", i) for i in range((SPLIT - 1) // 4 + 1)])
                product(bank(u)[:, 0:T], [(lambda l, k=k: v_blk[:, l, k, :], lambda l, k=k: p_t[:, l, k, :])
                                          for k in range(SPLIT)]).then_inc(heads_half, 1)

            def head_outputs_2(j, n):
                u = (f"PV{j}", 0)
                pe.wait_ge(vblk_loaded[1], (2 * n + j + 1) * (16 * V_LOADS[1]))
                v = (f"PT{2 * j + 1}", 2)
                pe.wait_ge(bank_free[BANK[v]], full_count(v, n))
                product(bank(u)[:, T:2 * T], [(lambda l, k=k: v_blk[:, l, SPLIT + k - FIRST2, :],
                                               lambda l, k=k: p_t[:, l, k, :]) for k in range(FIRST2, NCH)])\
                    .then_inc(bank_full[BANK[u]], 1)

            def project(u, n):
                j = int(u[0][1])
                refill(u, n, after=[(f"PV{j}", 0)])
                for t in (2 * j, 2 * j + 1):
                    mm = product(bank(u)[:, (t % 2) * E:(t % 2 + 1) * E],
                                 [(lambda l, c=c, t=t: xo_t[:, l, c, t * P:(t + 1) * P],
                                   w_half(w_qo, 1, c, 0, E)) for c in range(C)])
                mm.then_inc(bank_full[BANK[u]], 1)

            def logits(n):
                u = ("R", 0)
                if before_all(n - 1):
                    pe.wait_ge(qo_lo, 2)
                refill(u, n, after=[("X20", 0), ("X21", 0)])
                product(bank(u)[0:N_ROUTED, :],
                        [(lambda l, c=c: w_rt[:, l, c * N_ROUTED:(c + 1) * N_ROUTED],
                          lambda l, c=c: xo_t[:, l, c, :]) for c in range(C)]).then_inc(bank_full[BANK[u]], 1)

            def logits_rows(n):
                u = ("RT", 0)
                refill(u, n, after=[("R", 0)])
                for t in range(TILES):
                    mm = nc.tensor.transpose(bank(u)[:, t * P:(t + 1) * P], scr[:, 1, t * P:(t + 1) * P], ident[:, :])
                mm.then_inc(bank_full[BANK[u]], 1)

            def gate_columns(n):
                u = ("GT", 0)
                pe.wait_ge(router, ROUTER_STEPS * n + ROUTER_STEPS)
                refill(u, n)
                for t in range(TILES):
                    mm = nc.tensor.transpose(bank(u)[0:2 * N_ROUTED, t * P:(t + 1) * P], gate2[:, t, :], ident[:, :])
                mm.then_inc(bank_full[BANK[u]], 1)

            def fill(u, n):
                if u[0] == "XT":
                    transpose_rows(u, n)
                elif u[0][:2] == "X2":
                    transpose_batch(u, n)
                elif u[0] == "Q":
                    queries(u, n)
                elif u[0][0] == "S":
                    scores(u, n)
                elif u[0][:2] == "PT":
                    transpose_p(u, n)
                elif u[0][:2] == "PV":
                    head_outputs(u, n)
                elif u[0][0] == "O":
                    project(u, n)
                elif u[0] == "R":
                    logits(n)
                elif u[0] == "RT":
                    logits_rows(n)
                elif u[0] == "GT":
                    gate_columns(n)

            def up(e, g):
                if e == NE:
                    if before_all(g):
                        pe.wait_ge(w_lo, WP)
                    pe.wait_ge(x2_hi, g + 2)
                    pe.wait_ge(x2_lo, g + 2)
                pe.wait_ge(up_read, NE * g + e + 1)
                w = e % NE
                product(up_ps[e % 2][:, :], [(lambda l, c=c: w_ffn[:, l, w, c * P:(c + 1) * P],
                                              lambda l, c=c: x2_t[:, l, c, :]) for c in range(C)])\
                    .then_inc(up_full, 1)

            def spread_gate(e, g):
                r = e - N_SHARED
                if r == 0:
                    pe.wait_ge(picked, 1)
                    pe.wait_ge(bank_free[BANK[("GT", 0)]], full_count(("GT", 0), g))
                pe.wait_ge(gated, N_ROUTED * g + r + 1)
                nc.tensor.matmul(gt_ps[:, :], pick[:, r, :], gate_t[:, :], start=True, stop=True)\
                    .then_inc(gate_full, 1)

            def down(e, g):
                if e == 0:
                    pe.wait_ge(fout_added, 2 * g + 2)
                pe.wait_ge(h_lo, NE * g + e + 3)
                for m in range(C):
                    mm = product(dn_ps[m][:, :], [(lambda l: w_ffn[:, l, e, 2 * P + m * P:2 * P + (m + 1) * P],
                                                   lambda l: hid[:, e % HB, l, :])],
                                 first=e == 0, last=e == NE - 1)
                mm.then_inc(down_done, 1)

            def ffn_rows(g):
                pe.wait_ge(ffn_read, 2 * g + 2)
                for i in range(2):
                    for t in (2 * i, 2 * i + 1):
                        for m in range(C):
                            mm = nc.tensor.transpose(dn_ps[i][:, (t % 2) * E + m * P:(t % 2) * E + (m + 1) * P],
                                                     ffn_t[:, m, t * P:(t + 1) * P], ident[:, :])
                    mm.then_inc(fout_full, 1)

            def body(g, n, ffn=True, attend=True, ahead=True):
                for e in SLOTS:
                    if ffn and e == SLOTS[-1]:
                        down(e - LAG, g)
                    if (ffn and e < NE) or (attend and e >= NE):
                        up(e, g)
                    for pos in (e + q for q in QUARTERS):
                        if pos == e + 0.5 and ffn and e < SLOTS[-1]:
                            if e < NE:
                                spread_gate(e, g)
                            down(e - LAG, g)
                        if attend:
                            for j in range(2):
                                if pos == AT[f"PV{j}"] + 0.5:
                                    head_outputs_2(j, n)
                            for u in units_at(pos, AT):
                                fill(u, n)
                        if ahead:
                            for u in units_at(pos, AHEAD):
                                fill(u, n + 1)
                        if before_all(g):
                            context(pos)
                if ffn:
                    ffn_rows(g)

            def context(pos):
                for j in K_AT:
                    if pos == K_AT[j]:
                        keys(j)
                for i in V_AT:
                    if pos == V_AT[i]:
                        values(i)

            pe.wait_ge(ctx_lo, 1)
            pe.wait_ge(kv_lo, 1)
            keys(0)
            values(0)
            pe.wait_ge(ident_in, 16)
            fill(("XT", 0), 0)
            fill(("XT", 1), 0)
            pe.wait_ge(qo_lo, 1)
            fill(("Q", 0), 0)
            fill(("Q", 1), 0)
            body(-1, 0, ffn=False)
            with pe.Fori(0, G - 2) as g:
                body(g, g + 1)
            body(G - 2, G - 1, ahead=False)
            body(G - 1, G, attend=False, ahead=False)


def kernel(x, ctx_1024, fside_Bx16xSxS2_0, fside_SxS2_0, mask_BxS2_bf0, g_xattn, g_ffn, L0_xattn_Wq, L0_xattn_bq,
           L0_xattn_Wk, L0_xattn_bk, L0_xattn_Wv, L0_xattn_bv, L0_xattn_Wo, L0_xattn_bo, L0_ffn_shared_up,
           L0_ffn_shared_down, L0_ffn_routed_up, L0_ffn_routed_down, L0_ffn_router_w):
    import numpy as np
    import concourse.bacc as bacc
    from concourse.bass_utils import run_bass_kernel_spmd

    def by_half(w):
        w = np.asarray(w)
        return w.T.reshape(C, P, w.shape[0]).transpose(1, 0, 2).reshape(P, C * w.shape[0])

    def column(b):
        return np.asarray(b).reshape(C, P).T

    ups = np.concatenate([np.asarray(L0_ffn_shared_up), np.asarray(L0_ffn_routed_up)])
    downs = np.concatenate([np.asarray(L0_ffn_shared_down), np.asarray(L0_ffn_routed_down)])
    up_t = ups.reshape(NE, HID, C, P).transpose(3, 0, 2, 1)
    down_t = downs.transpose(2, 0, 1).reshape(HID, NE, C, P)
    arrays = {
        "x": np.asarray(x).reshape(B * T, E),
        "ctxT": np.asarray(ctx_1024).reshape(CTX, E).T.reshape(C, P, CTX).transpose(1, 0, 2),
        "mask": np.asarray(mask_BxS2_bf0),
        "attn_mask": np.asarray(fside_SxS2_0),
        "g_x": np.asarray(g_xattn).reshape(1, 1),
        "g_f": np.asarray(g_ffn).reshape(1, 1),
        "wkvT": np.concatenate([by_half(L0_xattn_Wk), by_half(L0_xattn_Wv)], axis=1),
        "wqoT": np.concatenate([by_half(L0_xattn_Wq), by_half(L0_xattn_Wo)], axis=1),
        "bqk": np.concatenate([column(L0_xattn_bq), column(L0_xattn_bk)], axis=1),
        "bo": np.asarray(L0_xattn_bo).reshape(1, E),
        "bv": np.asarray(L0_xattn_bv).reshape(1, E),
        "wffn": np.concatenate([up_t.reshape(P, NE, C * P), down_t.reshape(P, NE, C * P)], axis=2).reshape(P, -1),
        "wr": by_half(L0_ffn_router_w),
        "ident": np.eye(P, dtype=np.float32),
        "pick": np.concatenate([np.eye(N_ROUTED), np.eye(N_ROUTED), np.zeros((P - 2 * N_ROUTED, N_ROUTED))])
        .astype(np.float32),
        "iota": np.tile(np.arange(N_ROUTED, dtype=np.float32), (P, 1)),
    }
    arrays = {f"in_{k}": np.ascontiguousarray(v) for k, v in arrays.items()}
    nc = bacc.Bacc("TRN2", target_bir_lowering=False, num_devices=1)
    args = [nc.dram_tensor(k, v.shape, mybir.dt.from_np(v.dtype), kind="ExternalInput").ap()
            for k, v in arrays.items()]
    out = nc.dram_tensor("out_rows", (B * T, E), F32, kind="ExternalOutput").ap()
    block_program(nc, *args, out)
    r = run_bass_kernel_spmd(nc, [arrays], core_ids=[0])
    return r.results[0]["out_rows"].reshape(B, T, E)
```
